# Optimizing a Trainium2 kernel written in Bass

```python
import numpy as np
import jax
import jax.numpy as jnp

def _softmax(x, axis=-1):
    return jax.nn.softmax(x, axis=axis)

def _gelu(x):
    return jax.nn.gelu(x, approximate=True)

def _silu(x):
    return jax.nn.silu(x)

def _sigmoid(x):
    return jax.nn.sigmoid(x)

def _layernorm(x, axis=-1, eps=1e-05):
    m = jnp.mean(x, axis=axis, keepdims=True)
    v = jnp.var(x, axis=axis, keepdims=True)
    return (x - m) / jnp.sqrt(v + eps)

def _scatter_add(tgt, idx, src, axis=0):
    return tgt.at[idx].add(src)

def _segment_sum(src, seg, n):
    return jax.ops.segment_sum(src, seg, n)
kernel_name = 'mk_xattn_ffn_d4_seqx_r8_dcf9d3'

def setup_inputs(seed: int=0):
    np.random.seed(seed)
    _w = jnp.asarray

    def _rec_inputs():
        import jax
        import jax.numpy as jnp
        _rk = jax.random.key(seed)
        x = -0.0002928 + 1 * jax.random.normal(jax.random.fold_in(_rk, 1), (32, 128, 128), jnp.float32)
        _lenS = 128 - jax.random.randint(jax.random.fold_in(_rk, 7), (32,), 0, max(1, 128 // 4) + 1, jnp.int32)
        _lenS2 = 77 - jax.random.randint(jax.random.fold_in(_rk, 8), (32,), 0, max(1, 77 // 4) + 1, jnp.int32)
        _ctx_1024P = jax.random.normal(jax.random.fold_in(_rk, 11), (32, 16, 128), jnp.float32)
        _ctx_1024c = jax.random.dirichlet(jax.random.fold_in(_rk, 511), 0.3 * jnp.ones((16,), jnp.float32), (32, 77))
        _ctx_1024t = jnp.einsum('bsk,bkd->bsd', _ctx_1024c, _ctx_1024P)
        _ctx_1024t = _ctx_1024t * jax.lax.rsqrt(jnp.mean(jnp.square(_ctx_1024t)) + 1e-12) * 0.953939
        ctx_1024 = -1.39393e-06 + 0.999914 * (_ctx_1024t + 0.3 * jax.random.normal(jax.random.fold_in(_rk, 611), (32, 77, 128), jnp.float32))
        _validS = jnp.arange(128)[None, :] < _lenS[:, None]
        _validS2 = jnp.arange(77)[None, :] < _lenS2[:, None]
        _causal = jnp.tril(jnp.ones((128, 128), dtype=bool))
        mask_BxSxS2_if1 = jnp.where(jnp.ones((32, 128, 77), dtype=bool), 1, 0).astype(jnp.int32)
        mask_Bx1xSxS2_ik1 = jnp.where(jnp.broadcast_to(_validS2[:, None, None, :], (32, 1, 128, 77)), 1, 0).astype(jnp.int32)
        mask_BxSxS2_fk0 = jnp.where(jnp.broadcast_to(_validS2[:, None, :], (32, 128, 77)), -1000000000.0, 0.0).astype(jnp.float32)
        return (x, ctx_1024, mask_BxSxS2_if1, mask_Bx1xSxS2_ik1, mask_BxSxS2_fk0)
    x, ctx_1024, mask_BxSxS2_if1, mask_Bx1xSxS2_ik1, mask_BxSxS2_fk0 = _rec_inputs()

    def _L0_xattn_setup():
        import jax, jax.numpy as jnp
        import numpy as np
        EMB, HEADS = (128, 16)
        HEAD_DIM = EMB // HEADS

        def _linear(x, W, b):
            return jnp.einsum('bse,oe->bso', x, W) + b
        key = jax.random.key(seed)
        ks = jax.random.split(key, 11)
        B, S = (2, 256)
        sc = 1.0 / np.sqrt(EMB)
        inp = {'x': jax.random.normal(ks[0], (B, S, EMB), dtype=jnp.float32), 'y': jax.random.normal(ks[1], (B, S, EMB), dtype=jnp.float32), 'mask': jnp.ones((B, S, S), dtype=jnp.int32), 'Wq': jax.random.normal(ks[2], (EMB, EMB), dtype=jnp.float32) * sc, 'bq': jax.random.normal(ks[3], (EMB,), dtype=jnp.float32) * sc, 'Wk': jax.random.normal(ks[4], (EMB, EMB), dtype=jnp.float32) * sc, 'bk': jax.random.normal(ks[5], (EMB,), dtype=jnp.float32) * sc, 'Wv': jax.random.normal(ks[6], (EMB, EMB), dtype=jnp.float32) * sc, 'bv': jax.random.normal(ks[7], (EMB,), dtype=jnp.float32) * sc, 'Wo': jax.random.normal(ks[8], (EMB, EMB), dtype=jnp.float32) * sc, 'bo': jax.random.normal(ks[9], (EMB,), dtype=jnp.float32) * sc}
        return inp
    _L0_xattn_all = _L0_xattn_setup()
    _L0_xattn_in = {k: v for k, v in _L0_xattn_all.items() if k in ('Wq', 'bq', 'Wk', 'bk', 'Wv', 'bv', 'Wo', 'bo')}
    del _L0_xattn_all

    def _L0_ffn_setup():
        import jax, jax.numpy as jnp
        import numpy as np
        DIM = 128
        DEPTH = 7
        PAR = 8
        N_NODES = 2 ** (DEPTH + 1) - 1
        WIDTH = PAR * N_NODES
        key = jax.random.key(seed)
        k1, k2, k3, k4 = jax.random.split(key, 4)
        init_k = float(np.sqrt(1.0 / DIM))
        init_k2 = float(np.sqrt(1.0 / ((DEPTH + 1) * PAR)))
        oldx = jax.random.normal(k1, (4, 256, DIM), dtype=jnp.float32)
        W_in = jax.random.uniform(k2, (WIDTH, DIM), jnp.float32, -init_k, init_k)
        b_in = jax.random.uniform(k3, (WIDTH,), jnp.float32, -init_k, init_k)
        W_out = jax.random.uniform(k4, (DIM, WIDTH), jnp.float32, -init_k2, init_k2)
        return {'oldx': oldx, 'W_in': W_in, 'b_in': b_in, 'W_out': W_out}
    _L0_ffn_all = _L0_ffn_setup()
    _L0_ffn_in = {k: v for k, v in _L0_ffn_all.items() if k in ('W_in', 'b_in', 'W_out')}
    del _L0_ffn_all

    def _L1_xattn_setup():
        import jax, jax.numpy as jnp
        import numpy as np
        DIM = 128
        HEADS = 16
        HEAD_DIM = DIM // HEADS
        key = jax.random.key(seed)
        ks = jax.random.split(key, 12)
        B, Tq, Tk = (2, 256, 256)
        inp = {'query': jax.random.normal(ks[0], (B, Tq, DIM), jnp.float32), 'key': jax.random.normal(ks[1], (B, Tk, DIM), jnp.float32), 'value': jax.random.normal(ks[2], (B, Tk, DIM), jnp.float32), 'mask': jax.random.randint(ks[3], (B, 1, Tq, Tk), 0, 2, jnp.int32), 'wq': jax.random.uniform(ks[4], (DIM, DIM), jnp.float32, -1.0, 1.0) * np.sqrt(6.0 / (2 * DIM)), 'wk': jax.random.uniform(ks[5], (DIM, DIM), jnp.float32, -1.0, 1.0) * np.sqrt(6.0 / (2 * DIM)), 'wv': jax.random.uniform(ks[6], (DIM, DIM), jnp.float32, -1.0, 1.0) * np.sqrt(6.0 / (2 * DIM)), 'wo': jax.random.uniform(ks[7], (DIM, DIM), jnp.float32, -1.0, 1.0) * np.sqrt(6.0 / (2 * DIM)), 'bq': jnp.zeros((DIM,), jnp.float32), 'bk': jnp.zeros((DIM,), jnp.float32), 'bv': jnp.zeros((DIM,), jnp.float32), 'bo': jnp.zeros((DIM,), jnp.float32)}
        return inp
    _L1_xattn_all = _L1_xattn_setup()
    _L1_xattn_in = {k: v for k, v in _L1_xattn_all.items() if k in ('wq', 'wk', 'wv', 'wo', 'bq', 'bk', 'bv', 'bo')}
    del _L1_xattn_all

    def _L1_ffn_setup():
        import jax, jax.numpy as jnp
        import numpy as np
        H = 128
        I = 64
        IS = 128
        E = 16
        G = 4
        TOPK_G = 2
        TOPK = 4
        SCALE = 2.5
        B, S = (2, 128)

        def _relu2(x):
            r = jax.nn.relu(x)
            return r * r

        def _route(scores, bias_corr):
            T = scores.shape[0]
            s_choice = scores + bias_corr
            gs = s_choice.reshape(T, G, E // G)
            group_scores = jnp.sum(jax.lax.top_k(gs, 2)[0], axis=-1)
            gidx = jax.lax.top_k(group_scores, TOPK_G)[1]
            gmask = jnp.sum(jax.nn.one_hot(gidx, G, dtype=scores.dtype), axis=1)
            smask = jnp.repeat(gmask, E // G, axis=1)
            masked = jnp.where(smask > 0, s_choice, 0.0)
            topk_idx = jax.lax.top_k(masked, TOPK)[1]
            topk_w = jnp.take_along_axis(scores, topk_idx, axis=1)
            topk_w = topk_w / (jnp.sum(topk_w, axis=-1, keepdims=True) + 1e-20)
            topk_w = topk_w * SCALE
            return (topk_idx, topk_w)
        key = jax.random.key(seed)
        ks = jax.random.split(key, 8)
        sd = 0.02
        return {'hidden_states': jax.random.normal(ks[0], (B, S, H), jnp.float32), 'Wg': jax.random.normal(ks[1], (E, H), jnp.float32) * sd, 'bias_corr': jax.random.normal(ks[2], (E,), jnp.float32) * 0.01, 'W1': jax.random.normal(ks[3], (E, I, H), jnp.float32) * sd, 'W2': jax.random.normal(ks[4], (E, H, I), jnp.float32) * sd, 'Ws1': jax.random.normal(ks[5], (IS, H), jnp.float32) * sd, 'Ws2': jax.random.normal(ks[6], (H, IS), jnp.float32) * sd}
    _L1_ffn_all = _L1_ffn_setup()
    _L1_ffn_in = {k: v for k, v in _L1_ffn_all.items() if k in ('Wg', 'bias_corr', 'W1', 'W2', 'Ws1', 'Ws2')}
    del _L1_ffn_all

    def _L2_xattn_setup():
        import jax, jax.numpy as jnp
        import numpy as np
        D = 128
        NUM_ITERS = 3
        EPS = 1e-06
        SCALE = D ** (-0.5)

        def rmsnorm(x, w, eps=EPS):
            return x * jax.lax.rsqrt(jnp.mean(x * x, axis=-1, keepdims=True) + eps) * w

        def gru_cell(x, h, wih, whh, bih, bhh):
            gx = x @ wih.T + bih
            gh = h @ whh.T + bhh
            xr, xz, xn = jnp.split(gx, 3, axis=-1)
            hr, hz, hn = jnp.split(gh, 3, axis=-1)
            r = jax.nn.sigmoid(xr + hr)
            z = jax.nn.sigmoid(xz + hz)
            n = jnp.tanh(xn + r * hn)
            return (1.0 - z) * n + z * h
        key = jax.random.key(seed)
        ks = jax.random.split(key, 8)
        B, K, M, d = (8, 64, 512, D)
        w_std = d ** (-0.5)
        return {'slots': jax.random.normal(ks[0], (B, K, d), jnp.float32), 'P': jax.random.normal(ks[1], (B, M, d), jnp.float32), 'Wq': jax.random.normal(ks[2], (d, d), jnp.float32) * w_std, 'Wk': jax.random.normal(ks[3], (d, d), jnp.float32) * w_std, 'Wv': jax.random.normal(ks[4], (d, d), jnp.float32) * w_std, 'gru_wih': jax.random.normal(ks[5], (3 * d, d), jnp.float32) * w_std, 'gru_whh': jax.random.normal(ks[6], (3 * d, d), jnp.float32) * w_std, 'gru_bih': jnp.zeros((3 * d,), jnp.float32), 'gru_bhh': jnp.zeros((3 * d,), jnp.float32), 'slot_norm_w': jnp.ones((d,), jnp.float32), 'input_norm_w': jnp.ones((d,), jnp.float32)}
    _L2_xattn_all = _L2_xattn_setup()
    _L2_xattn_in = {k: v for k, v in _L2_xattn_all.items() if k in ('Wq', 'Wk', 'Wv', 'gru_wih', 'gru_whh', 'gru_bih', 'gru_bhh', 'slot_norm_w', 'input_norm_w')}
    del _L2_xattn_all

    def _L2_ffn_setup():
        import jax, jax.numpy as jnp
        import numpy as np
        B, S, D, O, E, K = (4, 256, 128, 128, 8, 2)
        key = jax.random.key(seed)
        ks = jax.random.split(key, 5)
        scale_in = 1.0 / np.sqrt(D)
        x = jax.random.normal(ks[0], (B, S, D), dtype=jnp.float32)
        gate_w = jax.random.uniform(ks[1], (E, D), jnp.float32, -scale_in, scale_in)
        gate_b = jax.random.uniform(ks[2], (E,), jnp.float32, -scale_in, scale_in)
        expert_w = jax.random.uniform(ks[3], (E, D, O), jnp.float32, -scale_in, scale_in)
        expert_b = jax.random.uniform(ks[4], (E, O), jnp.float32, -scale_in, scale_in)
        return {'x': x, 'gate_w': gate_w, 'gate_b': gate_b, 'expert_w': expert_w, 'expert_b': expert_b}
    _L2_ffn_all = _L2_ffn_setup()
    _L2_ffn_in = {k: v for k, v in _L2_ffn_all.items() if k in ('gate_w', 'gate_b', 'expert_w', 'expert_b')}
    del _L2_ffn_all

    def _L3_xattn_setup():
        import jax, jax.numpy as jnp
        import numpy as np
        B, NQ, NK, DQ, DV = (8, 256, 256, 128, 128)
        NEG = -1000000000.0
        key = jax.random.key(seed)
        kq, kk, kv = jax.random.split(key, 3)
        queries = jax.random.normal(kq, (B, NQ, DQ), dtype=jnp.float32)
        keys = jax.random.normal(kk, (B, NK, DQ), dtype=jnp.float32)
        values = jax.random.normal(kv, (B, NK, DV), dtype=jnp.float32)
        i = jnp.arange(NQ)[:, None]
        j = jnp.arange(NK)[None, :]
        attention_mask = jnp.where(j > i, jnp.float32(NEG), jnp.float32(0.0))
        attention_mask = jnp.broadcast_to(attention_mask, (B, NQ, NK)).copy()
        return {'queries': queries, 'keys': keys, 'values': values, 'attention_mask': attention_mask}
    _L3_xattn_all = _L3_xattn_setup()
    _L3_xattn_in = {k: v for k, v in _L3_xattn_all.items() if k in ()}
    del _L3_xattn_all

    def _L3_ffn_setup():
        import jax, jax.numpy as jnp
        import numpy as np
        DIM = 128

        def _reference_tuple_inner(x, W_r, W_k, W_v, mu_r, mu_k):
            B, T, C = x.shape
            x_prev = jnp.concatenate([jnp.zeros((B, 1, C), x.dtype), x[:, :-1, :]], axis=1)
            xr = mu_r * x + (1.0 - mu_r) * x_prev
            xk = mu_k * x + (1.0 - mu_k) * x_prev
            r = jax.nn.sigmoid(jnp.einsum('btc,dc->btd', xr, W_r))
            k = jnp.einsum('btc,dc->btd', xk, W_k)
            k_act = jnp.square(jax.nn.relu(k))
            out = r * jnp.einsum('btc,dc->btd', k_act, W_v)
            new_state = x[:, -1, :]
            return (out, new_state)
        key = jax.random.key(seed)
        ks = jax.random.split(key, 6)
        B, T, C = (8, 256, DIM)
        x = jax.random.normal(ks[0], (B, T, C), dtype=jnp.float32)
        s = 1.0 / np.sqrt(C)
        W_r = jax.random.uniform(ks[1], (C, C), jnp.float32, -s, s)
        W_k = jax.random.uniform(ks[2], (C, C), jnp.float32, -s, s)
        W_v = jax.random.uniform(ks[3], (C, C), jnp.float32, -s, s)
        mu_r = jax.random.uniform(ks[4], (C,), jnp.float32)
        mu_k = jax.random.uniform(ks[5], (C,), jnp.float32)
        return {'x': x, 'W_r': W_r, 'W_k': W_k, 'W_v': W_v, 'mu_r': mu_r, 'mu_k': mu_k}
    _L3_ffn_all = _L3_ffn_setup()
    _L3_ffn_in = {k: v for k, v in _L3_ffn_all.items() if k in ('W_r', 'W_k', 'W_v', 'mu_r', 'mu_k')}
    del _L3_ffn_all
    return {'x': x, 'ctx_1024': ctx_1024, 'mask_BxSxS2_if1': mask_BxSxS2_if1, 'mask_Bx1xSxS2_ik1': mask_Bx1xSxS2_ik1, 'mask_BxSxS2_fk0': mask_BxSxS2_fk0, 'L0_xattn_Wq': _L0_xattn_in['Wq'], 'L0_xattn_bq': _L0_xattn_in['bq'], 'L0_xattn_Wk': _L0_xattn_in['Wk'], 'L0_xattn_bk': _L0_xattn_in['bk'], 'L0_xattn_Wv': _L0_xattn_in['Wv'], 'L0_xattn_bv': _L0_xattn_in['bv'], 'L0_xattn_Wo': _L0_xattn_in['Wo'], 'L0_xattn_bo': _L0_xattn_in['bo'], 'L0_ffn_W_in': _L0_ffn_in['W_in'], 'L0_ffn_b_in': _L0_ffn_in['b_in'], 'L0_ffn_W_out': _L0_ffn_in['W_out'], 'L1_xattn_wq': _L1_xattn_in['wq'], 'L1_xattn_wk': _L1_xattn_in['wk'], 'L1_xattn_wv': _L1_xattn_in['wv'], 'L1_xattn_wo': _L1_xattn_in['wo'], 'L1_xattn_bq': _L1_xattn_in['bq'], 'L1_xattn_bk': _L1_xattn_in['bk'], 'L1_xattn_bv': _L1_xattn_in['bv'], 'L1_xattn_bo': _L1_xattn_in['bo'], 'L1_ffn_Wg': _L1_ffn_in['Wg'], 'L1_ffn_bias_corr': _L1_ffn_in['bias_corr'], 'L1_ffn_W1': _L1_ffn_in['W1'], 'L1_ffn_W2': _L1_ffn_in['W2'], 'L1_ffn_Ws1': _L1_ffn_in['Ws1'], 'L1_ffn_Ws2': _L1_ffn_in['Ws2'], 'L2_xattn_Wq': _L2_xattn_in['Wq'], 'L2_xattn_Wk': _L2_xattn_in['Wk'], 'L2_xattn_Wv': _L2_xattn_in['Wv'], 'L2_xattn_gru_wih': _L2_xattn_in['gru_wih'], 'L2_xattn_gru_whh': _L2_xattn_in['gru_whh'], 'L2_xattn_gru_bih': _L2_xattn_in['gru_bih'], 'L2_xattn_gru_bhh': _L2_xattn_in['gru_bhh'], 'L2_xattn_slot_norm_w': _L2_xattn_in['slot_norm_w'], 'L2_xattn_input_norm_w': _L2_xattn_in['input_norm_w'], 'L2_ffn_gate_w': _L2_ffn_in['gate_w'], 'L2_ffn_gate_b': _L2_ffn_in['gate_b'], 'L2_ffn_expert_w': _L2_ffn_in['expert_w'], 'L2_ffn_expert_b': _L2_ffn_in['expert_b'], 'L3_ffn_W_r': _L3_ffn_in['W_r'], 'L3_ffn_W_k': _L3_ffn_in['W_k'], 'L3_ffn_W_v': _L3_ffn_in['W_v'], 'L3_ffn_mu_r': _L3_ffn_in['mu_r'], 'L3_ffn_mu_k': _L3_ffn_in['mu_k']}

def reference(x, ctx_1024, mask_BxSxS2_if1, mask_Bx1xSxS2_ik1, mask_BxSxS2_fk0, L0_xattn_Wq, L0_xattn_bq, L0_xattn_Wk, L0_xattn_bk, L0_xattn_Wv, L0_xattn_bv, L0_xattn_Wo, L0_xattn_bo, L0_ffn_W_in, L0_ffn_b_in, L0_ffn_W_out, L1_xattn_wq, L1_xattn_wk, L1_xattn_wv, L1_xattn_wo, L1_xattn_bq, L1_xattn_bk, L1_xattn_bv, L1_xattn_bo, L1_ffn_Wg, L1_ffn_bias_corr, L1_ffn_W1, L1_ffn_W2, L1_ffn_Ws1, L1_ffn_Ws2, L2_xattn_Wq, L2_xattn_Wk, L2_xattn_Wv, L2_xattn_gru_wih, L2_xattn_gru_whh, L2_xattn_gru_bih, L2_xattn_gru_bhh, L2_xattn_slot_norm_w, L2_xattn_input_norm_w, L2_ffn_gate_w, L2_ffn_gate_b, L2_ffn_expert_w, L2_ffn_expert_b, L3_ffn_W_r, L3_ffn_W_k, L3_ffn_W_v, L3_ffn_mu_r, L3_ffn_mu_k):
    import jax
    import jax.numpy as jnp

    def _L0_xattn_ref(x, y, mask, Wq, bq, Wk, bk, Wv, bv, Wo, bo):
        import jax, jax.numpy as jnp
        import numpy as np
        EMB, HEADS = (128, 16)
        HEAD_DIM = EMB // HEADS

        def _linear(x, W, b):
            return jnp.einsum('bse,oe->bso', x, W) + b
        B, S, _ = x.shape
        q = _linear(x, Wq, bq).reshape(B, S, HEADS, HEAD_DIM).transpose(0, 2, 1, 3)
        k = _linear(y, Wk, bk).reshape(B, -1, HEADS, HEAD_DIM).transpose(0, 2, 1, 3)
        v = _linear(y, Wv, bv).reshape(B, -1, HEADS, HEAD_DIM).transpose(0, 2, 1, 3)
        score = jnp.einsum('bhqd,bhkd->bhqk', q, k) / jnp.sqrt(jnp.float32(HEAD_DIM))
        weights = jax.nn.softmax(score, axis=-1)
        attn = jnp.einsum('bhqk,bhkd->bhqd', weights, v)
        attn = attn.transpose(0, 2, 1, 3).reshape(B, S, EMB)
        return _linear(attn, Wo, bo)

    def _L0_ffn_ref(oldx, W_in, b_in, W_out):
        import jax, jax.numpy as jnp
        import numpy as np
        DIM = 128
        DEPTH = 7
        PAR = 8
        N_NODES = 2 ** (DEPTH + 1) - 1
        WIDTH = PAR * N_NODES
        x = oldx.reshape(-1, DIM)
        B = x.shape[0]
        logits = x @ W_in.T + b_in
        decisions = (logits > 0).astype(jnp.int32).reshape(B, PAR, N_NODES)
        acts = jax.nn.silu(logits).reshape(B, PAR, N_NODES)
        current = jnp.zeros((B, PAR), dtype=jnp.int32)
        dmap = jax.nn.one_hot(current, N_NODES, dtype=acts.dtype)
        for d in range(DEPTH):
            cur_platform = 2 ** d - 1
            next_platform = 2 ** (d + 1) - 1
            moves = jnp.take_along_axis(decisions, current[..., None], axis=2)[..., 0]
            current = (current - cur_platform) * 2 + moves + next_platform
            dmap = dmap + jax.nn.one_hot(current, N_NODES, dtype=acts.dtype)
        masked = acts * jax.lax.stop_gradient(dmap)
        out = masked.reshape(B, WIDTH) @ W_out.T
        return out.reshape(oldx.shape)

    def _L1_xattn_ref(query, key, value, mask, wq, wk, wv, wo, bq, bk, bv, bo):
        import jax, jax.numpy as jnp
        import numpy as np
        DIM = 128
        HEADS = 16
        HEAD_DIM = DIM // HEADS
        B, Tq, C = query.shape
        Tk = key.shape[1]
        scale = 1.0 / np.sqrt(HEAD_DIM)
        q = (query @ wq.T + bq).reshape(B, Tq, HEADS, HEAD_DIM).transpose(0, 2, 1, 3)
        k = (key @ wk.T + bk).reshape(B, Tk, HEADS, HEAD_DIM).transpose(0, 2, 1, 3)
        v = (value @ wv.T + bv).reshape(B, Tk, HEADS, HEAD_DIM).transpose(0, 2, 1, 3)
        scores = jnp.einsum('bhqd,bhkd->bhqk', q, k) * scale
        scores = jnp.clip(scores, -100.0, 100.0)
        scores = jnp.where(mask == 0, -jnp.inf, scores)
        attn = jax.nn.softmax(scores, axis=-1)
        out = jnp.einsum('bhqk,bhkd->bhqd', attn, v)
        out = out.transpose(0, 2, 1, 3).reshape(B, Tq, HEADS * HEAD_DIM)
        return out @ wo.T + bo

    def _L1_ffn_ref(hidden_states, Wg, bias_corr, W1, W2, Ws1, Ws2):
        import jax, jax.numpy as jnp
        import numpy as np
        H = 128
        I = 64
        IS = 128
        E = 16
        G = 4
        TOPK_G = 2
        TOPK = 4
        SCALE = 2.5
        B, S = (2, 128)

        def _relu2(x):
            r = jax.nn.relu(x)
            return r * r

        def _route(scores, bias_corr):
            T = scores.shape[0]
            s_choice = scores + bias_corr
            gs = s_choice.reshape(T, G, E // G)
            group_scores = jnp.sum(jax.lax.top_k(gs, 2)[0], axis=-1)
            gidx = jax.lax.top_k(group_scores, TOPK_G)[1]
            gmask = jnp.sum(jax.nn.one_hot(gidx, G, dtype=scores.dtype), axis=1)
            smask = jnp.repeat(gmask, E // G, axis=1)
            masked = jnp.where(smask > 0, s_choice, 0.0)
            topk_idx = jax.lax.top_k(masked, TOPK)[1]
            topk_w = jnp.take_along_axis(scores, topk_idx, axis=1)
            topk_w = topk_w / (jnp.sum(topk_w, axis=-1, keepdims=True) + 1e-20)
            topk_w = topk_w * SCALE
            return (topk_idx, topk_w)
        b, s, h = hidden_states.shape
        flat = hidden_states.reshape(-1, h)
        T = flat.shape[0]
        logits = flat.astype(jnp.float32) @ Wg.T
        scores = jax.nn.sigmoid(logits)
        topk_idx, topk_w = _route(scores, bias_corr)
        topk_w = topk_w.astype(hidden_states.dtype)
        cw = jnp.zeros((T, E), flat.dtype)
        cw = cw.at[jnp.arange(T)[:, None], topk_idx].add(topk_w)
        hid = _relu2(jnp.einsum('th,eih->eti', flat, W1))
        y = jnp.einsum('eti,ehi->eth', hid, W2)
        out = jnp.einsum('eth,te->th', y, cw)
        shared = _relu2(flat @ Ws1.T) @ Ws2.T
        return (out + shared).reshape(b, s, h)

    def _L2_xattn_ref(slots, P, Wq, Wk, Wv, gru_wih, gru_whh, gru_bih, gru_bhh, slot_norm_w, input_norm_w):
        import jax, jax.numpy as jnp
        import numpy as np
        D = 128
        NUM_ITERS = 3
        EPS = 1e-06
        SCALE = D ** (-0.5)

        def rmsnorm(x, w, eps=EPS):
            return x * jax.lax.rsqrt(jnp.mean(x * x, axis=-1, keepdims=True) + eps) * w

        def gru_cell(x, h, wih, whh, bih, bhh):
            gx = x @ wih.T + bih
            gh = h @ whh.T + bhh
            xr, xz, xn = jnp.split(gx, 3, axis=-1)
            hr, hz, hn = jnp.split(gh, 3, axis=-1)
            r = jax.nn.sigmoid(xr + hr)
            z = jax.nn.sigmoid(xz + hz)
            n = jnp.tanh(xn + r * hn)
            return (1.0 - z) * n + z * h
        Pn = rmsnorm(P, input_norm_w)
        k_proj = Pn @ Wk.T
        v_proj = Pn @ Wv.T
        for _ in range(NUM_ITERS):
            sn = rmsnorm(slots, slot_norm_w)
            q_proj = sn @ Wq.T
            scores = jnp.einsum('bkd,bmd->bkm', q_proj, k_proj) * SCALE
            attn = jax.nn.softmax(scores, axis=-2)
            attn = attn / (jnp.sum(attn, axis=-1, keepdims=True) + EPS)
            updates = jnp.einsum('bkm,bmd->bkd', attn, v_proj)
            slots = gru_cell(updates, slots, gru_wih, gru_whh, gru_bih, gru_bhh)
        return slots

    def _L2_ffn_ref(x, gate_w, gate_b, expert_w, expert_b):
        import jax, jax.numpy as jnp
        import numpy as np
        B, S, D, O, E, K = (4, 256, 128, 128, 8, 2)
        logits = jnp.einsum('bsd,ed->bse', x, gate_w) + gate_b
        if K < E:
            topv, topi = jax.lax.top_k(logits, K)
            keep = jax.nn.one_hot(topi, E, dtype=jnp.float32).sum(axis=-2)
            logits = jnp.where(keep > 0, logits, -jnp.inf)
        gate_score = jax.nn.softmax(logits, axis=-1)
        expert_out = jnp.einsum('bsd,edo->bseo', x, expert_w) + expert_b
        out = jnp.einsum('bseo,bse->bso', expert_out, gate_score)
        return out

    def _L3_xattn_ref(queries, keys, values, attention_mask):
        import jax, jax.numpy as jnp
        import numpy as np
        B, NQ, NK, DQ, DV = (8, 256, 256, 128, 128)
        NEG = -1000000000.0
        d_keys = jnp.sqrt(jnp.float32(keys.shape[-1]))
        logits = jnp.einsum('bqd,bkd->bqk', queries, keys) / d_keys
        logits = jnp.where(attention_mask < -1.0, attention_mask, logits)
        attn = jax.nn.softmax(logits, axis=-1)
        attn = jnp.where(jnp.isnan(attn), jnp.float32(0.0), attn)
        return jnp.einsum('bqk,bkv->bqv', attn, values)

    def _L3_ffn_ref(x, W_r, W_k, W_v, mu_r, mu_k):
        import jax, jax.numpy as jnp
        import numpy as np
        DIM = 128

        def _reference_tuple_inner(x, W_r, W_k, W_v, mu_r, mu_k):
            B, T, C = x.shape
            x_prev = jnp.concatenate([jnp.zeros((B, 1, C), x.dtype), x[:, :-1, :]], axis=1)
            xr = mu_r * x + (1.0 - mu_r) * x_prev
            xk = mu_k * x + (1.0 - mu_k) * x_prev
            r = jax.nn.sigmoid(jnp.einsum('btc,dc->btd', xr, W_r))
            k = jnp.einsum('btc,dc->btd', xk, W_k)
            k_act = jnp.square(jax.nn.relu(k))
            out = r * jnp.einsum('btc,dc->btd', k_act, W_v)
            new_state = x[:, -1, :]
            return (out, new_state)
        return _reference_tuple_inner(x, W_r, W_k, W_v, mu_r, mu_k)[0]
    x = x + _L0_xattn_ref(_layernorm(x, axis=-1), ctx_1024, mask_BxSxS2_if1, L0_xattn_Wq, L0_xattn_bq, L0_xattn_Wk, L0_xattn_bk, L0_xattn_Wv, L0_xattn_bv, L0_xattn_Wo, L0_xattn_bo)
    x = x + _L0_ffn_ref(_layernorm(x, axis=-1), L0_ffn_W_in, L0_ffn_b_in, L0_ffn_W_out)
    x = x + _L1_xattn_ref(_layernorm(x, axis=-1), ctx_1024, ctx_1024, mask_Bx1xSxS2_ik1, L1_xattn_wq, L1_xattn_wk, L1_xattn_wv, L1_xattn_wo, L1_xattn_bq, L1_xattn_bk, L1_xattn_bv, L1_xattn_bo)
    x = x + _L1_ffn_ref(_layernorm(x, axis=-1), L1_ffn_Wg, L1_ffn_bias_corr, L1_ffn_W1, L1_ffn_W2, L1_ffn_Ws1, L1_ffn_Ws2)
    x = x + _L2_xattn_ref(_layernorm(x, axis=-1), ctx_1024, L2_xattn_Wq, L2_xattn_Wk, L2_xattn_Wv, L2_xattn_gru_wih, L2_xattn_gru_whh, L2_xattn_gru_bih, L2_xattn_gru_bhh, L2_xattn_slot_norm_w, L2_xattn_input_norm_w)
    x = x + _L2_ffn_ref(_layernorm(x, axis=-1), L2_ffn_gate_w, L2_ffn_gate_b, L2_ffn_expert_w, L2_ffn_expert_b)
    x = x + _L3_xattn_ref(_layernorm(x, axis=-1), ctx_1024, ctx_1024, mask_BxSxS2_fk0)
    x = x + _L3_ffn_ref(_layernorm(x, axis=-1), L3_ffn_W_r, L3_ffn_W_k, L3_ffn_W_v, L3_ffn_mu_r, L3_ffn_mu_k)
    return x

_drawn_inputs = setup_inputs


def setup_inputs(seed=0):
    import zlib

    import numpy as np

    out = dict(_drawn_inputs(seed))
    spreads = {'L1_xattn_bq': (0.0, 0.1),
     'L1_xattn_bk': (0.0, 2.0),
     'L1_xattn_bv': (0.0, 0.1),
     'L1_xattn_bo': (0.0, 0.1),
     'L2_xattn_gru_bih': (0.0, 0.1),
     'L2_xattn_gru_bhh': (0.0, 0.1),
     'L2_xattn_slot_norm_w': (1.0, 0.545),
     'L2_xattn_input_norm_w': (1.0, 0.2)}
    factors = {'L0_xattn_bk': 64.0,
     'L1_ffn_Wg': 3.414,
     'L1_ffn_bias_corr': 6.899,
     'L1_ffn_W1': 3.217,
     'L1_ffn_W2': 3.048,
     'L1_ffn_Ws1': 2.795,
     'L1_ffn_Ws2': 2.774,
     'L2_ffn_expert_b': 2.675,
     'L3_ffn_W_r': 4.365,
     'L3_ffn_mu_r': 8.0}
    for name, (base, spread) in spreads.items():
        noise = np.random.default_rng([zlib.crc32(name.encode()), seed]).standard_normal(out[name].shape)
        drawn = base * np.exp(spread * noise) if base else spread * noise
        out[name] = jnp.asarray(drawn.astype(out[name].dtype))
    for name, factor in factors.items():
        out[name] = (out[name] * factor).astype(out[name].dtype)
    return out
```

```python
from contextlib import ExitStack

import numpy as np

import concourse.bass as bass
from concourse import mybir

F32 = mybir.dt.float32
BF16 = mybir.dt.bfloat16
I32 = mybir.dt.int32
U32 = mybir.dt.uint32
ALU = mybir.AluOpType
ACT = mybir.ActivationFunctionType
AX = mybir.AxisListType

SEQS, TOK, DIM, KEYS = 32, 128, 128, 77
GROUP = 4
BLOCKS = SEQS // GROUP
COLS = GROUP * TOK
KCOLS = GROUP * KEYS
LN_EPS = 1e-5
PAIR = 2 * DIM

TREES, DEPTH = 8, 7
NODES = 2 ** (DEPTH + 1) - 1
INNER = 2 ** DEPTH - 1
CHUNK = (128, NODES - 128)

EXPERTS, EXP_HID, EXP_GROUPS, TOP_GROUPS, TOP_EXPERTS, ROUTE_SCALE = 16, 64, 4, 2, 4, 2.5
PER_GROUP = EXPERTS // EXP_GROUPS
MOE_CHUNKS = EXPERTS * EXP_HID // 128
GATED, TOP_GATED = 8, 2

HEADS = 16
HEAD_DIM = DIM // HEADS
QUAD = 4
CLIP = 100.0
SLOT_ITERS, RMS_EPS = 3, 1e-6


def engine_loop(engine, body):
    with engine.Fori(0, BLOCKS - 1) as n:
        body(n, True)
    body(BLOCKS - 1, False)


def bc(ap, at, size):
    a = ap.unsqueeze(at)
    shape = list(a.shape)
    shape[at] = size
    return a.broadcast_to(shape)


class Chip:

    def __init__(self, nc, top, dram):
        self.nc, self.dram = nc, dram
        sb = lambda name, shape, dt=F32: top.enter_context(nc.sbuf_tensor(name, shape, dt))
        self.x = sb("x_res", [128, SEQS, DIM])
        self.mean_var = sb("mean_var", [128, SEQS, 2])
        self.rstd = sb("rstd", [128, SEQS])
        self.stats = sb("stats", [128, GROUP, 6])
        self.block_stats = sb("block_stats", [128, GROUP, 2])
        self.shifted_var = sb("shifted_var", [128, GROUP])
        self.carrier = sb("carrier", [128, 1])
        self.consts_set = top.enter_context(nc.semaphore("consts_set"))
        self.bank = top.enter_context(nc.psum_tensor("bank", [128, 8, 512], F32))
        self.semaphores, self.to_clear = [], []
        self.ident = sb("ident", [128, 128])
        self.ident16 = sb("ident16", [128, 128], BF16)
        self.ln_eps = sb("ln_eps", [128, GROUP])
        self.rms_eps = sb("rms_eps", [128, GROUP])
        self.minus_half = sb("minus_half", [128, GROUP])

    def clear_last(self):
        for old in self.to_clear:
            self.nc.gpsimd.sem_clear(old)

    def rows(self, n):
        return bass.ds(n * GROUP, GROUP)

    def normalise(self, n, xn):
        for j in range(GROUP):
            b = n * GROUP + j
            last = self.nc.vector.tensor_scalar(
                xn[:, j, :], self.x[:, bass.ds(b, 1), :].rearrange("p a d -> p (a d)"),
                self.mean_var[:, bass.ds(b, 1), 0], self.rstd[:, bass.ds(b, 1)],
                ALU.subtract, ALU.mult)
        return last

    def add_to_x(self, dve, n, added, ln):
        nc, r = self.nc, self.rows(n)
        nc.vector.tensor_tensor(out=self.x[:, r, :], in0=added, in1=self.x[:, r, :],
                                op=ALU.add).then_inc(ln.updated, 1)
        dve.wait_ge(ln.updated, n + 1)
        self.settle()
        self.statistics(dve, n, lambda j: self.x[:, bass.ds(n * GROUP + j, 1), :]
                        .rearrange("p a d -> p (a d)"), ln)

    def settle(self):
        self.nc.vector.memset(self.carrier[:, :], 0.0)

    def statistics(self, dve, n, seq, ln):
        nc = self.nc
        for j in range(GROUP):
            last = nc.vector.bn_stats(self.stats[:, j, :], seq(j))
        last.then_inc(ln.stats_ready, 1)
        dve.wait_ge(ln.shifted, n)
        dve.wait_ge(ln.stats_ready, n + 1)
        self.settle()
        for j in range(GROUP):
            last = nc.vector.bn_aggr(self.block_stats[:, j, :], self.stats[:, j, :])
        last.then_inc(ln.merged, 1)
        dve.wait_ge(ln.merged, n + 1)
        nc.vector.tensor_scalar(self.mean_var[:, self.rows(n), :], self.block_stats[:, :, :],
                                1.0, None, ALU.mult).then_inc(ln.var_ready, 1)

    def rstd_of(self, pool, n, ln):
        nc = self.nc
        pool.wait_ge(ln.rstd_ready, n)
        pool.wait_ge(ln.var_ready, n + 1)
        nc.gpsimd.tensor_tensor(out=self.shifted_var[:, :], in0=self.block_stats[:, :, 1],
                                in1=self.ln_eps[:, :], op=ALU.add).then_inc(ln.shifted, 1)
        pool.wait_ge(ln.shifted, n + 1)
        nc.gpsimd.tensor_tensor(out=self.rstd[:, self.rows(n)], in0=self.shifted_var[:, :],
                                in1=self.minus_half[:, :], op=ALU.pow).then_inc(ln.rstd_ready, 1)


class NormSignals:

    def __init__(self, sem):
        self.updated = sem("updated")
        self.stats_ready = sem("stats_ready")
        self.merged = sem("merged")
        self.var_ready = sem("var_ready")
        self.shifted = sem("shifted")
        self.rstd_ready = sem("rstd_ready")


def phase(chip, name):
    ctx, nc = ExitStack(), chip.nc
    chip.to_clear, own = chip.semaphores, []
    chip.semaphores = own

    def sb(t, shape, dt=F32):
        return ctx.enter_context(nc.sbuf_tensor(f"{name}_{t}", shape, dt))

    def sem(t):
        own.append(ctx.enter_context(nc.semaphore(f"{name}_{t}")))
        return own[-1]
    return ctx, sb, sem


def load_stream(chip):
    nc, d = chip.nc, chip.dram
    ctx, sb, sem = phase(chip, "load")
    with ctx:
        x_in = [sem(f"x_in{i}") for i in range(BLOCKS)]
        const_in = sem("const_in")
        ln = NormSignals(sem)
        block = ctx.enter_context(nc.Block())

        @block.sync
        def _(sp):
            for n in range(BLOCKS):
                r = slice(n * GROUP, (n + 1) * GROUP)
                sp.dma_start(chip.x[:, r, :], d["x"][r, :, :].rearrange("b t d -> t b d"))\
                    .then_inc(x_in[n], 16)
            sp.dma_start(chip.ident[:, :], d["ident"][:, :]).then_inc(const_in, 16)

        @block.vector
        def _(dve):
            for n in range(BLOCKS):
                dve.wait_ge(x_in[n], 16)
                chip.statistics(dve, n, lambda j: chip.x[:, n * GROUP + j, :],
                                ln)
            dve.wait_ge(const_in, 16)
            nc.vector.tensor_copy(chip.ident16[:, :], chip.ident[:, :])

        @block.gpsimd
        def _(pool):
            chip.clear_last()
            nc.gpsimd.memset(chip.ln_eps[:, :], LN_EPS).then_inc(chip.consts_set, 1)
            nc.gpsimd.memset(chip.rms_eps[:, :], RMS_EPS).then_inc(chip.consts_set, 1)
            nc.gpsimd.memset(chip.minus_half[:, :], -0.5).then_inc(chip.consts_set, 1)
            pool.wait_ge(chip.consts_set, 3)
            for n in range(BLOCKS):
                chip.rstd_of(pool, n, ln)


def tree_ffn(chip):
    nc, d, bank = chip.nc, chip.dram, chip.bank
    ctx, sb, sem = phase(chip, "tree")
    with ctx:
        w_in = sb("w_in", [128, TREES * NODES])
        b_in = sb("b_in", [128, TREES, 2])
        w_out = sb("w_out", [128, TREES, 2, DIM])
        ancestors = sb("ancestors", [128, NODES], BF16)
        target = sb("target", [128, 2])
        xn = sb("xn", [128, GROUP, DIM])
        xnT = sb("xnT", [128, COLS])
        decide = sb("decide", [128, 2, COLS], BF16)
        act_of = sb("act_of", [128, 4, COLS])
        masked = sb("masked", [128, 4, COLS])
        outT = sb("outT", [128, COLS])
        weights_in, xn_ready, turned, xnT_ready = (
            sem("weights_in"), sem("xn_ready"), sem("turned"), sem("xnT_ready"))
        logits_ready, decided, act_ready, counted, masked_ready, product_done = (
            sem("logits_ready"), sem("decided"), sem("act_ready"), sem("counted"),
            sem("masked_ready"), sem("product_done"))
        outT_ready, out_turned, ln = sem("outT_ready"), sem("out_turned"), NormSignals(sem)
        TURN, OUT, IN, COUNT = 0, 1, 2, 6
        PER = 2 * TREES
        block = ctx.enter_context(nc.Block())

        @block.sync
        def _(sp):
            sp.dma_start(w_in[:, :], d["tree_w_in"][:, :]).then_inc(weights_in, 16)
            sp.dma_start(b_in[:, :, :], d["tree_b_in"][:, :, :]).then_inc(weights_in, 16)
            sp.dma_start(ancestors[:, :], d["tree_ancestors"][:, :]).then_inc(weights_in, 16)
            sp.dma_start(target[:, :], d["tree_target"][:, :]).then_inc(weights_in, 16)
            sp.dma_start(w_out[:, :, :, :], d["tree_w_out"][:, :, :, :]).then_inc(weights_in, 16)

        @block.tensor
        def _(pe):
            def turn(n):
                pe.wait_ge(xn_ready, n + 1)
                for j in range(GROUP):
                    last = nc.tensor.transpose(bank[:, TURN, j * TOK:(j + 1) * TOK], xn[:, j, :],
                                               chip.ident[:, :])
                last.then_inc(turned, 1)

            def logits(n, k):
                t, c = divmod(k, 2)
                m = CHUNK[c]
                if k >= 4:
                    pe.wait_ge(act_ready, PER * n + k - 3)
                nc.tensor.matmul(bank[0:m, IN + k % 4, :],
                                 w_in[:, t * NODES + 128 * c:t * NODES + 128 * c + m], xnT[:, :],
                                 start=True, stop=True).then_inc(logits_ready, 1)

            def count(n, t):
                pe.wait_ge(decided, TREES * n + t + 1)
                for c in range(2):
                    if t:
                        pe.wait_ge(masked_ready, PER * n + 2 * t + c - 1)
                    nc.tensor.matmul(bank[0:CHUNK[c], COUNT + c, :],
                                     ancestors[0:INNER, 128 * c:128 * c + CHUNK[c]],
                                     decide[0:INNER, t % 2, :],
                                     start=True, stop=True).then_inc(counted, 1)

            def product(n, t):
                for c in range(2):
                    k = 2 * t + c
                    pe.wait_ge(masked_ready, PER * n + k + 1)
                    nc.tensor.matmul(bank[:, OUT, :], w_out[0:CHUNK[c], t, c, :],
                                     masked[0:CHUNK[c], k % 4, :],
                                     start=(k == 0), stop=(k == PER - 1)).then_inc(product_done, 1)

            def first_logits(n):
                pe.wait_ge(xnT_ready, n + 1)
                logits(n, 0)
                logits(n, 1)

            def body(n, more):
                for t in range(TREES):
                    if t < TREES - 1:
                        logits(n, 2 * t + 2)
                        logits(n, 2 * t + 3)
                    elif more:
                        turn(n + 1)
                    count(n, t)
                    if t:
                        product(n, t - 1)
                product(n, TREES - 1)
                if more:
                    first_logits(n + 1)
                pe.wait_ge(outT_ready, n + 1)
                for j in range(GROUP):
                    last = nc.tensor.transpose(bank[:, TURN, j * TOK:(j + 1) * TOK],
                                               outT[:, j * TOK:(j + 1) * TOK], chip.ident[:, :])
                last.then_inc(out_turned, 1)

            pe.wait_ge(weights_in, 80)
            turn(0)
            first_logits(0)
            engine_loop(pe, body)

        @block.scalar
        def _(act):
            def silu(n, k):
                t, c = divmod(k, 2)
                m = CHUNK[c]
                if c == 0:
                    act.wait_ge(decided, TREES * n + t + 1)
                else:
                    act.wait_ge(logits_ready, PER * n + k + 1)
                if k >= 4:
                    act.wait_ge(masked_ready, PER * n + k - 3)
                nc.scalar.activation(act_of[0:m, k % 4, :], bank[0:m, IN + k % 4, :], ACT.Silu,
                                     bias=b_in[0:m, t, c:c + 1]).then_inc(act_ready, 1)

            def take_turned(n):
                act.wait_ge(turned, n + 1)
                nc.scalar.copy(xnT[:, :], bank[:, TURN, :]).then_inc(xnT_ready, 1)

            def body(n, more):
                for k in range(2, PER):
                    silu(n, k)
                if more:
                    take_turned(n + 1)
                act.wait_ge(product_done, PER * (n + 1))
                nc.scalar.copy(outT[:, :], bank[:, OUT, :]).then_inc(outT_ready, 1)
                if more:
                    silu(n + 1, 0)
                    silu(n + 1, 1)

            act.wait_ge(weights_in, 80)
            take_turned(0)
            silu(0, 0)
            silu(0, 1)
            engine_loop(act, body)

        @block.vector
        def _(dve):
            def decisions(n, t):
                dve.wait_ge(logits_ready, PER * n + 2 * t + 1)
                if t >= 2:
                    dve.wait_ge(counted, PER * n + 2 * t - 2)
                nc.vector.tensor_scalar(decide[:, t % 2, :], bank[:, IN + (2 * t) % 4, :],
                                        b_in[:, t, 0:1], 0.0, ALU.add, ALU.is_gt)\
                    .then_inc(decided, 1)

            def mask(n, k):
                t, c = divmod(k, 2)
                m = CHUNK[c]
                dve.wait_ge(counted, PER * n + k + 1)
                dve.wait_ge(act_ready, PER * n + k + 1)
                if k >= 4:
                    dve.wait_ge(product_done, PER * n + k - 3)
                nc.vector.scalar_tensor_tensor(
                    out=masked[0:m, k % 4, :], in0=bank[0:m, COUNT + c, :],
                    scalar=target[0:m, c:c + 1], in1=act_of[0:m, k % 4, :],
                    op0=ALU.is_equal, op1=ALU.mult).then_inc(masked_ready, 1)

            def body(n, more):
                for t in range(TREES):
                    if t < TREES - 1:
                        decisions(n, t + 1)
                    mask(n, 2 * t)
                    mask(n, 2 * t + 1)
                    if t == TREES // 2 and more:
                        chip.normalise(n + 1, xn).then_inc(xn_ready, 1)
                if more:
                    decisions(n + 1, 0)
                dve.wait_ge(out_turned, n + 1)
                chip.add_to_x(dve, n, bank[:, TURN, :].rearrange("p (b d) -> p b d", b=GROUP),
                              ln)

            dve.wait_ge(weights_in, 80)
            chip.normalise(0, xn).then_inc(xn_ready, 1)
            decisions(0, 0)
            engine_loop(dve, body)

        @block.gpsimd
        def _(pool):
            chip.clear_last()
            def body(n, more):
                chip.rstd_of(pool, n, ln)
            engine_loop(pool, body)


def engine_loop_pairs(engine, body):
    with engine.Fori(0, BLOCKS // 2 - 1) as r:
        body(2 * r, 0, True)
        body(2 * r + 1, 1, True)
    body(BLOCKS - 2, 0, True)
    body(BLOCKS - 1, 1, False)


def later_wins(nc, size, sc, full, step, larger, equal_or_larger, earlier, rank):
    other, own = bc(sc, 2, size), bc(sc, 3, size)
    step(nc.vector.tensor_tensor(out=larger, in0=other, in1=own, op=ALU.is_gt))
    step(nc.vector.tensor_tensor(out=equal_or_larger, in0=other, in1=own, op=ALU.is_ge))
    step(nc.vector.tensor_tensor(out=equal_or_larger, in0=equal_or_larger, in1=bc(earlier, 1, GROUP),
                                 op=ALU.mult))
    step(nc.vector.tensor_tensor(out=larger, in0=larger, in1=equal_or_larger, op=ALU.max))
    step(nc.vector.tensor_reduce(rank, larger, AX.X, ALU.add))


def moe_ffn(chip):
    nc, d, bank = chip.nc, chip.dram, chip.bank
    ctx, sb, sem = phase(chip, "moe")
    with ctx:
        E, G, C = EXPERTS, EXP_GROUPS, MOE_CHUNKS + 1
        w_route = sb("w_route", [128, E])
        bias = sb("bias", [128, E])
        w_up = sb("w_up", [128, C, 128])
        w_down = sb("w_down", [128, C, DIM])
        spread = sb("spread", [3 * E, MOE_CHUNKS, 128], BF16)
        earlier_group = sb("earlier_group", [128, G, G])
        earlier_expert = sb("earlier_expert", [128, E, E], BF16)
        xn = sb("xn", [128, GROUP, DIM])
        xnT = sb("xnT", [128, 2, COLS])
        score = sb("score", [128, GROUP, E])
        choice = sb("choice", [128, GROUP, E])
        pair_sum = sb("pair_sum", [128, GROUP * G, 6])
        group_score = sb("group_score", [128, GROUP, G])
        group_larger = sb("group_larger", [128, GROUP, G, G])
        group_equal = sb("group_equal", [128, GROUP, G, G])
        group_rank = sb("group_rank", [128, GROUP, G])
        allowed = sb("allowed", [128, GROUP, E])
        larger = sb("larger", [128, GROUP, E, E], BF16)
        equal = sb("equal", [128, GROUP, E, E], BF16)
        rank = sb("rank", [128, GROUP, E])
        chosen = sb("chosen", [128, GROUP, E])
        total = sb("total", [128, GROUP])
        weight = sb("weight", [128, GROUP, E])
        rest = sb("rest", [128, GROUP, E])
        parts = sb("parts", [128, GROUP, 128], BF16)
        partsT = sb("partsT", [3 * E, 2, COLS], BF16)
        relu = sb("relu", [128, 3, COLS])
        weighted = sb("weighted", [128, 2, COLS])
        hidden = sb("hidden", [128, 3, COLS])
        outT = sb("outT", [128, COLS])
        weights_in, xn_ready, turned, xnT_ready = (
            sem("weights_in"), sem("xn_ready"), sem("turned"), sem("xnT_ready"))
        routed, scores_ready, step_done, parts_turned, partsT_ready = (
            sem("routed"), sem("scores_ready"), sem("step_done"), sem("parts_turned"),
            sem("partsT_ready"))
        up_ready, relu_ready, spread_ready, weighted_ready, hidden_ready, product_done = (
            sem("up_ready"), sem("relu_ready"), sem("spread_ready"), sem("weighted_ready"),
            sem("hidden_ready"), sem("product_done"))
        cleared = sem("cleared")
        outT_ready, out_turned, ln = sem("outT_ready"), sem("out_turned"), NormSignals(sem)
        TURN, ROUTE, OUT, UP, SPREAD, PARTS = 0, 1, 2, 3, 5, 7
        STEPS = 26
        partsT_bank = bank[:, PARTS, :].bitcast(BF16)
        block = ctx.enter_context(nc.Block())

        @block.sync
        def _(sp):
            for dst, name in ((w_route, "moe_w_route"), (bias, "moe_bias"), (w_up, "moe_w_up"),
                              (w_down, "moe_w_down"), (spread, "moe_spread"),
                              (earlier_group, "earlier4"), (earlier_expert, "earlier16")):
                dst = dst[:, :, :] if len(dst.shape) == 3 else dst[:, :]
                src = d[name][:, :, :] if len(dst.shape) == 3 else d[name][:, :]
                sp.dma_start(dst, src).then_inc(weights_in, 16)

        @block.tensor
        def _(pe):
            def turn(n):
                pe.wait_ge(xn_ready, n + 1)
                for j in range(GROUP):
                    last = nc.tensor.transpose(bank[:, TURN, j * TOK:(j + 1) * TOK], xn[:, j, :],
                                               chip.ident[:, :])
                last.then_inc(turned, 1)

            def route(n, u):
                pe.wait_ge(xnT_ready, n + 1)
                for j in range(GROUP):
                    last = nc.tensor.matmul(bank[:, ROUTE, j * E:(j + 1) * E],
                                            xnT[:, u, j * TOK:(j + 1) * TOK], w_route[:, :],
                                            start=True, stop=True)
                last.then_inc(routed, 1)

            def turn_parts(n):
                pe.wait_ge(step_done, STEPS * (n + 1))
                for j in range(GROUP):
                    last = nc.tensor.transpose(partsT_bank[:, j * TOK:(j + 1) * TOK], parts[:, j, :],
                                               chip.ident16[:, :])
                last.then_inc(parts_turned, 1)

            def up(n, u, k):
                if k >= 2:
                    pe.wait_ge(relu_ready, C * n + k - 1)
                nc.tensor.matmul(bank[:, UP + k % 2, :], w_up[:, k, :], xnT[:, u, :],
                                 start=True, stop=True).then_inc(up_ready, 1)
                if k < MOE_CHUNKS:
                    if k >= 2:
                        pe.wait_ge(weighted_ready, MOE_CHUNKS * n + k - 1)
                    if k == 0:
                        pe.wait_ge(partsT_ready, n + 1)
                    nc.tensor.matmul(bank[:, SPREAD + k % 2, :], spread[:, k, :], partsT[:, u, :],
                                     start=True, stop=True).then_inc(spread_ready, 1)

            def product(n, k):
                pe.wait_ge(hidden_ready, C * n + k + 1)
                nc.tensor.matmul(bank[:, OUT, :], w_down[:, k, :], hidden[:, k % 3, :],
                                 start=(k == 0), stop=(k == C - 1)).then_inc(product_done, 1)

            def body(n, u, more):
                for k in range(C):
                    if k == 0 and more:
                        turn(n + 1)
                    if k == 2 and more:
                        route(n + 1, 1 - u)
                    if k + 2 < C:
                        up(n, u, k + 2)
                    if k == C - 1 and more:
                        turn_parts(n + 1)
                    product(n, k)
                if more:
                    up(n + 1, 1 - u, 0)
                    up(n + 1, 1 - u, 1)
                pe.wait_ge(outT_ready, n + 1)
                for j in range(GROUP):
                    last = nc.tensor.transpose(bank[:, TURN, j * TOK:(j + 1) * TOK],
                                               outT[:, j * TOK:(j + 1) * TOK], chip.ident[:, :])
                last.then_inc(out_turned, 1)

            pe.wait_ge(weights_in, 7 * 16)
            turn(0)
            route(0, 0)
            turn_parts(0)
            up(0, 0, 0)
            up(0, 0, 1)
            engine_loop_pairs(pe, body)

        @block.scalar
        def _(act):
            def take_turned(n, u):
                act.wait_ge(turned, n + 1)
                nc.scalar.copy(xnT[:, u, :], bank[:, TURN, :]).then_inc(xnT_ready, 1)

            def scores(n):
                act.wait_ge(routed, n + 1)
                nc.scalar.activation(score[:, :, :].rearrange("p b e -> p (b e)"),
                                     bank[:, ROUTE, 0:GROUP * E], ACT.Sigmoid)\
                    .then_inc(scores_ready, 1)

            def take_parts(n, u):
                act.wait_ge(parts_turned, n + 1)
                nc.scalar.copy(partsT[:, u, :], partsT_bank[0:3 * E, 0:COLS])\
                    .then_inc(partsT_ready, 1)

            def rectify(n, k):
                act.wait_ge(up_ready, C * n + k + 1)
                if k >= 3:
                    act.wait_ge(hidden_ready, C * n + k - 2)
                nc.scalar.activation(relu[:, k % 3, :], bank[:, UP + k % 2, :], ACT.Relu)\
                    .then_inc(relu_ready, 1)

            def body(n, u, more):
                for k in range(C):
                    if k == 0 and more:
                        take_turned(n + 1, 1 - u)
                    if k + 2 < C:
                        rectify(n, k + 2)
                    if k == 2 and more:
                        scores(n + 1)
                    if k == C - 1 and more:
                        take_parts(n + 1, 1 - u)
                act.wait_ge(product_done, C * (n + 1))
                nc.scalar.copy(outT[:, :], bank[:, OUT, :]).then_inc(outT_ready, 1)
                if more:
                    rectify(n + 1, 0)
                    rectify(n + 1, 1)

            take_turned(0, 0)
            scores(0)
            take_parts(0, 0)
            rectify(0, 0)
            rectify(0, 1)
            engine_loop_pairs(act, body)

        @block.vector
        def _(dve):
            def routing(n):
                done = [0]

                def step(instruction):
                    instruction.then_inc(step_done, 1)
                    done[0] += 1
                    dve.wait_ge(step_done, STEPS * n + done[0])
                quads = lambda t: t[:, :, :].rearrange("p b (g e) -> p (b g) e", e=PER_GROUP)
                flat = lambda t: t[:, :, :].rearrange("p b g -> p (b g)")

                def group_sums():
                    dve.wait_ge(scores_ready, n + 1)
                    step(nc.vector.tensor_tensor(out=choice[:, :, :], in0=score[:, :, :],
                                                 in1=bc(bias[:, :], 1, GROUP), op=ALU.add))
                    c, at = quads(choice), 0
                    for apart in range(1, PER_GROUP):
                        size = PER_GROUP - apart
                        add = nc.vector.tensor_tensor(out=pair_sum[:, :, at:at + size],
                                                      in0=c[:, :, 0:size], in1=c[:, :, apart:],
                                                      op=ALU.add)
                        at += size
                        step(add)
                    step(nc.vector.tensor_reduce(flat(group_score), pair_sum[:, :, :], AX.X, ALU.max))

                def group_ranks():
                    later_wins(nc, G, group_score[:, :, :], None, step, group_larger[:, :, :, :],
                               group_equal[:, :, :, :], earlier_group[:, :, :], group_rank[:, :, :])

                def allow():
                    step(nc.vector.scalar_tensor_tensor(
                        out=quads(allowed), in0=bc(flat(group_rank), 2, PER_GROUP),
                        scalar=float(TOP_GROUPS), in1=quads(choice), op0=ALU.is_lt, op1=ALU.mult))

                def expert_ranks():
                    later_wins(nc, E, allowed[:, :, :], None, step, larger[:, :, :, :],
                               equal[:, :, :, :], earlier_expert[:, :, :], rank[:, :, :])

                def weigh():
                    step(nc.vector.scalar_tensor_tensor(
                        out=chosen[:, :, :], in0=rank[:, :, :], scalar=float(TOP_EXPERTS),
                        in1=score[:, :, :], op0=ALU.is_lt, op1=ALU.mult))
                    step(nc.vector.tensor_reduce(total[:, :], chosen[:, :, :], AX.X, ALU.add))
                    step(nc.vector.tensor_scalar(total[:, :], total[:, :], 1e-20, None, ALU.add))
                    step(nc.vector.reciprocal(total[:, :], total[:, :]))
                    step(nc.vector.scalar_tensor_tensor(
                        out=weight[:, :, :], in0=chosen[:, :, :], scalar=ROUTE_SCALE,
                        in1=bc(total[:, :], 2, E), op0=ALU.mult, op1=ALU.mult))

                def split():
                    bf16_parts(nc, step, weight[:, :, :], rest[:, :, :],
                               [parts[:, :, i * E:(i + 1) * E] for i in range(3)])
                return [group_sums, group_ranks, allow, expert_ranks, weigh, split]

            def weigh_hidden(n, k):
                dve.wait_ge(relu_ready, C * n + k + 1)
                dve.wait_ge(spread_ready, MOE_CHUNKS * n + k + 1)
                if k >= 2:
                    dve.wait_ge(hidden_ready, C * n + k - 1)
                nc.vector.tensor_tensor(out=weighted[:, k % 2, :], in0=relu[:, k % 3, :],
                                        in1=bank[:, SPREAD + k % 2, :], op=ALU.mult)\
                    .then_inc(weighted_ready, 1)

            def body(n, u, more):
                pieces = routing(n + 1) if more else []
                if more:
                    chip.normalise(n + 1, xn).then_inc(xn_ready, 1)
                for k in range(MOE_CHUNKS):
                    weigh_hidden(n, k)
                    if k >= 2 and pieces:
                        pieces.pop(0)()
                dve.wait_ge(out_turned, n + 1)
                chip.add_to_x(dve, n, bank[:, TURN, :].rearrange("p (b d) -> p b d", b=GROUP), ln)

            dve.wait_ge(weights_in, 7 * 16)
            nc.vector.memset(parts[:, :, :], 0.0).then_inc(cleared, 1)
            dve.wait_ge(cleared, 1)
            chip.normalise(0, xn).then_inc(xn_ready, 1)
            for piece in routing(0):
                piece()
            engine_loop_pairs(dve, body)

        @block.gpsimd
        def _(pool):
            chip.clear_last()
            def hide(n, k):
                if k < MOE_CHUNKS:
                    pool.wait_ge(weighted_ready, MOE_CHUNKS * n + k + 1)
                    other = weighted[:, k % 2, :]
                else:
                    pool.wait_ge(relu_ready, C * n + k + 1)
                    other = relu[:, k % 3, :]
                if k >= 3:
                    pool.wait_ge(product_done, C * n + k - 2)
                nc.gpsimd.tensor_tensor(out=hidden[:, k % 3, :], in0=relu[:, k % 3, :], in1=other,
                                        op=ALU.mult).then_inc(hidden_ready, 1)

            def body(n, u, more):
                for k in range(C):
                    hide(n, k)
                chip.rstd_of(pool, n, ln)
            engine_loop_pairs(pool, body)


def bf16_parts(nc, step, value, rest, parts):
    step(nc.vector.tensor_copy(parts[0], value))
    step(nc.vector.tensor_tensor(out=rest, in0=value, in1=parts[0], op=ALU.subtract))
    step(nc.vector.tensor_copy(parts[1], rest))
    step(nc.vector.tensor_tensor(out=rest, in0=rest, in1=parts[1], op=ALU.subtract))
    step(nc.vector.tensor_copy(parts[2], rest))


def gated_ffn(chip):
    nc, d, bank = chip.nc, chip.dram, chip.bank
    ctx, sb, sem = phase(chip, "gated")
    with ctx:
        E = GATED
        w_gate = sb("w_gate", [128, E])
        b_gate = sb("b_gate", [128, E])
        w_expert = sb("w_expert", [128, E, DIM])
        b_expert = sb("b_expert", [3 * E, DIM])
        spread = sb("spread", [3 * E, E, 128], BF16)
        earlier = sb("earlier", [128, E, E], BF16)
        xn = sb("xn", [128, GROUP, DIM])
        xnT = sb("xnT", [128, 2, COLS])
        logit = sb("logit", [128, GROUP, E])
        larger = sb("larger", [128, GROUP, E, E], BF16)
        equal = sb("equal", [128, GROUP, E, E], BF16)
        rank = sb("rank", [128, GROUP, E])
        best = sb("best", [128, GROUP])
        shifted = sb("shifted", [128, GROUP, E])
        power = sb("power", [128, GROUP, E])
        kept = sb("kept", [128, GROUP, E])
        total = sb("total", [128, GROUP])
        gate = sb("gate", [128, GROUP, E])
        rest = sb("rest", [128, GROUP, E])
        parts = sb("parts", [128, GROUP, 3, E], BF16)
        partsT = sb("partsT", [3 * E, 2, COLS], BF16)
        partsT32 = sb("partsT32", [3 * E, 2, COLS])
        gated = sb("gated", [128, 3, COLS])
        outT = sb("outT", [128, COLS])
        weights_in, xn_ready, turned, xnT_ready = (
            sem("weights_in"), sem("xn_ready"), sem("turned"), sem("xnT_ready"))
        routed, shift_ready, power_ready, step_done, parts_turned, partsT_ready = (
            sem("routed"), sem("shift_ready"), sem("power_ready"), sem("step_done"),
            sem("parts_turned"), sem("partsT_ready"))
        spread_ready, gated_ready, product_done = (
            sem("spread_ready"), sem("gated_ready"), sem("product_done"))
        outT_ready, out_turned, ln = sem("outT_ready"), sem("out_turned"), NormSignals(sem)
        TURN, ROUTE, OUT, SPREAD, PARTS = 0, 1, 2, 3, 7
        SPREADS = 4
        partsT_bank = bank[:, PARTS, :].bitcast(BF16)
        STEPS = 17
        block = ctx.enter_context(nc.Block())

        @block.sync
        def _(sp):
            for dst, name in ((w_gate, "gated_w_gate"), (b_gate, "gated_b_gate"),
                              (w_expert, "gated_w"), (b_expert, "gated_b"),
                              (spread, "gated_spread"), (earlier, "earlier8")):
                dst = dst[:, :, :] if len(dst.shape) == 3 else dst[:, :]
                src = d[name][:, :, :] if len(dst.shape) == 3 else d[name][:, :]
                sp.dma_start(dst, src).then_inc(weights_in, 16)

        @block.tensor
        def _(pe):
            def turn(n):
                pe.wait_ge(xn_ready, n + 1)
                for j in range(GROUP):
                    last = nc.tensor.transpose(bank[:, TURN, j * TOK:(j + 1) * TOK], xn[:, j, :],
                                               chip.ident[:, :])
                last.then_inc(turned, 1)

            def route(n, u):
                pe.wait_ge(xnT_ready, n + 1)
                for j in range(GROUP):
                    last = nc.tensor.matmul(bank[:, ROUTE, j * E:(j + 1) * E],
                                            xnT[:, u, j * TOK:(j + 1) * TOK], w_gate[:, :],
                                            start=True, stop=True)
                last.then_inc(routed, 1)

            def turn_parts(n):
                pe.wait_ge(step_done, STEPS * (n + 1))
                for j in range(GROUP):
                    last = nc.tensor.transpose(partsT_bank[0:3 * E, j * TOK:(j + 1) * TOK],
                                               parts[:, j, :, :].rearrange("p a e -> p (a e)"),
                                               chip.ident16[:, :])
                last.then_inc(parts_turned, 1)

            def spread_gate(n, u, k):
                if k == 0:
                    pe.wait_ge(partsT_ready, 2 * (n + 1))
                if k >= SPREADS:
                    pe.wait_ge(gated_ready, E * n + k - SPREADS + 1)
                nc.tensor.matmul(bank[:, SPREAD + k % SPREADS, :], spread[:, k, :], partsT[:, u, :],
                                 start=True, stop=True).then_inc(spread_ready, 1)

            def product(n, k):
                pe.wait_ge(gated_ready, E * n + k + 1)
                nc.tensor.matmul(bank[:, OUT, :], w_expert[:, k, :], gated[:, k % 3, :],
                                 start=False, stop=(k == E - 1)).then_inc(product_done, 1)

            def body(n, u, more):
                nc.tensor.matmul(bank[:, OUT, :], b_expert[:, :], partsT32[:, u, :],
                                 start=True, stop=False)
                for k in range(E):
                    if k == 0 and more:
                        turn(n + 1)
                    if k == 1 and more:
                        route(n + 1, 1 - u)
                    if k + 3 < E:
                        spread_gate(n, u, k + 3)
                    product(n, k)
                if more:
                    turn_parts(n + 1)
                    for k in range(3):
                        spread_gate(n + 1, 1 - u, k)
                pe.wait_ge(outT_ready, n + 1)
                for j in range(GROUP):
                    last = nc.tensor.transpose(bank[:, TURN, j * TOK:(j + 1) * TOK],
                                               outT[:, j * TOK:(j + 1) * TOK], chip.ident[:, :])
                last.then_inc(out_turned, 1)

            pe.wait_ge(weights_in, 6 * 16)
            turn(0)
            route(0, 0)
            turn_parts(0)
            for k in range(3):
                spread_gate(0, 0, k)
            engine_loop_pairs(pe, body)

        @block.scalar
        def _(act):
            def take_turned(n, u):
                act.wait_ge(turned, n + 1)
                nc.scalar.copy(xnT[:, u, :], bank[:, TURN, :]).then_inc(xnT_ready, 1)

            def exps(n):
                act.wait_ge(shift_ready, n + 1)
                nc.scalar.activation(power[:, :, :].rearrange("p b e -> p (b e)"),
                                     shifted[:, :, :].rearrange("p b e -> p (b e)"), ACT.Exp)\
                    .then_inc(power_ready, 1)

            def take_parts(n, u):
                act.wait_ge(parts_turned, n + 1)
                nc.scalar.copy(partsT[:, u, :], partsT_bank[0:3 * E, 0:COLS])\
                    .then_inc(partsT_ready, 1)
                nc.scalar.copy(partsT32[:, u, :], partsT_bank[0:3 * E, 0:COLS])\
                    .then_inc(partsT_ready, 1)

            def body(n, u, more):
                if more:
                    take_turned(n + 1, 1 - u)
                    exps(n + 1)
                act.wait_ge(product_done, E * (n + 1))
                nc.scalar.copy(outT[:, :], bank[:, OUT, :]).then_inc(outT_ready, 1)
                if more:
                    take_parts(n + 1, 1 - u)

            take_turned(0, 0)
            exps(0)
            take_parts(0, 0)
            engine_loop_pairs(act, body)

        @block.vector
        def _(dve):
            def gates(n):
                done = [0]

                def step(instruction):
                    instruction.then_inc(step_done, 1)
                    done[0] += 1
                    dve.wait_ge(step_done, STEPS * n + done[0])

                def logits():
                    dve.wait_ge(routed, n + 1)
                    step(nc.vector.tensor_tensor(
                        out=logit[:, :, :],
                        in0=bank[:, ROUTE, 0:GROUP * E].rearrange("p (b e) -> p b e", e=E),
                        in1=bc(b_gate[:, :], 1, GROUP), op=ALU.add))
                    step(nc.vector.tensor_reduce(best[:, :], logit[:, :, :], AX.X, ALU.max))
                    step(nc.vector.tensor_tensor(out=shifted[:, :, :], in0=logit[:, :, :],
                                                 in1=bc(best[:, :], 2, E), op=ALU.subtract))
                    nc.vector.memset(chip.carrier[:, :], 0.0).then_inc(shift_ready, 1)

                def ranks():
                    later_wins(nc, E, logit[:, :, :], None, step, larger[:, :, :, :],
                               equal[:, :, :, :], earlier[:, :, :], rank[:, :, :])

                def mix():
                    dve.wait_ge(power_ready, n + 1)
                    step(nc.vector.scalar_tensor_tensor(
                        out=kept[:, :, :], in0=rank[:, :, :], scalar=float(TOP_GATED),
                        in1=power[:, :, :], op0=ALU.is_lt, op1=ALU.mult))
                    step(nc.vector.tensor_reduce(total[:, :], kept[:, :, :], AX.X, ALU.add))
                    step(nc.vector.reciprocal(total[:, :], total[:, :]))
                    step(nc.vector.tensor_tensor(out=gate[:, :, :], in0=kept[:, :, :],
                                                 in1=bc(total[:, :], 2, E), op=ALU.mult))

                def split():
                    bf16_parts(nc, step, gate[:, :, :], rest[:, :, :],
                               [parts[:, :, i, :] for i in range(3)])
                return [logits, ranks, mix, split]

            def times_gate(n, u, k):
                dve.wait_ge(spread_ready, E * n + k + 1)
                if k >= 3:
                    dve.wait_ge(product_done, E * n + k - 2)
                nc.vector.tensor_tensor(out=gated[:, k % 3, :], in0=xnT[:, u, :],
                                        in1=bank[:, SPREAD + k % SPREADS, :], op=ALU.mult)\
                    .then_inc(gated_ready, 1)

            def body(n, u, more):
                pieces = gates(n + 1) if more else []
                if more:
                    chip.normalise(n + 1, xn).then_inc(xn_ready, 1)
                for k in range(E):
                    times_gate(n, u, k)
                    if k >= 3 and pieces:
                        pieces.pop(0)()
                dve.wait_ge(out_turned, n + 1)
                chip.add_to_x(dve, n, bank[:, TURN, :].rearrange("p (b d) -> p b d", b=GROUP), ln)

            dve.wait_ge(weights_in, 6 * 16)
            chip.normalise(0, xn).then_inc(xn_ready, 1)
            for piece in gates(0):
                piece()
            engine_loop_pairs(dve, body)

        @block.gpsimd
        def _(pool):
            chip.clear_last()
            def body(n, u, more):
                chip.rstd_of(pool, n, ln)
            engine_loop_pairs(pool, body)


def heads_attention(chip, name, clipped):
    nc, d, bank = chip.nc, chip.dram, chip.bank
    ctx, sb, sem = phase(chip, name)
    with ctx:
        QUARTERS = HEADS // QUAD
        scale = HEAD_DIM ** -0.5
        w_q, w_k, w_v, w_o = (sb(t, [128, DIM]) for t in ("w_q", "w_k", "w_v", "w_o"))
        b_q, b_k = sb("b_q", [128, 1]), sb("b_k", [128, 1])
        b_v = sb("b_v", [KEYS, DIM])
        b_o = sb("b_o", [1, DIM])
        ones = sb("ones", [1, TOK])
        own_head = sb("own_head", [128, QUAD])
        ctxT = sb("ctxT", [128, GROUP, KEYS])
        xn = sb("xn", [128, GROUP, DIM])
        xnT = sb("xnT", [128, COLS])
        qT = sb("qT", [128, COLS])
        kT = sb("kT", [128, GROUP, QUAD, KEYS])
        v = sb("v", [KEYS, GROUP, HEADS, HEAD_DIM + 1])
        largest = sb("largest", [128, HEADS])
        below = sb("below", [128, HEADS, KEYS])
        powers = sb("powers", [128, HEADS, KEYS])
        powersT = sb("powersT", [KEYS, QUARTERS, QUAD * TOK])
        inverse = sb("inverse", [128, HEADS])
        heads_out = sb("heads_out", [128, GROUP, DIM])
        heads_outT = sb("heads_outT", [128, COLS])
        if clipped:
            mask = sb("mask", [128, GROUP, KEYS], I32)
            limit = sb("limit", [128, GROUP, KEYS])
            mask_in, forbidden, limit_ready = sem("mask_in"), sem("forbidden"), sem("limit_ready")
        weights_in, ctx_in, consts, xn_ready, turned, xnT_ready = (
            sem("weights_in"), sem("ctx_in"), sem("consts"), sem("xn_ready"), sem("turned"),
            sem("xnT_ready"))
        q_made, k_made, v_made, q_ready, k_ready, v_ready = (
            sem("q_made"), sem("k_made"), sem("v_made"), sem("q_ready"), sem("k_ready"),
            sem("v_ready"))
        scores_ready, scores_taken, largest_ready, below_ready, powers_ready = (
            sem("scores_ready"), sem("scores_taken"), sem("largest_ready"), sem("below_ready"),
            sem("powers_ready"))
        powers_turned, powersT_ready, heads_summed, inverse_ready, heads_out_ready = (
            sem("powers_turned"), sem("powersT_ready"), sem("heads_summed"), sem("inverse_ready"),
            sem("heads_out_ready"))
        heads_turned, heads_outT_ready, projected, ln = (
            sem("heads_turned"), sem("heads_outT_ready"), sem("projected"), NormSignals(sem))
        SCORES, TURNED, SUMS, MISC = 0, 4, 6, 7
        LOADS = [(w_q, "w_q"), (w_k, "w_k"), (w_v, "w_v"), (w_o, "w_o"), (b_q, "b_q"),
                 (b_k, "b_k"), (b_v, "b_v"), (b_o, "b_o"), (own_head, "own_head")]
        PARTS = GROUP * QUARTERS
        sums = bank[:, SUMS, 0:HEADS * (HEAD_DIM + 1)].rearrange("p (h c) -> p h c", h=HEADS)
        block = ctx.enter_context(nc.Block())

        @block.sync
        def _(sp):
            for dst, t in LOADS:
                src = d[t if t == "own_head" else f"{name}_{t}"]
                sp.dma_start(dst[:, :], src[:, :]).then_inc(weights_in, 16)

            def load(n):
                r = chip.rows(n)
                sp.dma_start(ctxT[:, :, :], d["ctxT"][:, r, :]).then_inc(ctx_in, 16)
                if clipped:
                    sp.dma_start(mask[:, :, :], d["mask"][:, r, :]).then_inc(mask_in, 16)

            def body(n, more):
                if more:
                    sp.wait_ge(k_made, n + 1)
                    sp.wait_ge(v_made, n + 1)
                    if clipped:
                        sp.wait_ge(forbidden, n + 1)
                    load(n + 1)
            load(0)
            engine_loop(sp, body)

        @block.tensor
        def _(pe):
            def turn(n):
                pe.wait_ge(xn_ready, n + 1)
                for j in range(GROUP):
                    last = nc.tensor.transpose(bank[:, MISC, j * TOK:(j + 1) * TOK], xn[:, j, :],
                                               chip.ident[:, :])
                last.then_inc(turned, 1)

            def project_in(n):
                pe.wait_ge(xnT_ready, n + 1)
                nc.tensor.matmul(bank[:, TURNED, :], w_q[:, :], xnT[:, :], start=True, stop=True)\
                    .then_inc(q_made, 1)
                pe.wait_ge(ctx_in, 16 * (n + 1))
                nc.tensor.matmul(bank[:, TURNED + 1, 0:KCOLS], w_k[:, :],
                                 ctxT[:, :, :].rearrange("p b k -> p (b k)"),
                                 start=True, stop=True).then_inc(k_made, 1)
                for j in range(GROUP):
                    last = nc.tensor.matmul(bank[0:KEYS, MISC, j * DIM:(j + 1) * DIM],
                                            ctxT[:, j, :], w_v[:, :], start=True, stop=True)
                last.then_inc(v_made, 1)

            def scores(n, j):
                m = GROUP * n + j
                if j == 0:
                    pe.wait_ge(q_ready, n + 1)
                    pe.wait_ge(k_ready, n + 1)
                pe.wait_ge(scores_taken, m)
                for g in range(QUARTERS):
                    rows = slice(32 * g, 32 * g + 32)
                    last = nc.tensor.matmul(bank[:, SCORES + g, 0:QUAD * KEYS],
                                            qT[rows, j * TOK:(j + 1) * TOK],
                                            kT[rows, j, :, :].rearrange("p h k -> p (h k)"),
                                            start=True, stop=True)
                last.then_inc(scores_ready, 1)

            def turn_powers(n, j, g):
                m = PARTS * n + QUARTERS * j + g
                if g == 0:
                    pe.wait_ge(powers_ready, GROUP * n + j + 1)
                if j == 0 and g < 2:
                    pe.wait_ge(powersT_ready, PARTS * n)
                else:
                    pe.wait_ge(powersT_ready, m - 1)
                for i in range(QUAD):
                    last = nc.tensor.transpose(
                        bank[0:KEYS, TURNED + g % 2, i * TOK:(i + 1) * TOK],
                        powers[:, QUAD * g + i, :], chip.ident[:, :])
                last.then_inc(powers_turned, 1)

            def sum_values(n, j, g):
                if g == 0:
                    pe.wait_ge(heads_out_ready, GROUP * n + j)
                    if j == 0:
                        pe.wait_ge(v_ready, n + 1)
                        pe.wait_ge(heads_outT_ready, n)
                pe.wait_ge(powersT_ready, PARTS * n + QUARTERS * j + g + 1)
                for i in range(QUAD):
                    h = QUAD * g + i
                    last = nc.tensor.matmul(sums[:, h, :], powersT[:, g, i * TOK:(i + 1) * TOK],
                                            v[:, j, h, :], start=True, stop=True)
                last.then_inc(heads_summed, 1)

            def project_out(n, more):
                pe.wait_ge(heads_out_ready, GROUP * (n + 1))
                for j in range(GROUP):
                    last = nc.tensor.transpose(bank[:, SUMS, j * TOK:(j + 1) * TOK],
                                               heads_out[:, j, :], chip.ident[:, :])
                last.then_inc(heads_turned, 1)
                pe.wait_ge(v_ready, n + 2 if more else n + 1)
                pe.wait_ge(heads_outT_ready, n + 1)
                for j in range(GROUP):
                    nc.tensor.matmul(bank[:, MISC, j * DIM:(j + 1) * DIM],
                                     heads_outT[:, j * TOK:(j + 1) * TOK], w_o[:, :],
                                     start=True, stop=False)
                    last = nc.tensor.matmul(bank[:, MISC, j * DIM:(j + 1) * DIM], ones[:, :],
                                            b_o[:, :], start=False, stop=True)
                last.then_inc(projected, 1)

            def body(n, more):
                for j in range(GROUP):
                    if j < GROUP - 1:
                        scores(n, j + 1)
                    elif more:
                        pe.wait_ge(powersT_ready, PARTS * (n + 1) - QUARTERS)
                        project_in(n + 1)
                        scores(n + 1, 0)
                    turn_powers(n, j, 0)
                    for g in range(QUARTERS):
                        if g < QUARTERS - 1:
                            turn_powers(n, j, g + 1)
                        sum_values(n, j, g)
                    if j == 1 and more:
                        pe.wait_ge(ln.updated, n)
                        turn(n + 1)
                project_out(n, more)

            pe.wait_ge(weights_in, 16 * len(LOADS))
            pe.wait_ge(consts, 2)
            turn(0)
            project_in(0)
            scores(0, 0)
            engine_loop(pe, body)

        @block.scalar
        def _(act):
            def take_turned(n):
                act.wait_ge(turned, n + 1)
                nc.scalar.copy(xnT[:, :], bank[:, MISC, :]).then_inc(xnT_ready, 1)

            def take_q(n):
                act.wait_ge(q_made, n + 1)
                act.wait_ge(scores_ready, GROUP * n)
                nc.scalar.activation(qT[:, :], bank[:, TURNED, :], ACT.Identity,
                                     bias=b_q[:, 0:1]).then_inc(q_ready, 1)

            def exps(n, j):
                m = GROUP * n + j
                act.wait_ge(below_ready, m + 1)
                act.wait_ge(powers_turned, QUARTERS * m)
                nc.scalar.activation(powers[:, :, :].rearrange("p h k -> p (h k)"),
                                     below[:, :, :].rearrange("p h k -> p (h k)"),
                                     ACT.Exp, scale=scale).then_inc(powers_ready, 1)

            def take_powers(n, j, g):
                m = PARTS * n + QUARTERS * j + g
                act.wait_ge(powers_turned, m + 1)
                if j:
                    act.wait_ge(heads_summed, m - QUARTERS + 1)
                nc.scalar.copy(powersT[:, g, :], bank[0:KEYS, TURNED + g % 2, :])\
                    .then_inc(powersT_ready, 1)

            def body(n, more):
                for j in range(GROUP):
                    if j < GROUP - 1:
                        exps_next = (n, j + 1)
                    elif more:
                        take_q(n + 1)
                        exps_next = (n + 1, 0)
                    else:
                        exps_next = None
                    for g in range(QUARTERS):
                        take_powers(n, j, g)
                    if j == 1 and more:
                        take_turned(n + 1)
                    if exps_next:
                        exps(*exps_next)
                act.wait_ge(heads_turned, n + 1)
                nc.scalar.copy(heads_outT[:, :], bank[:, SUMS, :]).then_inc(heads_outT_ready, 1)

            act.wait_ge(weights_in, 16 * len(LOADS))
            take_turned(0)
            take_q(0)
            exps(0, 0)
            engine_loop(act, body)

        @block.vector
        def _(dve):
            def take_k(n):
                dve.wait_ge(k_made, n + 1)
                dve.wait_ge(scores_ready, GROUP * n)
                keys = bank[:, TURNED + 1, 0:KCOLS].rearrange("p (b k) -> p b k", b=GROUP)
                for j in range(GROUP):
                    last = nc.vector.scalar_tensor_tensor(
                        out=kT[:, j, :, :], in0=bc(keys[:, j, :], 1, QUAD), scalar=b_k[:, 0:1],
                        in1=bc(own_head[:, :], 2, KEYS), op0=ALU.add, op1=ALU.mult)
                last.then_inc(k_ready, 1)

            def take_v(n):
                dve.wait_ge(v_made, n + 1)
                nc.vector.tensor_tensor(
                    out=v[:, :, :, 0:HEAD_DIM],
                    in0=bank[0:KEYS, MISC, :].rearrange("p (b h c) -> p b h c", b=GROUP, h=HEADS),
                    in1=bc(b_v[:, :].rearrange("p (h c) -> p h c", h=HEADS), 1, GROUP),
                    op=ALU.add).then_inc(v_ready, 1)

            def limits(n):
                dve.wait_ge(mask_in, 16 * (n + 1))
                nc.vector.tensor_scalar(limit[:, :, :], mask[:, :, :], 0.0, -1e30, ALU.is_equal,
                                        ALU.mult).then_inc(forbidden, 1)
                dve.wait_ge(forbidden, n + 1)
                nc.vector.tensor_scalar(limit[:, :, :], limit[:, :, :], CLIP / scale, None,
                                        ALU.add).then_inc(limit_ready, 1)
                dve.wait_ge(limit_ready, n + 1)

            def softmax(n, j):
                m = GROUP * n + j
                scores = bank[:, SCORES:SCORES + QUARTERS, 0:QUAD * KEYS].rearrange(
                    "p g (h k) -> p g h k", k=KEYS)
                quarters = below[:, :, :].rearrange("p (g h) k -> p g h k", g=QUARTERS)
                dve.wait_ge(scores_ready, m + 1)
                if clipped:
                    dve.wait_ge(powers_ready, m)
                    for g in range(QUARTERS):
                        last = nc.vector.scalar_tensor_tensor(
                            out=quarters[:, g], in0=scores[:, g], scalar=-CLIP / scale,
                            in1=bc(limit[:, j, :], 1, QUAD), op0=ALU.max, op1=ALU.min)
                    last.then_inc(scores_taken, 1)
                    dve.wait_ge(scores_taken, m + 1)
                    scores = quarters
                nc.vector.tensor_reduce(largest[:, :].rearrange("p (g h) -> p g h", g=QUARTERS),
                                        scores, AX.X, ALU.max).then_inc(largest_ready, 1)
                if not clipped:
                    dve.wait_ge(powers_ready, m)
                dve.wait_ge(largest_ready, m + 1)
                off = nc.vector.tensor_tensor(
                    out=quarters, in0=scores,
                    in1=bc(largest[:, :].rearrange("p (g h) -> p g h", g=QUARTERS), 3, KEYS),
                    op=ALU.subtract)
                off.then_inc(below_ready, 1)
                if not clipped:
                    nc.vector.memset(chip.carrier[:, :], 0.0).then_inc(scores_taken, 1)

            def divide(n, j):
                m = GROUP * n + j
                dve.wait_ge(heads_summed, QUARTERS * (m + 1))
                nc.vector.reciprocal(inverse[:, :], sums[:, :, HEAD_DIM]).then_inc(inverse_ready, 1)
                dve.wait_ge(inverse_ready, m + 1)
                nc.vector.tensor_tensor(
                    out=heads_out[:, j, :].rearrange("p (h c) -> p h c", h=HEADS),
                    in0=sums[:, :, 0:HEAD_DIM], in1=bc(inverse[:, :], 2, HEAD_DIM),
                    op=ALU.mult).then_inc(heads_out_ready, 1)

            def body(n, more):
                if more:
                    chip.normalise(n + 1, xn).then_inc(xn_ready, 1)
                for j in range(GROUP):
                    if j < GROUP - 1:
                        softmax(n, j + 1)
                    elif more:
                        if clipped:
                            limits(n + 1)
                        take_k(n + 1)
                        softmax(n + 1, 0)
                    divide(n, j)
                if more:
                    take_v(n + 1)
                dve.wait_ge(projected, n + 1)
                chip.add_to_x(dve, n, bank[:, MISC, :].rearrange("p (b d) -> p b d", b=GROUP), ln)

            dve.wait_ge(weights_in, 16 * len(LOADS))
            chip.normalise(0, xn).then_inc(xn_ready, 1)
            if clipped:
                limits(0)
            take_k(0)
            dve.wait_ge(consts, 2)
            take_v(0)
            softmax(0, 0)
            engine_loop(dve, body)

        @block.gpsimd
        def _(pool):
            chip.clear_last()
            nc.gpsimd.memset(ones[:, :], 1.0).then_inc(consts, 1)
            nc.gpsimd.memset(v[:, :, :, HEAD_DIM], 1.0).then_inc(consts, 1)

            def body(n, more):
                chip.rstd_of(pool, n, ln)
            engine_loop(pool, body)


def slot_attention(chip):
    nc, d, bank = chip.nc, chip.dram, chip.bank
    ctx, sb, sem = phase(chip, "slots")
    with ctx:
        scale = DIM ** -0.5
        TWO = (0, 1)
        w_q, w_k, w_v = (sb(t, [128, DIM]) for t in ("w_q", "w_k", "w_v"))
        w_ih, w_hh = sb("w_ih", [128, 3, DIM]), sb("w_hh", [128, 3, DIM])
        b_ih, b_hh = sb("b_ih", [128, 3]), sb("b_hh", [128, 3])
        half_b = sb("half_b", [128, 3])
        slot_norm, input_norm = sb("slot_norm", [128, 1]), sb("input_norm", [128, 1])
        mean_col = sb("mean_col", [128, 1])
        ones = sb("ones", [KEYS, 1])
        each = lambda t, shape: [sb(f"{t}{u}", shape) for u in TWO]
        context = each("context", [KEYS, GROUP, DIM])
        square = each("square", [128, COLS])
        energy = each("energy", [128, GROUP])
        rms = each("rms", [128, GROUP])
        unit = each("unit", [KEYS, GROUP, DIM])
        unitT = each("unitT", [128, KCOLS])
        kT = each("kT", [128, KCOLS])
        v = each("v", [KEYS, GROUP, DIM])
        xn = each("xn", [128, GROUP, DIM])
        h = each("h", [128, COLS])
        spread = each("spread", [128, COLS])
        qT = each("qT", [128, COLS])
        offset = each("offset", [KEYS, GROUP])
        powers = each("powers", [KEYS, COLS])
        total = each("total", [KEYS, GROUP])
        update = each("update", [128, COLS])
        half_hidden = each("half_hidden", [128, COLS])
        tanh_r, tanh_z = each("tanh_r", [128, COLS]), each("tanh_z", [128, COLS])
        new = each("new", [128, COLS])
        weights_in, consts, folded = sem("weights_in"), sem("consts"), sem("folded")
        context_in = [sem("context_in0"), sem("context_in1")]
        context_squared, context_rms, unit_ready, unit_turned, unitT_ready, k_made, v_made, \
            k_ready, v_ready, xn_ready, turned, out_turned = (sem(t) for t in (
                "context_squared", "context_rms", "unit_ready", "unit_turned", "unitT_ready",
                "k_made", "v_made", "k_ready", "v_ready", "xn_ready", "turned", "out_turned"))
        h_ready, squared, squares_summed, energy_ready, rms_ready, rms_spread, q_made, \
            hidden_made, rms_taken, q_ready, scores_ready, offset_ready, powers_ready = (
                sem(t) for t in (
                    "h_ready", "squared", "squares_summed", "energy_ready", "rms_ready",
                    "rms_spread", "q_made", "hidden_made", "rms_taken", "q_ready",
                    "scores_ready", "offset_ready", "powers_ready"))
        shares_ready, slots_summed, inverse_ready, inverse_spread, updates_made, hidden_taken, \
            inverse_taken, update_ready, gates_made, gates_ready, drive_ready, new_ready = (
                sem(t) for t in (
                    "shares_ready", "slots_summed", "inverse_ready", "inverse_spread",
                    "updates_made", "hidden_taken", "inverse_taken", "update_ready",
                    "gates_made", "gates_ready", "drive_ready", "new_ready"))
        context_energy, dve_step, ln = sem("context_energy"), sem("dve_step"), NormSignals(sem)
        LOADS = [(w_q, "w_q"), (w_k, "w_k"), (w_v, "w_v"), (w_ih, "w_ih"), (w_hh, "w_hh"),
                 (b_ih, "b_ih"), (b_hh, "b_hh"), (slot_norm, "slot_norm"),
                 (input_norm, "input_norm")]
        seq = lambda j: slice(j * TOK, (j + 1) * TOK)
        count = lambda r, it, u: 2 * SLOT_ITERS * r + 2 * it + u + 1
        HS = 2 * (SLOT_ITERS + 1)
        R, Z, NEW = 0, 1, 2
        block = ctx.enter_context(nc.Block())

        def loop(engine, body):
            with engine.Fori(0, BLOCKS // 2) as r:
                body(r)

        @block.sync
        def _(sp):
            for dst, t in LOADS:
                sp.dma_start(dst[(slice(None),) * len(dst.shape)], d[f"slots_{t}"][
                    (slice(None),) * len(dst.shape)]).then_inc(weights_in, 16)

            def load(n, u):
                sp.dma_start(context[u][:, :, :], d["ctx"][:, chip.rows(n), :])\
                    .then_inc(context_in[u], 16)
            for u in TWO:
                load(u, u)
            with sp.Fori(0, BLOCKS // 2 - 1) as r:
                for u in TWO:
                    sp.wait_ge(unit_ready, 2 * r + u + 1)
                    load(2 * (r + 1) + u, u)

        @block.tensor
        def _(pe):
            def turn(n, u):
                pe.wait_ge(xn_ready, n + 1)
                pe.wait_ge(ln.updated, n - u)
                for j in range(GROUP):
                    last = nc.tensor.transpose(bank[:, 4 * u, seq(j)], xn[u][:, j, :],
                                               chip.ident[:, :])
                last.then_inc(turned, 1)

            def turn_context(n, u):
                pe.wait_ge(unit_ready, n + 1)
                for j in range(GROUP):
                    last = nc.tensor.transpose(bank[:, 4 * u + 1, j * KEYS:(j + 1) * KEYS],
                                               unit[u][:, j, :], chip.ident[0:KEYS, 0:KEYS])
                last.then_inc(unit_turned, 1)

            def keys_and_values(n, u):
                pe.wait_ge(unitT_ready, n + 1)
                nc.tensor.matmul(bank[:, 4 * u + 2, 0:KCOLS], w_k[:, :], unitT[u][:, :],
                                 start=True, stop=True).then_inc(k_made, 1)
                for j in range(GROUP):
                    last = nc.tensor.matmul(bank[0:KEYS, 4 * u + 3, seq(j)],
                                            unitT[u][:, j * KEYS:(j + 1) * KEYS], w_v[:, :],
                                            start=True, stop=True)
                last.then_inc(v_made, 1)

            def sum_squares(r, it, u):
                pe.wait_ge(squared, count(r, it, u))
                for j in range(GROUP):
                    last = nc.tensor.matmul(bank[:, 4 * u, j:j + 1], square[u][:, seq(j)],
                                            mean_col[:, :], start=True, stop=True)
                last.then_inc(squares_summed, 1)

            def from_h(r, it, u):
                nc.tensor.matmul(bank[:, 4 * u + 1, :], w_q[:, :], h[u][:, :],
                                 start=True, stop=True).then_inc(q_made, 1)
                if it == 0:
                    pe.wait_ge(v_ready, 2 * r + u + 1)
                    pe.wait_ge(k_ready, 2 * r + u + 1)
                nc.tensor.matmul(bank[:, 4 * u + 3, :], w_hh[:, NEW, :], h[u][:, :],
                                 start=True, stop=True).then_inc(hidden_made, 1)

            def spread_factor(u, factor, done):
                for j in range(GROUP):
                    last = nc.tensor.matmul(bank[:, 4 * u, seq(j)],
                                            factor[u][:, j:j + 1].broadcast_to([128, 128]),
                                            chip.ident[:, :], start=True, stop=True)
                last.then_inc(done, 1)

            def scores(r, it, u):
                pe.wait_ge(q_ready, count(r, it, u))
                for j in range(GROUP):
                    last = nc.tensor.matmul(bank[0:KEYS, 4 * u + 2, seq(j)],
                                            kT[u][:, j * KEYS:(j + 1) * KEYS],
                                            qT[u][:, seq(j)], start=True, stop=True)
                last.then_inc(scores_ready, 1)

            def from_shares(r, it, u):
                pe.wait_ge(shares_ready, count(r, it, u))
                for j in range(GROUP):
                    last = nc.tensor.matmul(bank[:, 4 * u, j:j + 1], powers[u][:, seq(j)],
                                            ones[:, :], start=True, stop=True)
                last.then_inc(slots_summed, 1)
                for j in range(GROUP):
                    last = nc.tensor.matmul(bank[:, 4 * u + 1, seq(j)], v[u][:, j, :],
                                            powers[u][:, seq(j)], start=True, stop=True)
                last.then_inc(updates_made, 1)
                nc.tensor.matmul(bank[:, 4 * u + 2, :], w_hh[:, R, :], h[u][:, :],
                                 start=True, stop=False)

            def gates(r, it, u):
                pe.wait_ge(update_ready, count(r, it, u))
                nc.tensor.matmul(bank[:, 4 * u + 2, :], w_ih[:, R, :], update[u][:, :],
                                 start=False, stop=True)
                nc.tensor.matmul(bank[:, 4 * u, :], w_hh[:, Z, :], h[u][:, :],
                                 start=True, stop=False)
                nc.tensor.matmul(bank[:, 4 * u, :], w_ih[:, Z, :], update[u][:, :],
                                 start=False, stop=True)
                nc.tensor.matmul(bank[:, 4 * u + 1, :], w_ih[:, NEW, :], update[u][:, :],
                                 start=True, stop=True).then_inc(gates_made, 1)

            def body(r):
                for u in TWO:
                    turn(2 * r + u, u)
                for u in TWO:
                    turn_context(2 * r + u, u)
                for u in TWO:
                    keys_and_values(2 * r + u, u)
                for it in range(SLOT_ITERS):
                    for u in TWO:
                        sum_squares(r, it, u)
                        from_h(r, it, u)
                    for u in TWO:
                        pe.wait_ge(rms_ready, count(r, it, u))
                        spread_factor(u, rms, rms_spread)
                    for u in TWO:
                        scores(r, it, u)
                    for u in TWO:
                        from_shares(r, it, u)
                    for u in TWO:
                        pe.wait_ge(inverse_ready, count(r, it, u))
                        spread_factor(u, rms, inverse_spread)
                    for u in TWO:
                        gates(r, it, u)
                for u in TWO:
                    pe.wait_ge(h_ready, HS * r + 2 * SLOT_ITERS + u + 1)
                    for j in range(GROUP):
                        last = nc.tensor.transpose(bank[:, 4 * u, seq(j)], h[u][:, seq(j)],
                                                   chip.ident[:, :])
                    last.then_inc(out_turned, 1)

            pe.wait_ge(folded, 3)
            pe.wait_ge(consts, 2)
            loop(pe, body)

        @block.scalar
        def _(act):
            def body(r):
                for u in TWO:
                    n = 2 * r + u
                    act.wait_ge(context_in[u], 16 * (r + 1))
                    act.wait_ge(context_rms, 2 * r)
                    for j in range(GROUP):
                        last = nc.scalar.activation(unit[u][:, j, :], context[u][:, j, :],
                                                    ACT.Square, scale=scale,
                                                    accum_out=energy[u][0:KEYS, j:j + 1])
                    last.then_inc(context_squared, 1)
                for u in TWO:
                    act.wait_ge(turned, 2 * r + u + 1)
                    nc.scalar.copy(h[u][:, :], bank[:, 4 * u, :]).then_inc(h_ready, 1)
                for u in TWO:
                    act.wait_ge(unit_turned, 2 * r + u + 1)
                    nc.scalar.copy(unitT[u][:, :], bank[:, 4 * u + 1, 0:KCOLS])\
                        .then_inc(unitT_ready, 1)
                for u in TWO:
                    act.wait_ge(k_made, 2 * r + u + 1)
                    nc.scalar.copy(kT[u][:, :], bank[:, 4 * u + 2, 0:KCOLS]).then_inc(k_ready, 1)
                for it in range(SLOT_ITERS):
                    for u in TWO:
                        act.wait_ge(h_ready, HS * r + 2 * it + u + 1)
                        nc.scalar.activation(square[u][:, :], h[u][:, :], ACT.Square)\
                            .then_inc(squared, 1)
                    for u in TWO:
                        act.wait_ge(rms_spread, count(r, it, u))
                        nc.scalar.copy(spread[u][:, :], bank[:, 4 * u, :]).then_inc(rms_taken, 1)
                    for u in TWO:
                        act.wait_ge(hidden_made, count(r, it, u))
                        nc.scalar.activation(half_hidden[u][:, :], bank[:, 4 * u + 3, :],
                                             ACT.Identity, bias=half_b[:, NEW:NEW + 1],
                                             scale=0.5).then_inc(hidden_taken, 1)
                    for u in TWO:
                        act.wait_ge(offset_ready, count(r, it, u))
                        for j in range(GROUP):
                            last = nc.scalar.activation(
                                powers[u][:, seq(j)], bank[0:KEYS, 4 * u + 2, seq(j)], ACT.Exp,
                                bias=offset[u][:, j:j + 1], scale=scale,
                                accum_out=total[u][:, j:j + 1])
                        last.then_inc(powers_ready, 1)
                    for u in TWO:
                        act.wait_ge(inverse_spread, count(r, it, u))
                        nc.scalar.copy(spread[u][:, :], bank[:, 4 * u, :])\
                            .then_inc(inverse_taken, 1)
                    for u in TWO:
                        act.wait_ge(gates_made, count(r, it, u))
                        nc.scalar.activation(tanh_r[u][:, :], bank[:, 4 * u + 2, :], ACT.Tanh,
                                             bias=half_b[:, R:R + 1], scale=0.5)
                        nc.scalar.activation(tanh_z[u][:, :], bank[:, 4 * u, :], ACT.Tanh,
                                             bias=half_b[:, Z:Z + 1], scale=0.5)\
                            .then_inc(gates_ready, 1)
                    for u in TWO:
                        act.wait_ge(drive_ready, count(r, it, u))
                        nc.scalar.activation(new[u][:, :], new[u][:, :], ACT.Tanh,
                                             bias=b_ih[:, NEW:NEW + 1]).then_inc(new_ready, 1)

            act.wait_ge(folded, 3)
            loop(act, body)

        @block.vector
        def _(dve):
            OWN = 2 * SLOT_ITERS * 6

            def body(r):
                done = [0]

                def step(instruction):
                    instruction.then_inc(dve_step, 1)
                    done[0] += 1
                    dve.wait_ge(dve_step, OWN * r + done[0])
                for u in TWO:
                    n = 2 * r + u
                    dve.wait_ge(turned, 2 * r)
                    chip.normalise(n, xn[u]).then_inc(xn_ready, 1)
                for u in TWO:
                    dve.wait_ge(context_rms, 2 * r + u + 1)
                    nc.vector.tensor_tensor(out=unit[u][:, :, :], in0=context[u][:, :, :],
                                            in1=bc(rms[u][0:KEYS, :], 2, DIM),
                                            op=ALU.mult).then_inc(unit_ready, 1)
                for u in TWO:
                    dve.wait_ge(v_made, 2 * r + u + 1)
                    nc.vector.tensor_copy(v[u][:, :, :].rearrange("p b d -> p (b d)"),
                                          bank[0:KEYS, 4 * u + 3, :]).then_inc(v_ready, 1)
                for it in range(SLOT_ITERS):
                    for u in TWO:
                        dve.wait_ge(squares_summed, count(r, it, u))
                        nc.vector.tensor_tensor(out=energy[u][:, :], in0=bank[:, 4 * u, 0:GROUP],
                                                in1=chip.rms_eps[:, :],
                                                op=ALU.add).then_inc(energy_ready, 1)
                    for u in TWO:
                        dve.wait_ge(rms_taken, count(r, it, u))
                        dve.wait_ge(q_made, count(r, it, u))
                        nc.vector.tensor_tensor(out=qT[u][:, :], in0=bank[:, 4 * u + 1, :],
                                                in1=spread[u][:, :],
                                                op=ALU.mult).then_inc(q_ready, 1)
                    for u in TWO:
                        dve.wait_ge(scores_ready, count(r, it, u))
                        step(nc.vector.tensor_reduce(
                            offset[u][:, :], bank[0:KEYS, 4 * u + 2, :].rearrange(
                                "p (b s) -> p b s", b=GROUP), AX.X, ALU.max))
                        nc.vector.tensor_scalar(offset[u][:, :], offset[u][:, :], -scale, None,
                                                ALU.mult).then_inc(offset_ready, 1)
                    for u in TWO:
                        dve.wait_ge(powers_ready, count(r, it, u))
                        step(nc.vector.reciprocal(total[u][:, :], total[u][:, :]))
                        by_seq = powers[u][:, :].rearrange("p (b s) -> p b s", b=GROUP)
                        nc.vector.tensor_tensor(out=by_seq, in0=by_seq,
                                                in1=bc(total[u][:, :], 2, TOK),
                                                op=ALU.mult).then_inc(shares_ready, 1)
                    for u in TWO:
                        dve.wait_ge(slots_summed, count(r, it, u))
                        step(nc.vector.tensor_tensor(out=rms[u][:, :],
                                                     in0=bank[:, 4 * u, 0:GROUP],
                                                     in1=chip.rms_eps[:, :], op=ALU.add))
                        nc.vector.reciprocal(rms[u][:, :], rms[u][:, :])\
                            .then_inc(inverse_ready, 1)
                    for u in TWO:
                        dve.wait_ge(inverse_taken, count(r, it, u))
                        dve.wait_ge(updates_made, count(r, it, u))
                        nc.vector.tensor_tensor(out=update[u][:, :], in0=bank[:, 4 * u + 1, :],
                                                in1=spread[u][:, :],
                                                op=ALU.mult).then_inc(update_ready, 1)
                    for u in TWO:
                        dve.wait_ge(gates_ready, count(r, it, u))
                        dve.wait_ge(hidden_taken, count(r, it, u))
                        step(nc.vector.scalar_tensor_tensor(
                            out=new[u][:, :], in0=tanh_r[u][:, :], scalar=1.0,
                            in1=half_hidden[u][:, :], op0=ALU.add, op1=ALU.mult))
                        nc.vector.tensor_tensor(out=new[u][:, :], in0=new[u][:, :],
                                                in1=bank[:, 4 * u + 1, :],
                                                op=ALU.add).then_inc(drive_ready, 1)
                    for u in TWO:
                        dve.wait_ge(new_ready, count(r, it, u))
                        step(nc.vector.tensor_tensor(out=h[u][:, :], in0=h[u][:, :],
                                                     in1=new[u][:, :], op=ALU.subtract))
                        step(nc.vector.scalar_tensor_tensor(
                            out=h[u][:, :], in0=tanh_z[u][:, :], scalar=1.0, in1=h[u][:, :],
                            op0=ALU.add, op1=ALU.mult))
                        nc.vector.scalar_tensor_tensor(
                            out=h[u][:, :], in0=h[u][:, :], scalar=0.5, in1=new[u][:, :],
                            op0=ALU.mult, op1=ALU.add).then_inc(h_ready, 1)
                assert done[0] == OWN
                for u in TWO:
                    n = 2 * r + u
                    dve.wait_ge(out_turned, n + 1)
                    chip.add_to_x(dve, n, bank[:, 4 * u, :].rearrange(
                        "p (b d) -> p b d", b=GROUP), ln)

            dve.wait_ge(weights_in, 16 * len(LOADS))
            nc.vector.tensor_scalar(w_q[:, :], w_q[:, :], slot_norm[:, 0:1], None, ALU.mult)
            nc.vector.tensor_scalar(w_k[:, :], w_k[:, :], input_norm[:, 0:1], None, ALU.mult)
            nc.vector.tensor_scalar(w_v[:, :], w_v[:, :], input_norm[:, 0:1], None, ALU.mult)\
                .then_inc(folded, 1)
            nc.vector.tensor_tensor(out=half_b[:, 0:2], in0=b_ih[:, 0:2], in1=b_hh[:, 0:2],
                                    op=ALU.add)
            nc.vector.tensor_scalar(half_b[:, 2:3], b_hh[:, 2:3], 0.5, None, ALU.mult)\
                .then_inc(folded, 1)
            dve.wait_ge(folded, 2)
            nc.vector.tensor_scalar(half_b[:, 0:2], half_b[:, 0:2], 0.5, None, ALU.mult)\
                .then_inc(folded, 1)
            loop(dve, body)

        @block.gpsimd
        def _(pool):
            chip.clear_last()
            def body(r):
                for u in TWO:
                    n = 2 * r + u
                    pool.wait_ge(context_squared, n + 1)
                    nc.gpsimd.tensor_tensor(out=energy[u][0:KEYS, :], in0=energy[u][0:KEYS, :],
                                            in1=chip.rms_eps[0:KEYS, :],
                                            op=ALU.add).then_inc(context_energy, 1)
                    pool.wait_ge(context_energy, n + 1)
                    nc.gpsimd.tensor_tensor(out=rms[u][0:KEYS, :], in0=energy[u][0:KEYS, :],
                                            in1=chip.minus_half[0:KEYS, :],
                                            op=ALU.pow).then_inc(context_rms, 1)
                for it in range(SLOT_ITERS):
                    for u in TWO:
                        pool.wait_ge(energy_ready, count(r, it, u))
                        nc.gpsimd.tensor_tensor(out=rms[u][:, :], in0=energy[u][:, :],
                                                in1=chip.minus_half[:, :],
                                                op=ALU.pow).then_inc(rms_ready, 1)
                for u in TWO:
                    chip.rstd_of(pool, 2 * r + u, ln)
            nc.gpsimd.memset(mean_col[:, :], 1.0 / DIM).then_inc(consts, 1)
            nc.gpsimd.memset(ones[:, :], 1.0).then_inc(consts, 1)
            loop(pool, body)


def context_attention(chip):
    nc, d, bank = chip.nc, chip.dram, chip.bank
    ctx, sb, sem = phase(chip, "x3")
    with ctx:
        scale = DIM ** -0.5
        ctxT = sb("ctxT", [128, 2, GROUP, KEYS])
        values = sb("values", [KEYS, 2, GROUP, DIM])
        mask = sb("mask", [128, 2, GROUP, KEYS])
        xn = sb("xn", [128, GROUP, DIM])
        xnT = sb("xnT", [128, 2, COLS])
        scaled = sb("scaled", [128, GROUP, KEYS])
        masks = sb("masks", [128, GROUP, KEYS], U32)
        largest = sb("largest", [128, GROUP])
        below = sb("below", [128, GROUP, KEYS])
        powers = sb("powers", [128, GROUP, KEYS])
        total = sb("total", [128, GROUP])
        share = sb("share", [128, GROUP, KEYS])
        number = sb("number", [128, GROUP, KEYS], U32)
        weight = sb("weight", [128, GROUP, KEYS])
        weightT = sb("weightT", [KEYS, COLS])
        loaded, xn_ready, turned, xnT_ready = (
            [sem("loaded0"), sem("loaded1")], sem("xn_ready"), sem("turned"), sem("xnT_ready"))
        scores_ready, step_done, below_ready, powers_ready = (
            sem("scores_ready"), sem("step_done"), sem("below_ready"), sem("powers_ready"))
        weight_turned, weightT_ready, summed, ln = (
            sem("weight_turned"), sem("weightT_ready"), sem("summed"), NormSignals(sem))
        TURN, SCORES, WEIGHTS, OUT = 0, 1, 3, 4
        STEPS = 11
        block = ctx.enter_context(nc.Block())

        @block.sync
        def _(sp):
            def load(n, u, r=None):
                rows = chip.rows(n)
                sp.dma_start(ctxT[:, u, :, :], d["ctxT"][:, rows, :]).then_inc(loaded[u], 16)
                sp.dma_start(values[:, u, :, :], d["ctx"][:, rows, :]).then_inc(loaded[u], 16)
                sp.dma_start(mask[:, u, :, :], d["x3_mask"][:, rows, :]).then_inc(loaded[u], 16)

            def body(n, u, more):
                if more:
                    sp.wait_ge(summed, n)
                    load(n + 1, 1 - u)
            load(0, 0)
            engine_loop_pairs(sp, body)

        def landed(engine, n, u):
            engine.wait_ge(loaded[u], 24 * (n - u) + 48)

        @block.tensor
        def _(pe):
            def turn(n):
                pe.wait_ge(xn_ready, n + 1)
                for j in range(GROUP):
                    last = nc.tensor.transpose(bank[:, TURN, j * TOK:(j + 1) * TOK], xn[:, j, :],
                                               chip.ident[:, :])
                last.then_inc(turned, 1)

            def scores(n, u):
                landed(pe, n, u)
                pe.wait_ge(xnT_ready, n + 1)
                for j in range(GROUP):
                    last = nc.tensor.matmul(bank[:, SCORES + u, j * KEYS:(j + 1) * KEYS],
                                            xnT[:, u, j * TOK:(j + 1) * TOK], ctxT[:, u, j, :],
                                            start=True, stop=True)
                last.then_inc(scores_ready, 1)

            def body(n, u, more):
                if more:
                    turn(n + 1)
                    scores(n + 1, 1 - u)
                pe.wait_ge(step_done, STEPS * (n + 1))
                for j in range(GROUP):
                    last = nc.tensor.transpose(bank[0:KEYS, WEIGHTS, j * TOK:(j + 1) * TOK],
                                               weight[:, j, :], chip.ident[:, :])
                last.then_inc(weight_turned, 1)
                pe.wait_ge(ln.updated, n)
                pe.wait_ge(weightT_ready, n + 1)
                for j in range(GROUP):
                    last = nc.tensor.matmul(bank[:, OUT, j * DIM:(j + 1) * DIM],
                                            weightT[:, j * TOK:(j + 1) * TOK], values[:, u, j, :],
                                            start=True, stop=True)
                last.then_inc(summed, 1)

            turn(0)
            scores(0, 0)
            engine_loop_pairs(pe, body)

        @block.scalar
        def _(act):
            def take_turned(n, u):
                act.wait_ge(turned, n + 1)
                nc.scalar.copy(xnT[:, u, :], bank[:, TURN, :]).then_inc(xnT_ready, 1)

            def body(n, u, more):
                if more:
                    take_turned(n + 1, 1 - u)
                act.wait_ge(below_ready, n + 1)
                nc.scalar.activation(powers[:, :, :].rearrange("p b k -> p (b k)"),
                                     below[:, :, :].rearrange("p b k -> p (b k)"), ACT.Exp)\
                    .then_inc(powers_ready, 1)
                act.wait_ge(weight_turned, n + 1)
                nc.scalar.copy(weightT[:, :], bank[0:KEYS, WEIGHTS, :]).then_inc(weightT_ready, 1)

            take_turned(0, 0)
            engine_loop_pairs(act, body)

        @block.vector
        def _(dve):
            def body(n, u, more):
                done = [0]

                def step(instruction):
                    instruction.then_inc(step_done, 1)
                    done[0] += 1
                    dve.wait_ge(step_done, STEPS * n + done[0])
                if more:
                    dve.wait_ge(turned, n + 1)
                    chip.normalise(n + 1, xn).then_inc(xn_ready, 1)
                landed(dve, n, u)
                dve.wait_ge(scores_ready, n + 1)
                step(nc.vector.tensor_scalar(
                    scaled[:, :, :], bank[:, SCORES + u, 0:KCOLS].rearrange(
                        "p (b k) -> p b k", b=GROUP), scale, None, ALU.mult))
                step(nc.vector.tensor_scalar(masks[:, :, :], mask[:, u, :, :], -1.0, None,
                                             ALU.is_lt))
                chip.settle()
                step(nc.vector.copy_predicated(scaled[:, :, :], masks[:, :, :], mask[:, u, :, :]))
                step(nc.vector.tensor_reduce(largest[:, :], scaled[:, :, :], AX.X, ALU.max))
                step(nc.vector.tensor_tensor(out=below[:, :, :], in0=scaled[:, :, :],
                                             in1=bc(largest[:, :], 2, KEYS), op=ALU.subtract))
                nc.vector.memset(weight[:, :, :], 0.0).then_inc(below_ready, 1)
                dve.wait_ge(powers_ready, n + 1)
                step(nc.vector.tensor_reduce(total[:, :], powers[:, :, :], AX.X, ALU.add))
                step(nc.vector.reciprocal(total[:, :], total[:, :]))
                step(nc.vector.tensor_tensor(out=share[:, :, :], in0=powers[:, :, :],
                                             in1=bc(total[:, :], 2, KEYS), op=ALU.mult))
                step(nc.vector.tensor_tensor(out=number[:, :, :], in0=share[:, :, :],
                                             in1=share[:, :, :], op=ALU.is_equal))
                dve.wait_ge(below_ready, n + 1)
                chip.settle()
                step(nc.vector.copy_predicated(weight[:, :, :], number[:, :, :], share[:, :, :]))
                step(nc.vector.memset(chip.carrier[:, :], 0.0))
                dve.wait_ge(summed, n + 1)
                chip.add_to_x(dve, n, bank[:, OUT, :].rearrange("p (b d) -> p b d", b=GROUP), ln)

            chip.normalise(0, xn).then_inc(xn_ready, 1)
            engine_loop_pairs(dve, body)

        @block.gpsimd
        def _(pool):
            chip.clear_last()
            def body(n, u, more):
                chip.rstd_of(pool, n, ln)
            engine_loop_pairs(pool, body)


def mix_ffn(chip):
    nc, d, bank = chip.nc, chip.dram, chip.bank
    ctx, sb, sem = phase(chip, "mix")
    with ctx:
        w_r, w_k, w_v = (sb(t, [128, DIM]) for t in ("w_r", "w_k", "w_v"))
        mu = sb("mu", [128, 2])
        one_less_mu = sb("one_less_mu", [128, 2])
        xn = sb("xn", [128, GROUP, DIM])
        padded = sb("padded", [128, 2, GROUP, TOK + 1])
        scaled = sb("scaled", [128, 2, GROUP, TOK])
        mixed = sb("mixed", [128, 2, GROUP, TOK])
        gate = sb("gate", [128, COLS])
        relu = sb("relu", [128, COLS])
        square = sb("square", [128, COLS])
        outT = sb("outT", [128, COLS])
        weights_in, xn_ready, turned, padded_ready = (
            sem("weights_in"), sem("xn_ready"), sem("turned"), sem("padded_ready"))
        mu_ready, cleared, scaled_ready, mixed_ready = (
            sem("mu_ready"), sem("cleared"), sem("scaled_ready"), sem("mixed_ready"))
        pre_ready, gate_ready, relu_ready, square_ready, value_ready, outT_ready, out_turned, updated = (
            sem("pre_ready"), sem("gate_ready"), sem("relu_ready"), sem("square_ready"),
            sem("value_ready"), sem("outT_ready"), sem("out_turned"), sem("updated"))
        stored = sem("stored")
        TURN, R, K, V, BACK = 0, 1, 2, 3, 4
        block = ctx.enter_context(nc.Block())

        @block.sync
        def _(sp):
            for dst, name in ((w_r, "mix_w_r"), (w_k, "mix_w_k"), (w_v, "mix_w_v"), (mu, "mix_mu")):
                sp.dma_start(dst[:, :], d[name][:, :]).then_inc(weights_in, 16)

            def body(n, u, more):
                sp.wait_ge(updated, n + 1)
                r = chip.rows(n)
                sp.dma_start(d["out"][r, :, :].rearrange("b t d -> t b d"), chip.x[:, r, :])\
                    .then_inc(stored, 16)
            engine_loop_pairs(sp, body)
            sp.wait_ge(stored, 16 * BLOCKS)

        @block.tensor
        def _(pe):
            def turn(n):
                pe.wait_ge(xn_ready, n + 1)
                for j in range(GROUP):
                    last = nc.tensor.transpose(bank[:, TURN, j * TOK:(j + 1) * TOK], xn[:, j, :],
                                               chip.ident[:, :])
                last.then_inc(turned, 1)

            def pre(n):
                for i, (w, at) in enumerate(((w_k, K), (w_r, R))):
                    if i:
                        pe.wait_ge(gate_ready, n)
                    pe.wait_ge(mixed_ready, 2 * n + i + 1)
                    nc.tensor.matmul(bank[:, at, :], w[:, :],
                                     mixed[:, i, :, :].rearrange("p b t -> p (b t)"),
                                     start=True, stop=True).then_inc(pre_ready, 1)

            def body(n, u, more):
                if more:
                    turn(n + 1)
                pe.wait_ge(square_ready, n + 1)
                nc.tensor.matmul(bank[:, V, :], w_v[:, :], square[:, :], start=True, stop=True)\
                    .then_inc(value_ready, 1)
                if more:
                    pre(n + 1)
                pe.wait_ge(outT_ready, n + 1)
                for j in range(GROUP):
                    last = nc.tensor.transpose(bank[:, BACK, j * TOK:(j + 1) * TOK],
                                               outT[:, j * TOK:(j + 1) * TOK], chip.ident[:, :])
                last.then_inc(out_turned, 1)

            pe.wait_ge(weights_in, 64)
            turn(0)
            pre(0)
            engine_loop_pairs(pe, body)

        @block.scalar
        def _(act):
            def take_turned(n, u):
                act.wait_ge(turned, n + 1)
                nc.scalar.copy(padded[:, u, :, 1:], bank[:, TURN, :].rearrange(
                    "p (b t) -> p b t", b=GROUP)).then_inc(padded_ready, 1)

            def body(n, u, more):
                if more:
                    take_turned(n + 1, 1 - u)
                act.wait_ge(pre_ready, 2 * n + 1)
                nc.scalar.activation(relu[:, :], bank[:, K, :], ACT.Relu).then_inc(relu_ready, 1)
                act.wait_ge(pre_ready, 2 * n + 2)
                act.wait_ge(outT_ready, n)
                nc.scalar.activation(gate[:, :], bank[:, R, :], ACT.Sigmoid).then_inc(gate_ready, 1)

            act.wait_ge(cleared, 1)
            take_turned(0, 0)
            engine_loop_pairs(act, body)

        @block.vector
        def _(dve):
            def mix(n, u):
                dve.wait_ge(padded_ready, n + 1)
                for i in range(2):
                    at = 1 - i
                    nc.vector.tensor_scalar(scaled[:, i, :, :], padded[:, u, :, 1:],
                                            mu[:, at:at + 1], None, ALU.mult)\
                        .then_inc(scaled_ready, 1)
                for i in range(2):
                    at = 1 - i
                    dve.wait_ge(scaled_ready, 2 * n + i + 1)
                    nc.vector.scalar_tensor_tensor(
                        out=mixed[:, i, :, :], in0=padded[:, u, :, 0:TOK],
                        scalar=one_less_mu[:, at:at + 1], in1=scaled[:, i, :, :],
                        op0=ALU.mult, op1=ALU.add).then_inc(mixed_ready, 1)

            def body(n, u, more):
                if more:
                    dve.wait_ge(pre_ready, 2 * n + 2)
                    mix(n + 1, 1 - u)
                dve.wait_ge(gate_ready, n + 1)
                dve.wait_ge(value_ready, n + 1)
                nc.vector.tensor_tensor(out=outT[:, :], in0=gate[:, :], in1=bank[:, V, :],
                                        op=ALU.mult).then_inc(outT_ready, 1)
                dve.wait_ge(out_turned, n + 1)
                r = chip.rows(n)
                nc.vector.tensor_tensor(out=chip.x[:, r, :], in1=chip.x[:, r, :],
                                        in0=bank[:, BACK, :].rearrange("p (b d) -> p b d", b=GROUP),
                                        op=ALU.add).then_inc(updated, 1)

            dve.wait_ge(weights_in, 64)
            nc.vector.tensor_scalar(one_less_mu[:, :], mu[:, :], -1.0, 1.0, ALU.mult, ALU.add)\
                .then_inc(mu_ready, 1)
            chip.normalise(0, xn).then_inc(xn_ready, 1)
            dve.wait_ge(mu_ready, 1)
            mix(0, 0)

            def whole(n, u, more):
                if more:
                    dve.wait_ge(turned, n + 1)
                    chip.normalise(n + 1, xn).then_inc(xn_ready, 1)
                body(n, u, more)
            engine_loop_pairs(dve, whole)

        @block.gpsimd
        def _(pool):
            chip.clear_last()
            nc.gpsimd.memset(padded[:, :, :, 0], 0.0).then_inc(cleared, 1)

            def body(n, u, more):
                pool.wait_ge(relu_ready, n + 1)
                nc.gpsimd.tensor_tensor(out=square[:, :], in0=relu[:, :], in1=relu[:, :],
                                        op=ALU.mult).then_inc(square_ready, 1)
            engine_loop_pairs(pool, body)


def store_stream(chip):
    nc, d = chip.nc, chip.dram
    ctx, sb, sem = phase(chip, "store")
    with ctx:
        stored = sem("stored")
        block = ctx.enter_context(nc.Block())

        @block.sync
        def _(sp):
            sp.dma_start(d["out"].rearrange("b t d -> t b d"), chip.x[:, :, :]).then_inc(stored, 16)
            sp.wait_ge(stored, 16)


PHASES = ["x0", "tree", "x1", "moe", "slots", "gated", "x3", "mix"]


def build(nc, dram):
    with ExitStack() as top:
        chip = Chip(nc, top, dram)
        load_stream(chip)
        fns = {"x0": lambda c: heads_attention(c, "x0", False),
               "x1": lambda c: heads_attention(c, "x1", True), "x3": context_attention, "slots": slot_attention,
               "tree": tree_ffn, "moe": moe_ffn, "gated": gated_ffn, "mix": mix_ffn}
        for p in PHASES:
            fns[p](chip)
        if PHASES[-1] != "mix":
            store_stream(chip)


def ancestor_matrix():
    a = np.zeros((128, NODES), np.float32)
    rights = np.zeros(NODES, np.float32)
    for node in range(1, NODES):
        m = node
        while m:
            up = (m - 1) // 2
            right = m == 2 * up + 2
            a[up, node] = 1.0 if right else -1.0
            rights[node] += right
            m = up
    return a, rights


def layouts(inputs):
    g = {k: np.ascontiguousarray(v) for k, v in inputs.items()}
    t = lambda name: np.ascontiguousarray(g[name].T)
    rows = lambda a: np.ascontiguousarray(np.broadcast_to(a, (128,) + a.shape))
    bf16 = mybir.dt.np(BF16)
    out = {"x": g["x"], "ident": np.eye(128, dtype=np.float32)}

    out["tree_w_in"] = t("L0_ffn_W_in")
    two = np.zeros((TREES, 256) + (DIM,), np.float32)
    two[:, :NODES] = g["L0_ffn_W_out"].T.reshape(TREES, NODES, DIM)
    out["tree_w_out"] = np.ascontiguousarray(two.reshape(TREES, 2, 128, DIM).transpose(2, 0, 1, 3))
    b = np.zeros((TREES, 256), np.float32)
    b[:, :NODES] = g["L0_ffn_b_in"].reshape(TREES, NODES)
    out["tree_b_in"] = np.ascontiguousarray(b.reshape(TREES, 2, 128).transpose(2, 0, 1))
    a, rights = ancestor_matrix()
    out["tree_ancestors"] = a.astype(bf16)
    r = np.zeros(256, np.float32)
    r[:NODES] = rights
    out["tree_target"] = np.ascontiguousarray(r.reshape(2, 128).T)

    for name, at, upper in (("x0", "L0_xattn", True), ("x1", "L1_xattn", False)):
        for p in "qkvo":
            w = f"{at}_W{p}" if upper else f"{at}_w{p}"
            out[f"{name}_w_{p}"] = t(w)
        out[f"{name}_b_q"], out[f"{name}_b_k"] = g[f"{at}_bq"][:, None], g[f"{at}_bk"][:, None]
        out[f"{name}_b_v"] = rows(g[f"{at}_bv"])[:KEYS]
        out[f"{name}_b_o"] = g[f"{at}_bo"][None, :]
    part = np.arange(128)[:, None]
    out["own_head"] = ((part % 32) // HEAD_DIM == np.arange(QUAD)).astype(np.float32)
    out["ctxT"] = np.ascontiguousarray(g["ctx_1024"].transpose(2, 0, 1))
    out["ctx"] = np.ascontiguousarray(g["ctx_1024"].transpose(1, 0, 2))
    out["mask"] = np.ascontiguousarray(g["mask_Bx1xSxS2_ik1"][:, 0].transpose(1, 0, 2))
    out["x3_mask"] = np.ascontiguousarray(g["mask_BxSxS2_fk0"].transpose(1, 0, 2))

    out["moe_w_route"] = t("L1_ffn_Wg")
    out["moe_bias"] = rows(g["L1_ffn_bias_corr"])
    up = g["L1_ffn_W1"].reshape(MOE_CHUNKS, 128, DIM)
    up = np.concatenate([up, g["L1_ffn_Ws1"][None]])
    out["moe_w_up"] = np.ascontiguousarray(up.transpose(2, 0, 1))
    down = g["L1_ffn_W2"].transpose(0, 2, 1).reshape(MOE_CHUNKS, 128, DIM)
    down = np.concatenate([down, g["L1_ffn_Ws2"].T[None]])
    out["moe_w_down"] = np.ascontiguousarray(down.transpose(1, 0, 2))
    e = np.arange(EXPERTS)[:, None]
    owner = (np.arange(MOE_CHUNKS * 128) // EXP_HID)[None, :]
    out["moe_spread"] = np.tile(e == owner, (3, 1)).reshape(3 * EXPERTS, MOE_CHUNKS, 128).astype(bf16)
    for size, dt in ((EXP_GROUPS, np.float32), (GATED, bf16), (EXPERTS, bf16)):
        out[f"earlier{size}"] = rows(np.tril(np.ones((size, size), np.float32), -1).astype(dt))

    for p in "qkv":
        out[f"slots_w_{p}"] = t(f"L2_xattn_W{p}")
    for p in ("ih", "hh"):
        w = g[f"L2_xattn_gru_w{p}"].reshape(3, DIM, DIM)
        out[f"slots_w_{p}"] = np.ascontiguousarray(w.transpose(2, 0, 1))
        out[f"slots_b_{p}"] = np.ascontiguousarray(g[f"L2_xattn_gru_b{p}"].reshape(3, DIM).T)
    out["slots_slot_norm"] = g["L2_xattn_slot_norm_w"][:, None]
    out["slots_input_norm"] = g["L2_xattn_input_norm_w"][:, None]

    out["gated_w_gate"] = t("L2_ffn_gate_w")
    out["gated_b_gate"] = rows(g["L2_ffn_gate_b"])
    out["gated_w"] = np.ascontiguousarray(g["L2_ffn_expert_w"].transpose(1, 0, 2))
    out["gated_b"] = np.tile(g["L2_ffn_expert_b"], (3, 1))
    out["gated_spread"] = np.broadcast_to(np.tile(np.eye(GATED), (3, 1))[:, :, None],
                                          (3 * GATED, GATED, 128)).astype(bf16)

    out["mix_w_r"], out["mix_w_k"], out["mix_w_v"] = t("L3_ffn_W_r"), t("L3_ffn_W_k"), t("L3_ffn_W_v")
    out["mix_mu"] = np.stack([g["L3_ffn_mu_r"], g["L3_ffn_mu_k"]], axis=1)
    return out


def kernel(**inputs):
    import concourse.bacc as bacc
    from concourse.bass_utils import run_bass_kernel_spmd

    arrays = layouts(inputs)
    nc = bacc.Bacc("TRN2", target_bir_lowering=False, num_devices=1)
    dram = {k: nc.dram_tensor(f"in_{k}", v.shape, mybir.dt.from_np(v.dtype), kind="ExternalInput").ap()
            for k, v in arrays.items()}
    dram["out"] = nc.dram_tensor("out", (SEQS, TOK, DIM), F32, kind="ExternalOutput").ap()
    build(nc, dram)
    r = run_bass_kernel_spmd(nc, [{f"in_{k}": v for k, v in arrays.items()}], core_ids=[0])
    return r.results[0]["out"]
```

```python
from contextlib import ExitStack

import numpy as np

import concourse.bass as bass
from concourse import mybir

F32 = mybir.dt.float32
BF16 = mybir.dt.bfloat16
I32 = mybir.dt.int32
U32 = mybir.dt.uint32
ALU = mybir.AluOpType
ACT = mybir.ActivationFunctionType
AX = mybir.AxisListType

SEQS, TOK, DIM, KEYS = 32, 128, 128, 77
GROUP = 4
BLOCKS = SEQS // GROUP
COLS = GROUP * TOK
KCOLS = GROUP * KEYS
LN_EPS = 1e-5
PAIR = 2 * DIM

TREES, DEPTH = 8, 7
NODES = 2 ** (DEPTH + 1) - 1
INNER = 2 ** DEPTH - 1
CHUNK = (128, NODES - 128)

EXPERTS, EXP_HID, EXP_GROUPS, TOP_GROUPS, TOP_EXPERTS, ROUTE_SCALE = 16, 64, 4, 2, 4, 2.5
PER_GROUP = EXPERTS // EXP_GROUPS
MOE_CHUNKS = EXPERTS * EXP_HID // 128
GATED, TOP_GATED = 8, 2

HEADS = 16
HEAD_DIM = DIM // HEADS
QUAD = 4
CLIP = 100.0
SLOT_ITERS, RMS_EPS = 3, 1e-6


def engine_loop(engine, body):
    with engine.Fori(0, BLOCKS - 1) as n:
        body(n, True)
    body(BLOCKS - 1, False)


def bc(ap, at, size):
    a = ap.unsqueeze(at)
    shape = list(a.shape)
    shape[at] = size
    return a.broadcast_to(shape)


class Chip:

    def __init__(self, nc, top, dram):
        self.nc, self.dram = nc, dram
        sb = lambda name, shape, dt=F32: top.enter_context(nc.sbuf_tensor(name, shape, dt))
        self.x = sb("x_res", [128, SEQS, DIM])
        self.mean_var = sb("mean_var", [128, SEQS, 2])
        self.rstd = sb("rstd", [128, SEQS])
        self.stats = sb("stats", [128, GROUP, 6])
        self.block_stats = sb("block_stats", [128, GROUP, 2])
        self.shifted_var = sb("shifted_var", [128, GROUP])
        self.carrier = sb("carrier", [128, 1])
        self.consts_set = top.enter_context(nc.semaphore("consts_set"))
        self.bank = top.enter_context(nc.psum_tensor("bank", [128, 8, 512], F32))
        self.semaphores, self.to_clear = [], []
        self.ident = sb("ident", [128, 128])
        self.ident16 = sb("ident16", [128, 128], BF16)
        self.ln_eps = sb("ln_eps", [128, GROUP])
        self.rms_eps = sb("rms_eps", [128, GROUP])
        self.minus_half = sb("minus_half", [128, GROUP])

    def clear_last(self):
        for old in self.to_clear:
            self.nc.gpsimd.sem_clear(old)

    def rows(self, n):
        return bass.ds(n * GROUP, GROUP)

    def normalise(self, n, xn):
        for j in range(GROUP):
            b = n * GROUP + j
            last = self.nc.vector.tensor_scalar(
                xn[:, j, :], self.x[:, bass.ds(b, 1), :].rearrange("p a d -> p (a d)"),
                self.mean_var[:, bass.ds(b, 1), 0], self.rstd[:, bass.ds(b, 1)],
                ALU.subtract, ALU.mult)
        return last

    def add_to_x(self, dve, n, added, ln):
        nc, r = self.nc, self.rows(n)
        nc.vector.tensor_tensor(out=self.x[:, r, :], in0=added, in1=self.x[:, r, :],
                                op=ALU.add).then_inc(ln.updated, 1)
        dve.wait_ge(ln.updated, n + 1)
        self.settle()
        self.statistics(dve, n, lambda j: self.x[:, bass.ds(n * GROUP + j, 1), :]
                        .rearrange("p a d -> p (a d)"), ln)

    def settle(self):
        self.nc.vector.memset(self.carrier[:, :], 0.0)

    def statistics(self, dve, n, seq, ln):
        nc = self.nc
        for j in range(GROUP):
            last = nc.vector.bn_stats(self.stats[:, j, :], seq(j))
        last.then_inc(ln.stats_ready, 1)
        dve.wait_ge(ln.shifted, n)
        dve.wait_ge(ln.stats_ready, n + 1)
        self.settle()
        for j in range(GROUP):
            last = nc.vector.bn_aggr(self.block_stats[:, j, :], self.stats[:, j, :])
        last.then_inc(ln.merged, 1)
        dve.wait_ge(ln.merged, n + 1)
        nc.vector.tensor_scalar(self.mean_var[:, self.rows(n), :], self.block_stats[:, :, :],
                                1.0, None, ALU.mult).then_inc(ln.var_ready, 1)

    def rstd_of(self, pool, n, ln):
        nc = self.nc
        pool.wait_ge(ln.rstd_ready, n)
        pool.wait_ge(ln.var_ready, n + 1)
        nc.gpsimd.tensor_tensor(out=self.shifted_var[:, :], in0=self.block_stats[:, :, 1],
                                in1=self.ln_eps[:, :], op=ALU.add).then_inc(ln.shifted, 1)
        pool.wait_ge(ln.shifted, n + 1)
        nc.gpsimd.tensor_tensor(out=self.rstd[:, self.rows(n)], in0=self.shifted_var[:, :],
                                in1=self.minus_half[:, :], op=ALU.pow).then_inc(ln.rstd_ready, 1)


class NormSignals:

    def __init__(self, sem):
        self.updated = sem("updated")
        self.stats_ready = sem("stats_ready")
        self.merged = sem("merged")
        self.var_ready = sem("var_ready")
        self.shifted = sem("shifted")
        self.rstd_ready = sem("rstd_ready")


def phase(chip, name):
    ctx, nc = ExitStack(), chip.nc
    chip.to_clear, own = chip.semaphores, []
    chip.semaphores = own

    def sb(t, shape, dt=F32):
        return ctx.enter_context(nc.sbuf_tensor(f"{name}_{t}", shape, dt))

    def sem(t):
        own.append(ctx.enter_context(nc.semaphore(f"{name}_{t}")))
        return own[-1]
    return ctx, sb, sem


def load_stream(chip):
    nc, d = chip.nc, chip.dram
    ctx, sb, sem = phase(chip, "load")
    with ctx:
        x_in = [sem(f"x_in{i}") for i in range(BLOCKS)]
        const_in = sem("const_in")
        ln = NormSignals(sem)
        block = ctx.enter_context(nc.Block())

        @block.sync
        def _(sp):
            for n in range(BLOCKS):
                r = slice(n * GROUP, (n + 1) * GROUP)
                sp.dma_start(chip.x[:, r, :], d["x"][r, :, :].rearrange("b t d -> t b d"))\
                    .then_inc(x_in[n], 16)
            sp.dma_start(chip.ident[:, :], d["ident"][:, :]).then_inc(const_in, 16)

        @block.vector
        def _(dve):
            for n in range(BLOCKS):
                dve.wait_ge(x_in[n], 16)
                chip.statistics(dve, n, lambda j: chip.x[:, n * GROUP + j, :],
                                ln)
            dve.wait_ge(const_in, 16)
            nc.vector.tensor_copy(chip.ident16[:, :], chip.ident[:, :])

        @block.gpsimd
        def _(pool):
            chip.clear_last()
            nc.gpsimd.memset(chip.ln_eps[:, :], LN_EPS).then_inc(chip.consts_set, 1)
            nc.gpsimd.memset(chip.rms_eps[:, :], RMS_EPS).then_inc(chip.consts_set, 1)
            nc.gpsimd.memset(chip.minus_half[:, :], -0.5).then_inc(chip.consts_set, 1)
            pool.wait_ge(chip.consts_set, 3)
            for n in range(BLOCKS):
                chip.rstd_of(pool, n, ln)


def tree_ffn(chip):
    nc, d, bank = chip.nc, chip.dram, chip.bank
    ctx, sb, sem = phase(chip, "tree")
    with ctx:
        w_in = sb("w_in", [128, TREES * NODES])
        b_in = sb("b_in", [128, TREES, 2])
        w_out = sb("w_out", [128, TREES, 2, DIM])
        ancestors = sb("ancestors", [128, NODES], BF16)
        target = sb("target", [128, 2])
        xn = sb("xn", [128, GROUP, DIM])
        xnT = sb("xnT", [128, COLS])
        decide = sb("decide", [128, 2, COLS], BF16)
        act_of = sb("act_of", [128, 4, COLS])
        masked = sb("masked", [128, 4, COLS])
        outT = sb("outT", [128, COLS])
        weights_in, xn_ready, turned, xnT_ready = (
            sem("weights_in"), sem("xn_ready"), sem("turned"), sem("xnT_ready"))
        logits_ready, decided, act_ready, counted, masked_ready, product_done = (
            sem("logits_ready"), sem("decided"), sem("act_ready"), sem("counted"),
            sem("masked_ready"), sem("product_done"))
        outT_ready, out_turned, ln = sem("outT_ready"), sem("out_turned"), NormSignals(sem)
        TURN, OUT, IN, COUNT = 0, 1, 2, 6
        PER = 2 * TREES
        block = ctx.enter_context(nc.Block())

        @block.sync
        def _(sp):
            sp.dma_start(w_in[:, :], d["tree_w_in"][:, :]).then_inc(weights_in, 16)
            sp.dma_start(b_in[:, :, :], d["tree_b_in"][:, :, :]).then_inc(weights_in, 16)
            sp.dma_start(ancestors[:, :], d["tree_ancestors"][:, :]).then_inc(weights_in, 16)
            sp.dma_start(target[:, :], d["tree_target"][:, :]).then_inc(weights_in, 16)
            sp.dma_start(w_out[:, :, :, :], d["tree_w_out"][:, :, :, :]).then_inc(weights_in, 16)

        @block.tensor
        def _(pe):
            def turn(n):
                pe.wait_ge(xn_ready, n + 1)
                for j in range(GROUP):
                    last = nc.tensor.transpose(bank[:, TURN, j * TOK:(j + 1) * TOK], xn[:, j, :],
                                               chip.ident[:, :])
                last.then_inc(turned, 1)

            def logits(n, k):
                t, c = divmod(k, 2)
                m = CHUNK[c]
                if k >= 4:
                    pe.wait_ge(act_ready, PER * n + k - 3)
                nc.tensor.matmul(bank[0:m, IN + k % 4, :],
                                 w_in[:, t * NODES + 128 * c:t * NODES + 128 * c + m], xnT[:, :],
                                 start=True, stop=True).then_inc(logits_ready, 1)

            def count(n, t):
                pe.wait_ge(decided, TREES * n + t + 1)
                for c in range(2):
                    if t:
                        pe.wait_ge(masked_ready, PER * n + 2 * t + c - 1)
                    nc.tensor.matmul(bank[0:CHUNK[c], COUNT + c, :],
                                     ancestors[0:INNER, 128 * c:128 * c + CHUNK[c]],
                                     decide[0:INNER, t % 2, :],
                                     start=True, stop=True).then_inc(counted, 1)

            def product(n, t):
                for c in range(2):
                    k = 2 * t + c
                    pe.wait_ge(masked_ready, PER * n + k + 1)
                    nc.tensor.matmul(bank[:, OUT, :], w_out[0:CHUNK[c], t, c, :],
                                     masked[0:CHUNK[c], k % 4, :],
                                     start=(k == 0), stop=(k == PER - 1)).then_inc(product_done, 1)

            def first_logits(n):
                pe.wait_ge(xnT_ready, n + 1)
                logits(n, 0)
                logits(n, 1)

            def body(n, more):
                for t in range(TREES):
                    if t < TREES - 1:
                        logits(n, 2 * t + 2)
                        logits(n, 2 * t + 3)
                    elif more:
                        turn(n + 1)
                    count(n, t)
                    if t:
                        product(n, t - 1)
                product(n, TREES - 1)
                if more:
                    first_logits(n + 1)
                pe.wait_ge(outT_ready, n + 1)
                for j in range(GROUP):
                    last = nc.tensor.transpose(bank[:, TURN, j * TOK:(j + 1) * TOK],
                                               outT[:, j * TOK:(j + 1) * TOK], chip.ident[:, :])
                last.then_inc(out_turned, 1)

            pe.wait_ge(weights_in, 80)
            turn(0)
            first_logits(0)
            engine_loop(pe, body)

        @block.scalar
        def _(act):
            def silu(n, k):
                t, c = divmod(k, 2)
                m = CHUNK[c]
                if c == 0:
                    act.wait_ge(decided, TREES * n + t + 1)
                else:
                    act.wait_ge(logits_ready, PER * n + k + 1)
                if k >= 4:
                    act.wait_ge(masked_ready, PER * n + k - 3)
                nc.scalar.activation(act_of[0:m, k % 4, :], bank[0:m, IN + k % 4, :], ACT.Silu,
                                     bias=b_in[0:m, t, c:c + 1]).then_inc(act_ready, 1)

            def take_turned(n):
                act.wait_ge(turned, n + 1)
                nc.scalar.copy(xnT[:, :], bank[:, TURN, :]).then_inc(xnT_ready, 1)

            def body(n, more):
                for k in range(2, PER):
                    silu(n, k)
                if more:
                    take_turned(n + 1)
                act.wait_ge(product_done, PER * (n + 1))
                nc.scalar.copy(outT[:, :], bank[:, OUT, :]).then_inc(outT_ready, 1)
                if more:
                    silu(n + 1, 0)
                    silu(n + 1, 1)

            act.wait_ge(weights_in, 80)
            take_turned(0)
            silu(0, 0)
            silu(0, 1)
            engine_loop(act, body)

        @block.vector
        def _(dve):
            def decisions(n, t):
                dve.wait_ge(logits_ready, PER * n + 2 * t + 1)
                if t >= 2:
                    dve.wait_ge(counted, PER * n + 2 * t - 2)
                nc.vector.tensor_scalar(decide[:, t % 2, :], bank[:, IN + (2 * t) % 4, :],
                                        b_in[:, t, 0:1], 0.0, ALU.add, ALU.is_gt)\
                    .then_inc(decided, 1)

            def mask(n, k):
                t, c = divmod(k, 2)
                m = CHUNK[c]
                dve.wait_ge(counted, PER * n + k + 1)
                dve.wait_ge(act_ready, PER * n + k + 1)
                if k >= 4:
                    dve.wait_ge(product_done, PER * n + k - 3)
                nc.vector.scalar_tensor_tensor(
                    out=masked[0:m, k % 4, :], in0=bank[0:m, COUNT + c, :],
                    scalar=target[0:m, c:c + 1], in1=act_of[0:m, k % 4, :],
                    op0=ALU.is_equal, op1=ALU.mult).then_inc(masked_ready, 1)

            def body(n, more):
                for t in range(TREES):
                    if t < TREES - 1:
                        decisions(n, t + 1)
                    mask(n, 2 * t)
                    mask(n, 2 * t + 1)
                    if t == TREES // 2 and more:
                        chip.normalise(n + 1, xn).then_inc(xn_ready, 1)
                if more:
                    decisions(n + 1, 0)
                dve.wait_ge(out_turned, n + 1)
                chip.add_to_x(dve, n, bank[:, TURN, :].rearrange("p (b d) -> p b d", b=GROUP),
                              ln)

            dve.wait_ge(weights_in, 80)
            chip.normalise(0, xn).then_inc(xn_ready, 1)
            decisions(0, 0)
            engine_loop(dve, body)

        @block.gpsimd
        def _(pool):
            chip.clear_last()
            def body(n, more):
                chip.rstd_of(pool, n, ln)
            engine_loop(pool, body)


def engine_loop_pairs(engine, body):
    with engine.Fori(0, BLOCKS // 2 - 1) as r:
        body(2 * r, 0, True)
        body(2 * r + 1, 1, True)
    body(BLOCKS - 2, 0, True)
    body(BLOCKS - 1, 1, False)


def later_wins(nc, size, sc, full, step, larger, equal_or_larger, earlier, rank):
    other, own = bc(sc, 2, size), bc(sc, 3, size)
    step(nc.vector.tensor_tensor(out=larger, in0=other, in1=own, op=ALU.is_gt))
    step(nc.vector.tensor_tensor(out=equal_or_larger, in0=other, in1=own, op=ALU.is_ge))
    step(nc.vector.tensor_tensor(out=equal_or_larger, in0=equal_or_larger, in1=bc(earlier, 1, GROUP),
                                 op=ALU.mult))
    step(nc.vector.tensor_tensor(out=larger, in0=larger, in1=equal_or_larger, op=ALU.max))
    step(nc.vector.tensor_reduce(rank, larger, AX.X, ALU.add))


def moe_ffn(chip):
    nc, d, bank = chip.nc, chip.dram, chip.bank
    ctx, sb, sem = phase(chip, "moe")
    with ctx:
        E, G, C = EXPERTS, EXP_GROUPS, MOE_CHUNKS + 1
        w_route = sb("w_route", [128, E])
        bias = sb("bias", [128, E])
        w_up = sb("w_up", [128, C, 128])
        w_down = sb("w_down", [128, C, DIM])
        spread = sb("spread", [3 * E, MOE_CHUNKS, 128], BF16)
        earlier_group = sb("earlier_group", [128, G, G])
        earlier_expert = sb("earlier_expert", [128, E, E], BF16)
        xn = sb("xn", [128, GROUP, DIM])
        xnT = sb("xnT", [128, 2, COLS])
        score = sb("score", [128, GROUP, E])
        choice = sb("choice", [128, GROUP, E])
        pair_sum = sb("pair_sum", [128, GROUP * G, 6])
        group_score = sb("group_score", [128, GROUP, G])
        group_larger = sb("group_larger", [128, GROUP, G, G])
        group_equal = sb("group_equal", [128, GROUP, G, G])
        group_rank = sb("group_rank", [128, GROUP, G])
        allowed = sb("allowed", [128, GROUP, E])
        larger = sb("larger", [128, GROUP, E, E], BF16)
        equal = sb("equal", [128, GROUP, E, E], BF16)
        rank = sb("rank", [128, GROUP, E])
        chosen = sb("chosen", [128, GROUP, E])
        total = sb("total", [128, GROUP])
        weight = sb("weight", [128, GROUP, E])
        rest = sb("rest", [128, GROUP, E])
        parts = sb("parts", [128, GROUP, 128], BF16)
        partsT = sb("partsT", [3 * E, 2, COLS], BF16)
        relu = sb("relu", [128, 3, COLS])
        weighted = sb("weighted", [128, 2, COLS])
        hidden = sb("hidden", [128, 3, COLS])
        outT = sb("outT", [128, COLS])
        weights_in, xn_ready, turned, xnT_ready = (
            sem("weights_in"), sem("xn_ready"), sem("turned"), sem("xnT_ready"))
        routed, scores_ready, step_done, parts_turned, partsT_ready = (
            sem("routed"), sem("scores_ready"), sem("step_done"), sem("parts_turned"),
            sem("partsT_ready"))
        up_ready, relu_ready, spread_ready, weighted_ready, hidden_ready, product_done = (
            sem("up_ready"), sem("relu_ready"), sem("spread_ready"), sem("weighted_ready"),
            sem("hidden_ready"), sem("product_done"))
        cleared = sem("cleared")
        outT_ready, out_turned, ln = sem("outT_ready"), sem("out_turned"), NormSignals(sem)
        TURN, ROUTE, OUT, UP, SPREAD, PARTS = 0, 1, 2, 3, 5, 7
        STEPS = 26
        partsT_bank = bank[:, PARTS, :].bitcast(BF16)
        block = ctx.enter_context(nc.Block())

        @block.sync
        def _(sp):
            for dst, name in ((w_route, "moe_w_route"), (bias, "moe_bias"), (w_up, "moe_w_up"),
                              (w_down, "moe_w_down"), (spread, "moe_spread"),
                              (earlier_group, "earlier4"), (earlier_expert, "earlier16")):
                dst = dst[:, :, :] if len(dst.shape) == 3 else dst[:, :]
                src = d[name][:, :, :] if len(dst.shape) == 3 else d[name][:, :]
                sp.dma_start(dst, src).then_inc(weights_in, 16)

        @block.tensor
        def _(pe):
            def turn(n):
                pe.wait_ge(xn_ready, n + 1)
                for j in range(GROUP):
                    last = nc.tensor.transpose(bank[:, TURN, j * TOK:(j + 1) * TOK], xn[:, j, :],
                                               chip.ident[:, :])
                last.then_inc(turned, 1)

            def route(n, u):
                pe.wait_ge(xnT_ready, n + 1)
                for j in range(GROUP):
                    last = nc.tensor.matmul(bank[:, ROUTE, j * E:(j + 1) * E],
                                            xnT[:, u, j * TOK:(j + 1) * TOK], w_route[:, :],
                                            start=True, stop=True)
                last.then_inc(routed, 1)

            def turn_parts(n):
                pe.wait_ge(step_done, STEPS * (n + 1))
                for j in range(GROUP):
                    last = nc.tensor.transpose(partsT_bank[:, j * TOK:(j + 1) * TOK], parts[:, j, :],
                                               chip.ident16[:, :])
                last.then_inc(parts_turned, 1)

            def up(n, u, k):
                if k >= 2:
                    pe.wait_ge(relu_ready, C * n + k - 1)
                nc.tensor.matmul(bank[:, UP + k % 2, :], w_up[:, k, :], xnT[:, u, :],
                                 start=True, stop=True).then_inc(up_ready, 1)
                if k < MOE_CHUNKS:
                    if k >= 2:
                        pe.wait_ge(weighted_ready, MOE_CHUNKS * n + k - 1)
                    if k == 0:
                        pe.wait_ge(partsT_ready, n + 1)
                    nc.tensor.matmul(bank[:, SPREAD + k % 2, :], spread[:, k, :], partsT[:, u, :],
                                     start=True, stop=True).then_inc(spread_ready, 1)

            def product(n, k):
                pe.wait_ge(hidden_ready, C * n + k + 1)
                nc.tensor.matmul(bank[:, OUT, :], w_down[:, k, :], hidden[:, k % 3, :],
                                 start=(k == 0), stop=(k == C - 1)).then_inc(product_done, 1)

            def body(n, u, more):
                for k in range(C):
                    if k == 0 and more:
                        turn(n + 1)
                    if k == 2 and more:
                        route(n + 1, 1 - u)
                    if k + 2 < C:
                        up(n, u, k + 2)
                    if k == C - 1 and more:
                        turn_parts(n + 1)
                    product(n, k)
                if more:
                    up(n + 1, 1 - u, 0)
                    up(n + 1, 1 - u, 1)
                pe.wait_ge(outT_ready, n + 1)
                for j in range(GROUP):
                    last = nc.tensor.transpose(bank[:, TURN, j * TOK:(j + 1) * TOK],
                                               outT[:, j * TOK:(j + 1) * TOK], chip.ident[:, :])
                last.then_inc(out_turned, 1)

            pe.wait_ge(weights_in, 7 * 16)
            turn(0)
            route(0, 0)
            turn_parts(0)
            up(0, 0, 0)
            up(0, 0, 1)
            engine_loop_pairs(pe, body)

        @block.scalar
        def _(act):
            def take_turned(n, u):
                act.wait_ge(turned, n + 1)
                nc.scalar.copy(xnT[:, u, :], bank[:, TURN, :]).then_inc(xnT_ready, 1)

            def scores(n):
                act.wait_ge(routed, n + 1)
                nc.scalar.activation(score[:, :, :].rearrange("p b e -> p (b e)"),
                                     bank[:, ROUTE, 0:GROUP * E], ACT.Sigmoid)\
                    .then_inc(scores_ready, 1)

            def take_parts(n, u):
                act.wait_ge(parts_turned, n + 1)
                nc.scalar.copy(partsT[:, u, :], partsT_bank[0:3 * E, 0:COLS])\
                    .then_inc(partsT_ready, 1)

            def rectify(n, k):
                act.wait_ge(up_ready, C * n + k + 1)
                if k >= 3:
                    act.wait_ge(hidden_ready, C * n + k - 2)
                nc.scalar.activation(relu[:, k % 3, :], bank[:, UP + k % 2, :], ACT.Relu)\
                    .then_inc(relu_ready, 1)

            def body(n, u, more):
                for k in range(C):
                    if k == 0 and more:
                        take_turned(n + 1, 1 - u)
                    if k + 2 < C:
                        rectify(n, k + 2)
                    if k == 2 and more:
                        scores(n + 1)
                    if k == C - 1 and more:
                        take_parts(n + 1, 1 - u)
                act.wait_ge(product_done, C * (n + 1))
                nc.scalar.copy(outT[:, :], bank[:, OUT, :]).then_inc(outT_ready, 1)
                if more:
                    rectify(n + 1, 0)
                    rectify(n + 1, 1)

            take_turned(0, 0)
            scores(0)
            take_parts(0, 0)
            rectify(0, 0)
            rectify(0, 1)
            engine_loop_pairs(act, body)

        @block.vector
        def _(dve):
            def routing(n):
                done = [0]

                def step(instruction):
                    instruction.then_inc(step_done, 1)
                    done[0] += 1
                    dve.wait_ge(step_done, STEPS * n + done[0])
                quads = lambda t: t[:, :, :].rearrange("p b (g e) -> p (b g) e", e=PER_GROUP)
                flat = lambda t: t[:, :, :].rearrange("p b g -> p (b g)")

                def group_sums():
                    dve.wait_ge(scores_ready, n + 1)
                    step(nc.vector.tensor_tensor(out=choice[:, :, :], in0=score[:, :, :],
                                                 in1=bc(bias[:, :], 1, GROUP), op=ALU.add))
                    c, at = quads(choice), 0
                    for apart in range(1, PER_GROUP):
                        size = PER_GROUP - apart
                        add = nc.vector.tensor_tensor(out=pair_sum[:, :, at:at + size],
                                                      in0=c[:, :, 0:size], in1=c[:, :, apart:],
                                                      op=ALU.add)
                        at += size
                        step(add)
                    step(nc.vector.tensor_reduce(flat(group_score), pair_sum[:, :, :], AX.X, ALU.max))

                def group_ranks():
                    later_wins(nc, G, group_score[:, :, :], None, step, group_larger[:, :, :, :],
                               group_equal[:, :, :, :], earlier_group[:, :, :], group_rank[:, :, :])

                def allow():
                    step(nc.vector.scalar_tensor_tensor(
                        out=quads(allowed), in0=bc(flat(group_rank), 2, PER_GROUP),
                        scalar=float(TOP_GROUPS), in1=quads(choice), op0=ALU.is_lt, op1=ALU.mult))

                def expert_ranks():
                    later_wins(nc, E, allowed[:, :, :], None, step, larger[:, :, :, :],
                               equal[:, :, :, :], earlier_expert[:, :, :], rank[:, :, :])

                def weigh():
                    step(nc.vector.scalar_tensor_tensor(
                        out=chosen[:, :, :], in0=rank[:, :, :], scalar=float(TOP_EXPERTS),
                        in1=score[:, :, :], op0=ALU.is_lt, op1=ALU.mult))
                    step(nc.vector.tensor_reduce(total[:, :], chosen[:, :, :], AX.X, ALU.add))
                    step(nc.vector.tensor_scalar(total[:, :], total[:, :], 1e-20, None, ALU.add))
                    step(nc.vector.reciprocal(total[:, :], total[:, :]))
                    step(nc.vector.scalar_tensor_tensor(
                        out=weight[:, :, :], in0=chosen[:, :, :], scalar=ROUTE_SCALE,
                        in1=bc(total[:, :], 2, E), op0=ALU.mult, op1=ALU.mult))

                def split():
                    bf16_parts(nc, step, weight[:, :, :], rest[:, :, :],
                               [parts[:, :, i * E:(i + 1) * E] for i in range(3)])
                return [group_sums, group_ranks, allow, expert_ranks, weigh, split]

            def weigh_hidden(n, k):
                dve.wait_ge(relu_ready, C * n + k + 1)
                dve.wait_ge(spread_ready, MOE_CHUNKS * n + k + 1)
                if k >= 2:
                    dve.wait_ge(hidden_ready, C * n + k - 1)
                nc.vector.tensor_tensor(out=weighted[:, k % 2, :], in0=relu[:, k % 3, :],
                                        in1=bank[:, SPREAD + k % 2, :], op=ALU.mult)\
                    .then_inc(weighted_ready, 1)

            def body(n, u, more):
                pieces = routing(n + 1) if more else []
                if more:
                    chip.normalise(n + 1, xn).then_inc(xn_ready, 1)
                for k in range(MOE_CHUNKS):
                    weigh_hidden(n, k)
                    if k >= 2 and pieces:
                        pieces.pop(0)()
                dve.wait_ge(out_turned, n + 1)
                chip.add_to_x(dve, n, bank[:, TURN, :].rearrange("p (b d) -> p b d", b=GROUP), ln)

            dve.wait_ge(weights_in, 7 * 16)
            nc.vector.memset(parts[:, :, :], 0.0).then_inc(cleared, 1)
            dve.wait_ge(cleared, 1)
            chip.normalise(0, xn).then_inc(xn_ready, 1)
            for piece in routing(0):
                piece()
            engine_loop_pairs(dve, body)

        @block.gpsimd
        def _(pool):
            chip.clear_last()
            def hide(n, k):
                if k < MOE_CHUNKS:
                    pool.wait_ge(weighted_ready, MOE_CHUNKS * n + k + 1)
                    other = weighted[:, k % 2, :]
                else:
                    pool.wait_ge(relu_ready, C * n + k + 1)
                    other = relu[:, k % 3, :]
                if k >= 3:
                    pool.wait_ge(product_done, C * n + k - 2)
                nc.gpsimd.tensor_tensor(out=hidden[:, k % 3, :], in0=relu[:, k % 3, :], in1=other,
                                        op=ALU.mult).then_inc(hidden_ready, 1)

            def body(n, u, more):
                for k in range(C):
                    hide(n, k)
                chip.rstd_of(pool, n, ln)
            engine_loop_pairs(pool, body)


def bf16_parts(nc, step, value, rest, parts):
    step(nc.vector.tensor_copy(parts[0], value))
    step(nc.vector.tensor_tensor(out=rest, in0=value, in1=parts[0], op=ALU.subtract))
    step(nc.vector.tensor_copy(parts[1], rest))
    step(nc.vector.tensor_tensor(out=rest, in0=rest, in1=parts[1], op=ALU.subtract))
    step(nc.vector.tensor_copy(parts[2], rest))


def gated_ffn(chip):
    nc, d, bank = chip.nc, chip.dram, chip.bank
    ctx, sb, sem = phase(chip, "gated")
    with ctx:
        E = GATED
        w_gate = sb("w_gate", [128, E])
        b_gate = sb("b_gate", [128, E])
        w_expert = sb("w_expert", [128, E, DIM])
        b_expert = sb("b_expert", [3 * E, DIM])
        spread = sb("spread", [3 * E, E, 128], BF16)
        earlier = sb("earlier", [128, E, E], BF16)
        xn = sb("xn", [128, GROUP, DIM])
        xnT = sb("xnT", [128, 2, COLS])
        logit = sb("logit", [128, GROUP, E])
        larger = sb("larger", [128, GROUP, E, E], BF16)
        equal = sb("equal", [128, GROUP, E, E], BF16)
        rank = sb("rank", [128, GROUP, E])
        best = sb("best", [128, GROUP])
        shifted = sb("shifted", [128, GROUP, E])
        power = sb("power", [128, GROUP, E])
        kept = sb("kept", [128, GROUP, E])
        total = sb("total", [128, GROUP])
        gate = sb("gate", [128, GROUP, E])
        rest = sb("rest", [128, GROUP, E])
        parts = sb("parts", [128, GROUP, 3, E], BF16)
        partsT = sb("partsT", [3 * E, 2, COLS], BF16)
        partsT32 = sb("partsT32", [3 * E, 2, COLS])
        gated = sb("gated", [128, 3, COLS])
        outT = sb("outT", [128, COLS])
        weights_in, xn_ready, turned, xnT_ready = (
            sem("weights_in"), sem("xn_ready"), sem("turned"), sem("xnT_ready"))
        routed, shift_ready, power_ready, step_done, parts_turned, partsT_ready = (
            sem("routed"), sem("shift_ready"), sem("power_ready"), sem("step_done"),
            sem("parts_turned"), sem("partsT_ready"))
        spread_ready, gated_ready, product_done = (
            sem("spread_ready"), sem("gated_ready"), sem("product_done"))
        outT_ready, out_turned, ln = sem("outT_ready"), sem("out_turned"), NormSignals(sem)
        TURN, ROUTE, OUT, SPREAD, PARTS = 0, 1, 2, 3, 7
        SPREADS = 4
        partsT_bank = bank[:, PARTS, :].bitcast(BF16)
        STEPS = 17
        block = ctx.enter_context(nc.Block())

        @block.sync
        def _(sp):
            for dst, name in ((w_gate, "gated_w_gate"), (b_gate, "gated_b_gate"),
                              (w_expert, "gated_w"), (b_expert, "gated_b"),
                              (spread, "gated_spread"), (earlier, "earlier8")):
                dst = dst[:, :, :] if len(dst.shape) == 3 else dst[:, :]
                src = d[name][:, :, :] if len(dst.shape) == 3 else d[name][:, :]
                sp.dma_start(dst, src).then_inc(weights_in, 16)

        @block.tensor
        def _(pe):
            def turn(n):
                pe.wait_ge(xn_ready, n + 1)
                for j in range(GROUP):
                    last = nc.tensor.transpose(bank[:, TURN, j * TOK:(j + 1) * TOK], xn[:, j, :],
                                               chip.ident[:, :])
                last.then_inc(turned, 1)

            def route(n, u):
                pe.wait_ge(xnT_ready, n + 1)
                for j in range(GROUP):
                    last = nc.tensor.matmul(bank[:, ROUTE, j * E:(j + 1) * E],
                                            xnT[:, u, j * TOK:(j + 1) * TOK], w_gate[:, :],
                                            start=True, stop=True)
                last.then_inc(routed, 1)

            def turn_parts(n):
                pe.wait_ge(step_done, STEPS * (n + 1))
                for j in range(GROUP):
                    last = nc.tensor.transpose(partsT_bank[0:3 * E, j * TOK:(j + 1) * TOK],
                                               parts[:, j, :, :].rearrange("p a e -> p (a e)"),
                                               chip.ident16[:, :])
                last.then_inc(parts_turned, 1)

            def spread_gate(n, u, k):
                if k == 0:
                    pe.wait_ge(partsT_ready, 2 * (n + 1))
                if k >= SPREADS:
                    pe.wait_ge(gated_ready, E * n + k - SPREADS + 1)
                nc.tensor.matmul(bank[:, SPREAD + k % SPREADS, :], spread[:, k, :], partsT[:, u, :],
                                 start=True, stop=True).then_inc(spread_ready, 1)

            def product(n, k):
                pe.wait_ge(gated_ready, E * n + k + 1)
                nc.tensor.matmul(bank[:, OUT, :], w_expert[:, k, :], gated[:, k % 3, :],
                                 start=False, stop=(k == E - 1)).then_inc(product_done, 1)

            def body(n, u, more):
                nc.tensor.matmul(bank[:, OUT, :], b_expert[:, :], partsT32[:, u, :],
                                 start=True, stop=False)
                for k in range(E):
                    if k == 0 and more:
                        turn(n + 1)
                    if k == 1 and more:
                        route(n + 1, 1 - u)
                    if k + 3 < E:
                        spread_gate(n, u, k + 3)
                    product(n, k)
                if more:
                    turn_parts(n + 1)
                    for k in range(3):
                        spread_gate(n + 1, 1 - u, k)
                pe.wait_ge(outT_ready, n + 1)
                for j in range(GROUP):
                    last = nc.tensor.transpose(bank[:, TURN, j * TOK:(j + 1) * TOK],
                                               outT[:, j * TOK:(j + 1) * TOK], chip.ident[:, :])
                last.then_inc(out_turned, 1)

            pe.wait_ge(weights_in, 6 * 16)
            turn(0)
            route(0, 0)
            turn_parts(0)
            for k in range(3):
                spread_gate(0, 0, k)
            engine_loop_pairs(pe, body)

        @block.scalar
        def _(act):
            def take_turned(n, u):
                act.wait_ge(turned, n + 1)
                nc.scalar.copy(xnT[:, u, :], bank[:, TURN, :]).then_inc(xnT_ready, 1)

            def exps(n):
                act.wait_ge(shift_ready, n + 1)
                nc.scalar.activation(power[:, :, :].rearrange("p b e -> p (b e)"),
                                     shifted[:, :, :].rearrange("p b e -> p (b e)"), ACT.Exp)\
                    .then_inc(power_ready, 1)

            def take_parts(n, u):
                act.wait_ge(parts_turned, n + 1)
                nc.scalar.copy(partsT[:, u, :], partsT_bank[0:3 * E, 0:COLS])\
                    .then_inc(partsT_ready, 1)
                nc.scalar.copy(partsT32[:, u, :], partsT_bank[0:3 * E, 0:COLS])\
                    .then_inc(partsT_ready, 1)

            def body(n, u, more):
                if more:
                    take_turned(n + 1, 1 - u)
                    exps(n + 1)
                act.wait_ge(product_done, E * (n + 1))
                nc.scalar.copy(outT[:, :], bank[:, OUT, :]).then_inc(outT_ready, 1)
                if more:
                    take_parts(n + 1, 1 - u)

            take_turned(0, 0)
            exps(0)
            take_parts(0, 0)
            engine_loop_pairs(act, body)

        @block.vector
        def _(dve):
            def gates(n):
                done = [0]

                def step(instruction):
                    instruction.then_inc(step_done, 1)
                    done[0] += 1
                    dve.wait_ge(step_done, STEPS * n + done[0])

                def logits():
                    dve.wait_ge(routed, n + 1)
                    step(nc.vector.tensor_tensor(
                        out=logit[:, :, :],
                        in0=bank[:, ROUTE, 0:GROUP * E].rearrange("p (b e) -> p b e", e=E),
                        in1=bc(b_gate[:, :], 1, GROUP), op=ALU.add))
                    step(nc.vector.tensor_reduce(best[:, :], logit[:, :, :], AX.X, ALU.max))
                    step(nc.vector.tensor_tensor(out=shifted[:, :, :], in0=logit[:, :, :],
                                                 in1=bc(best[:, :], 2, E), op=ALU.subtract))
                    nc.vector.memset(chip.carrier[:, :], 0.0).then_inc(shift_ready, 1)

                def ranks():
                    later_wins(nc, E, logit[:, :, :], None, step, larger[:, :, :, :],
                               equal[:, :, :, :], earlier[:, :, :], rank[:, :, :])

                def mix():
                    dve.wait_ge(power_ready, n + 1)
                    step(nc.vector.scalar_tensor_tensor(
                        out=kept[:, :, :], in0=rank[:, :, :], scalar=float(TOP_GATED),
                        in1=power[:, :, :], op0=ALU.is_lt, op1=ALU.mult))
                    step(nc.vector.tensor_reduce(total[:, :], kept[:, :, :], AX.X, ALU.add))
                    step(nc.vector.reciprocal(total[:, :], total[:, :]))
                    step(nc.vector.tensor_tensor(out=gate[:, :, :], in0=kept[:, :, :],
                                                 in1=bc(total[:, :], 2, E), op=ALU.mult))

                def split():
                    bf16_parts(nc, step, gate[:, :, :], rest[:, :, :],
                               [parts[:, :, i, :] for i in range(3)])
                return [logits, ranks, mix, split]

            def times_gate(n, u, k):
                dve.wait_ge(spread_ready, E * n + k + 1)
                if k >= 3:
                    dve.wait_ge(product_done, E * n + k - 2)
                nc.vector.tensor_tensor(out=gated[:, k % 3, :], in0=xnT[:, u, :],
                                        in1=bank[:, SPREAD + k % SPREADS, :], op=ALU.mult)\
                    .then_inc(gated_ready, 1)

            def body(n, u, more):
                pieces = gates(n + 1) if more else []
                if more:
                    chip.normalise(n + 1, xn).then_inc(xn_ready, 1)
                for k in range(E):
                    times_gate(n, u, k)
                    if k >= 3 and pieces:
                        pieces.pop(0)()
                dve.wait_ge(out_turned, n + 1)
                chip.add_to_x(dve, n, bank[:, TURN, :].rearrange("p (b d) -> p b d", b=GROUP), ln)

            dve.wait_ge(weights_in, 6 * 16)
            chip.normalise(0, xn).then_inc(xn_ready, 1)
            for piece in gates(0):
                piece()
            engine_loop_pairs(dve, body)

        @block.gpsimd
        def _(pool):
            chip.clear_last()
            def body(n, u, more):
                chip.rstd_of(pool, n, ln)
            engine_loop_pairs(pool, body)


def heads_attention(chip, name, clipped):
    nc, d, bank = chip.nc, chip.dram, chip.bank
    ctx, sb, sem = phase(chip, name)
    with ctx:
        QUARTERS = HEADS // QUAD
        HALF = HEADS // 2
        UNITS = 2 * GROUP
        scale = HEAD_DIM ** -0.5
        w_q, w_k, w_v, w_o = (sb(t, [128, DIM]) for t in ("w_q", "w_k", "w_v", "w_o"))
        b_q, b_k = sb("b_q", [128, 1]), sb("b_k", [128, 1])
        b_v = sb("b_v", [KEYS, DIM])
        b_o = sb("b_o", [1, DIM])
        ones = sb("ones", [1, TOK])
        own_head = sb("own_head", [128, HEADS])
        ctxT = sb("ctxT", [128, GROUP, KEYS])
        xn = sb("xn", [128, GROUP, DIM])
        xnT = sb("xnT", [128, COLS])
        qT = sb("qT", [128, COLS])
        kT = sb("kT", [128, GROUP, KEYS])
        own_kT = sb("own_kT", [128, 2, HEADS, KEYS])
        v = sb("v", [KEYS, GROUP, HEADS, HEAD_DIM + 1])
        largest = sb("largest", [128, 2, HALF])
        below = sb("below", [128, 2, HALF, KEYS])
        powers = sb("powers", [128, 2, HALF, KEYS])
        powersT = sb("powersT", [KEYS, QUARTERS, QUAD * TOK])
        raw = sb("raw", [128, 2, HEADS, HEAD_DIM + 1])
        inverse = sb("inverse", [128, 2, HEADS])
        heads_out = sb("heads_out", [128, GROUP, DIM])
        heads_outT = sb("heads_outT", [128, COLS])
        if clipped:
            mask = sb("mask", [128, GROUP, KEYS], I32)
            limit = sb("limit", [128, GROUP, KEYS])
            mask_in, forbidden, limit_ready = sem("mask_in"), sem("forbidden"), sem("limit_ready")
        weights_in, ctx_in, consts, xn_ready, turned, xnT_ready = (
            sem("weights_in"), sem("ctx_in"), sem("consts"), sem("xn_ready"), sem("turned"),
            sem("xnT_ready"))
        own_ready, sums_taken = sem("own_ready"), sem("sums_taken")
        q_made, k_made, v_made, q_ready, k_ready, v_ready = (
            sem("q_made"), sem("k_made"), sem("v_made"), sem("q_ready"), sem("k_ready"),
            sem("v_ready"))
        scores_ready, scores_taken, largest_ready, below_ready, powers_ready = (
            sem("scores_ready"), sem("scores_taken"), sem("largest_ready"), sem("below_ready"),
            sem("powers_ready"))
        powers_turned, powersT_ready, heads_summed, inverse_ready, heads_out_ready = (
            sem("powers_turned"), sem("powersT_ready"), sem("heads_summed"), sem("inverse_ready"),
            sem("heads_out_ready"))
        heads_turned, heads_outT_ready, projected, ln = (
            sem("heads_turned"), sem("heads_outT_ready"), sem("projected"), NormSignals(sem))
        SCORES, TURNED, SUMS, MISC = 0, 4, 6, 7
        LOADS = [(w_q, "w_q"), (w_k, "w_k"), (w_v, "w_v"), (w_o, "w_o"), (b_q, "b_q"),
                 (b_k, "b_k"), (b_v, "b_v"), (b_o, "b_o"), (own_head, "own_head")]
        PARTS = GROUP * QUARTERS
        sums = bank[:, SUMS, 0:HEADS * (HEAD_DIM + 1)].rearrange("p (h c) -> p h c", h=HEADS)
        block = ctx.enter_context(nc.Block())

        @block.sync
        def _(sp):
            for dst, t in LOADS:
                src = d[t if t == "own_head" else f"{name}_{t}"]
                sp.dma_start(dst[:, :], src[:, :]).then_inc(weights_in, 16)

            def load(n):
                r = chip.rows(n)
                sp.dma_start(ctxT[:, :, :], d["ctxT"][:, r, :]).then_inc(ctx_in, 16)
                if clipped:
                    sp.dma_start(mask[:, :, :], d["mask"][:, r, :]).then_inc(mask_in, 16)

            def body(n, more):
                if more:
                    sp.wait_ge(k_made, n + 1)
                    sp.wait_ge(v_made, n + 1)
                    if clipped:
                        sp.wait_ge(forbidden, n + 1)
                    load(n + 1)
            load(0)
            engine_loop(sp, body)

        @block.tensor
        def _(pe):
            def turn(n):
                pe.wait_ge(xn_ready, n + 1)
                for j in range(GROUP):
                    last = nc.tensor.transpose(bank[:, MISC, j * TOK:(j + 1) * TOK], xn[:, j, :],
                                               chip.ident[:, :])
                last.then_inc(turned, 1)

            def project_q(n, half):
                if half == 0:
                    pe.wait_ge(xnT_ready, n + 1)
                else:
                    pe.wait_ge(q_ready, 2 * n + 1)
                cols = slice(half * COLS // 2, (half + 1) * COLS // 2)
                nc.tensor.matmul(bank[:, MISC, cols], w_q[:, :], xnT[:, cols],
                                 start=True, stop=True).then_inc(q_made, 1)

            def project_k(n):
                pe.wait_ge(ctx_in, 16 * (n + 1))
                nc.tensor.matmul(bank[:, MISC, 0:KCOLS], w_k[:, :],
                                 ctxT[:, :, :].rearrange("p b k -> p (b k)"),
                                 start=True, stop=True).then_inc(k_made, 1)

            def project_v(n):
                pe.wait_ge(q_ready, 2 * n + 2)
                for j in range(GROUP):
                    last = nc.tensor.matmul(bank[0:KEYS, MISC, j * DIM:(j + 1) * DIM],
                                            ctxT[:, j, :], w_v[:, :], start=True, stop=True)
                last.then_inc(v_made, 1)

            def scores(n, i, first=False):
                j, half = divmod(i, 2)
                x = UNITS * n + i
                if i % 4 == 0:
                    pe.wait_ge(q_ready, 2 * n + i // 4 + 1)
                if half == 0:
                    pe.wait_ge(own_ready, GROUP * n + j + 1)
                if not first:
                    pe.wait_ge(scores_taken, x - 1)
                for g in range(2):
                    h = HALF * half + QUAD * g
                    last = nc.tensor.matmul(bank[:, SCORES + 2 * half + g, 0:QUAD * KEYS],
                                            qT[:, j * TOK:(j + 1) * TOK],
                                            own_kT[:, j % 2, h:h + QUAD, :]
                                            .rearrange("p h k -> p (h k)"),
                                            start=True, stop=True)
                last.then_inc(scores_ready, 1)

            def turn_powers(n, i, g, first=False):
                x = UNITS * n + i
                if g == 0:
                    pe.wait_ge(powers_ready, x + 1)
                if not first:
                    pe.wait_ge(powersT_ready, 2 * x + g - 1)
                for h in range(QUAD):
                    last = nc.tensor.transpose(
                        bank[0:KEYS, TURNED + g, h * TOK:(h + 1) * TOK],
                        powers[:, i % 2, QUAD * g + h, :], chip.ident[:, :])
                last.then_inc(powers_turned, 1)

            def sum_values(n, i, g):
                j, half = divmod(i, 2)
                if half == 0 and g == 0:
                    pe.wait_ge(sums_taken, GROUP * n + j)
                    if j == 0:
                        pe.wait_ge(v_ready, n + 1)
                        pe.wait_ge(heads_outT_ready, n)
                pe.wait_ge(powersT_ready, 2 * (UNITS * n + i) + g + 1)
                part = 2 * half + g
                for t in range(QUAD):
                    h = QUAD * part + t
                    last = nc.tensor.matmul(sums[:, h, :], powersT[:, part, t * TOK:(t + 1) * TOK],
                                            v[:, j, h, :], start=True, stop=True)
                last.then_inc(heads_summed, 1)

            def project_out(n, more):
                pe.wait_ge(heads_out_ready, GROUP * (n + 1))
                pe.wait_ge(sums_taken, GROUP * (n + 1))
                for j in range(GROUP):
                    last = nc.tensor.transpose(bank[:, SUMS, j * TOK:(j + 1) * TOK],
                                               heads_out[:, j, :], chip.ident[:, :])
                last.then_inc(heads_turned, 1)
                pe.wait_ge(v_ready, n + 2 if more else n + 1)
                pe.wait_ge(heads_outT_ready, n + 1)
                for j in range(GROUP):
                    nc.tensor.matmul(bank[:, MISC, j * DIM:(j + 1) * DIM],
                                     heads_outT[:, j * TOK:(j + 1) * TOK], w_o[:, :],
                                     start=True, stop=False)
                    last = nc.tensor.matmul(bank[:, MISC, j * DIM:(j + 1) * DIM], ones[:, :],
                                            b_o[:, :], start=False, stop=True)
                last.then_inc(projected, 1)

            def body(n, more):
                for i in range(UNITS):
                    if i:
                        turn_powers(n, i, 0)
                    if i < UNITS - 2:
                        scores(n, i + 2)
                    elif more:
                        scores(n + 1, i + 2 - UNITS)
                    if i:
                        turn_powers(n, i, 1)
                    sum_values(n, i, 0)
                    if more:
                        if i == 2:
                            pe.wait_ge(ln.updated, n)
                            project_k(n + 1)
                        elif i == 3:
                            pe.wait_ge(k_ready, n + 2)
                            turn(n + 1)
                        elif i == 4:
                            project_q(n + 1, 0)
                        elif i == 6:
                            project_q(n + 1, 1)
                        elif i == 7:
                            project_v(n + 1)
                    sum_values(n, i, 1)
                if more:
                    turn_powers(n + 1, 0, 0)
                    turn_powers(n + 1, 0, 1)
                project_out(n, more)

            pe.wait_ge(weights_in, 16 * len(LOADS))
            pe.wait_ge(consts, 2)
            project_k(0)
            pe.wait_ge(k_ready, 1)
            turn(0)
            project_q(0, 0)
            project_q(0, 1)
            project_v(0)
            scores(0, 0, True)
            scores(0, 1, True)
            turn_powers(0, 0, 0, True)
            turn_powers(0, 0, 1, True)
            engine_loop(pe, body)

        @block.scalar
        def _(act):
            def take_turned(n):
                act.wait_ge(turned, n + 1)
                nc.scalar.copy(xnT[:, :], bank[:, MISC, :]).then_inc(xnT_ready, 1)

            def take_q(n, half):
                act.wait_ge(q_made, 2 * n + half + 1)
                act.wait_ge(scores_ready, UNITS * n - 4 + 4 * half)
                cols = slice(half * COLS // 2, (half + 1) * COLS // 2)
                nc.scalar.activation(qT[:, cols], bank[:, MISC, cols], ACT.Identity,
                                     bias=b_q[:, 0:1]).then_inc(q_ready, 1)

            def exps(n, i, first=False):
                x = UNITS * n + i
                act.wait_ge(below_ready, x + 1)
                if not first:
                    act.wait_ge(powers_turned, 2 * (x - 1))
                nc.scalar.activation(powers[:, i % 2, :, :].rearrange("p h k -> p (h k)"),
                                     below[:, i % 2, :, :].rearrange("p h k -> p (h k)"),
                                     ACT.Exp, scale=scale).then_inc(powers_ready, 1)

            def take_powers(n, i, g, first=False):
                q = 2 * (UNITS * n + i) + g
                act.wait_ge(powers_turned, q + 1)
                if not first:
                    act.wait_ge(heads_summed, q - QUARTERS + 1)
                nc.scalar.copy(powersT[:, 2 * (i % 2) + g, :], bank[0:KEYS, TURNED + g, :])\
                    .then_inc(powersT_ready, 1)

            def take_sums(n, j):
                m = GROUP * n + j
                act.wait_ge(heads_summed, QUARTERS * (m + 1))
                if j >= 2:
                    act.wait_ge(heads_out_ready, m - 1)
                elif j == 0:
                    act.wait_ge(heads_out_ready, GROUP * n)
                nc.scalar.copy(raw[:, j % 2, :, :], sums).then_inc(sums_taken, 1)

            def body(n, more):
                for i in range(UNITS):
                    if i:
                        take_powers(n, i, 0, i < 2)
                        take_powers(n, i, 1, i < 2)
                    if i < UNITS - 1:
                        exps(n, i + 1)
                    elif more:
                        exps(n + 1, 0)
                    if i % 2:
                        take_sums(n, i // 2)
                    if more:
                        if i == 3:
                            take_turned(n + 1)
                        elif i == 4:
                            take_q(n + 1, 0)
                        elif i == 6:
                            take_q(n + 1, 1)
                if more:
                    take_powers(n + 1, 0, 0)
                    take_powers(n + 1, 0, 1)
                act.wait_ge(heads_turned, n + 1)
                nc.scalar.copy(heads_outT[:, :], bank[:, SUMS, :]).then_inc(heads_outT_ready, 1)

            act.wait_ge(weights_in, 16 * len(LOADS))
            take_turned(0)
            for half in range(2):
                act.wait_ge(q_made, half + 1)
                cols = slice(half * COLS // 2, (half + 1) * COLS // 2)
                nc.scalar.activation(qT[:, cols], bank[:, MISC, cols], ACT.Identity,
                                     bias=b_q[:, 0:1]).then_inc(q_ready, 1)
            exps(0, 0, True)
            take_powers(0, 0, 0, True)
            take_powers(0, 0, 1, True)
            engine_loop(act, body)

        @block.vector
        def _(dve):
            def take_k(n):
                dve.wait_ge(k_made, n + 1)
                dve.wait_ge(own_ready, GROUP * n)
                nc.vector.tensor_scalar(
                    kT[:, :, :], bank[:, MISC, 0:KCOLS].rearrange("p (b k) -> p b k", b=GROUP),
                    b_k[:, 0:1], None, ALU.add).then_inc(k_ready, 1)

            def take_v(n):
                dve.wait_ge(v_made, n + 1)
                nc.vector.tensor_tensor(
                    out=v[:, :, :, 0:HEAD_DIM],
                    in0=bank[0:KEYS, MISC, :].rearrange("p (b h c) -> p b h c", b=GROUP, h=HEADS),
                    in1=bc(b_v[:, :].rearrange("p (h c) -> p h c", h=HEADS), 1, GROUP),
                    op=ALU.add).then_inc(v_ready, 1)

            def limits(n):
                dve.wait_ge(mask_in, 16 * (n + 1))
                nc.vector.tensor_scalar(limit[:, :, :], mask[:, :, :], 0.0, -1e30, ALU.is_equal,
                                        ALU.mult).then_inc(forbidden, 1)
                dve.wait_ge(forbidden, n + 1)
                nc.vector.tensor_scalar(limit[:, :, :], limit[:, :, :], CLIP / scale, None,
                                        ALU.add).then_inc(limit_ready, 1)
                dve.wait_ge(limit_ready, n + 1)

            def softmax(n, i, first=False):
                j, half = divmod(i, 2)
                x = UNITS * n + i
                scores = bank[:, SCORES + 2 * half:SCORES + 2 * half + 2, 0:QUAD * KEYS].rearrange(
                    "p g (h k) -> p g h k", k=KEYS)
                result = below[:, half, :, :].rearrange("p (g h) k -> p g h k", g=2)
                dve.wait_ge(scores_ready, x + 1)
                if clipped:
                    if not first:
                        dve.wait_ge(powers_ready, x - 1)
                    for g in range(2):
                        last = nc.vector.scalar_tensor_tensor(
                            out=result[:, g], in0=scores[:, g], scalar=-CLIP / scale,
                            in1=bc(limit[:, j, :], 1, QUAD), op0=ALU.max, op1=ALU.min)
                    last.then_inc(scores_taken, 1)
                    dve.wait_ge(scores_taken, x + 1)
                    scores = result
                nc.vector.tensor_reduce(largest[:, half, :].rearrange("p (g h) -> p g h", g=2),
                                        scores, AX.X, ALU.max).then_inc(largest_ready, 1)
                if not clipped and not first:
                    dve.wait_ge(powers_ready, x - 1)
                dve.wait_ge(largest_ready, x + 1)
                nc.vector.tensor_tensor(
                    out=result, in0=scores,
                    in1=bc(largest[:, half, :].rearrange("p (g h) -> p g h", g=2), 3, KEYS),
                    op=ALU.subtract).then_inc(below_ready, 1)
                if not clipped:
                    nc.vector.memset(chip.carrier[:, :], 0.0).then_inc(scores_taken, 1)

            def divide(n, j):
                m = GROUP * n + j
                dve.wait_ge(sums_taken, m + 1)
                nc.vector.reciprocal(inverse[:, j % 2, :], raw[:, j % 2, :, HEAD_DIM])\
                    .then_inc(inverse_ready, 1)
                dve.wait_ge(inverse_ready, m + 1)
                nc.vector.tensor_tensor(
                    out=heads_out[:, j, :].rearrange("p (h c) -> p h c", h=HEADS),
                    in0=raw[:, j % 2, :, 0:HEAD_DIM], in1=bc(inverse[:, j % 2, :], 2, HEAD_DIM),
                    op=ALU.mult).then_inc(heads_out_ready, 1)

            def body(n, more):
                for i in range(1, UNITS):
                    if i < UNITS - 2:
                        softmax(n, i + 2)
                    elif more:
                        if clipped and i == UNITS - 2:
                            limits(n + 1)
                        softmax(n + 1, i + 2 - UNITS)
                    if i == 2 and more:
                        chip.normalise(n + 1, xn).then_inc(xn_ready, 1)
                        take_k(n + 1)
                    if i % 2:
                        divide(n, i // 2)
                if more:
                    take_v(n + 1)
                    softmax(n + 1, 2)
                dve.wait_ge(projected, n + 1)
                chip.add_to_x(dve, n, bank[:, MISC, :].rearrange("p (b d) -> p b d", b=GROUP), ln)

            dve.wait_ge(weights_in, 16 * len(LOADS))
            chip.normalise(0, xn).then_inc(xn_ready, 1)
            if clipped:
                limits(0)
            take_k(0)
            dve.wait_ge(consts, 2)
            take_v(0)
            softmax(0, 0, True)
            softmax(0, 1, True)
            softmax(0, 2)
            engine_loop(dve, body)

        @block.gpsimd
        def _(pool):
            chip.clear_last()
            nc.gpsimd.memset(ones[:, :], 1.0).then_inc(consts, 1)
            nc.gpsimd.memset(v[:, :, :, HEAD_DIM], 1.0).then_inc(consts, 1)

            def own(n, j):
                if j == 0:
                    pool.wait_ge(k_ready, n + 1)
                nc.gpsimd.tensor_tensor(out=own_kT[:, j % 2, :, :], in0=bc(kT[:, j, :], 1, HEADS),
                                        in1=bc(own_head[:, :], 2, KEYS),
                                        op=ALU.mult).then_inc(own_ready, 1)

            def body(n, more):
                pool.wait_ge(scores_ready, UNITS * n + 4)
                own(n, 3)
                if more:
                    for j in range(3):
                        pool.wait_ge(scores_ready, UNITS * n + 2 * (j + 3))
                        own(n + 1, j)
                chip.rstd_of(pool, n, ln)
            pool.wait_ge(weights_in, 16 * len(LOADS))
            own(0, 0)
            own(0, 1)
            pool.wait_ge(scores_ready, 2)
            own(0, 2)
            engine_loop(pool, body)


def slot_attention(chip):
    nc, d, bank = chip.nc, chip.dram, chip.bank
    ctx, sb, sem = phase(chip, "slots")
    with ctx:
        scale = DIM ** -0.5
        TWO = (0, 1)
        w_q, w_k, w_v = (sb(t, [128, DIM]) for t in ("w_q", "w_k", "w_v"))
        w_ih, w_hh = sb("w_ih", [128, 3, DIM]), sb("w_hh", [128, 3, DIM])
        b_ih, b_hh = sb("b_ih", [128, 3]), sb("b_hh", [128, 3])
        half_b = sb("half_b", [128, 3])
        slot_norm, input_norm = sb("slot_norm", [128, 1]), sb("input_norm", [128, 1])
        mean_col = sb("mean_col", [128, 1])
        each = lambda t, shape: [sb(f"{t}{u}", shape) for u in TWO]
        context = each("context", [KEYS, GROUP, DIM])
        square = each("square", [128, COLS])
        energy = each("energy", [128, GROUP])
        rms = each("rms", [128, GROUP])
        context_energy = each("context_energy", [KEYS, GROUP])
        context_rms = each("context_rms", [KEYS, GROUP])
        inverse = each("inverse", [128, GROUP])
        unit = each("unit", [KEYS, GROUP, DIM])
        unitT = each("unitT", [128, KCOLS])
        kT = each("kT", [128, KCOLS])
        v = each("v", [KEYS, GROUP, DIM + 1])
        xn = each("xn", [128, GROUP, DIM])
        h = each("h", [128, COLS])
        spread = each("spread", [128, COLS])
        qT = each("qT", [128, COLS])
        offset = each("offset", [KEYS, GROUP])
        powers = each("powers", [KEYS, COLS])
        total = each("total", [KEYS, GROUP])
        mixed = each("mixed", [128, GROUP, DIM])
        update = each("update", [128, COLS])
        half_hidden = each("half_hidden", [128, COLS])
        tanh_r, tanh_z = each("tanh_r", [128, COLS]), each("tanh_z", [128, COLS])
        new = each("new", [128, COLS])
        weights_in, consts, folded = sem("weights_in"), sem("consts"), sem("folded")
        context_in = [sem("context_in0"), sem("context_in1")]
        pair = lambda t: [sem(f"{t}{u}") for u in TWO]
        context_squared, context_shifted, context_rms_ready, unit_ready, unit_turned = (
            pair("context_squared"), pair("context_shifted"), pair("context_rms_ready"),
            pair("unit_ready"), pair("unit_turned"))
        unitT_ready, k_made, v_made, k_ready, v_ready = (
            pair("unitT_ready"), pair("k_made"), pair("v_made"), pair("k_ready"), pair("v_ready"))
        xn_ready, turned, out_turned = pair("xn_ready"), pair("turned"), pair("out_turned")
        h_ready, squared, squares_summed, energy_ready, rms_ready = (
            pair("h_ready"), pair("squared"), pair("squares_summed"), pair("energy_ready"),
            pair("rms_ready"))
        rms_spread, q_made, hidden_made, rms_taken, hidden_taken, q_ready = (
            pair("rms_spread"), pair("q_made"), pair("hidden_made"), pair("rms_taken"),
            pair("hidden_taken"), pair("q_ready"))
        scores_ready, offset_ready, powers_ready, shares_ready = (
            pair("scores_ready"), pair("offset_ready"), pair("powers_ready"),
            pair("shares_ready"))
        updates_made, mixed_ready, update_turned = (
            pair("updates_made"), pair("mixed_ready"), pair("update_turned"))
        update_ready, r_made, new_made, z_made, r_ready, z_ready, drive_ready, new_ready = (
            pair("update_ready"), pair("r_made"), pair("new_made"), pair("z_made"),
            pair("r_ready"), pair("z_ready"), pair("drive_ready"), pair("new_ready"))
        dve_step, ln = sem("dve_step"), NormSignals(sem)
        LOADS = [(w_q, "w_q"), (w_k, "w_k"), (w_v, "w_v"), (w_ih, "w_ih"), (w_hh, "w_hh"),
                 (b_ih, "b_ih"), (b_hh, "b_hh"), (slot_norm, "slot_norm"),
                 (input_norm, "input_norm")]
        seq = lambda j: slice(j * TOK, (j + 1) * TOK)
        count = lambda r, it: SLOT_ITERS * r + it + 1
        HS = SLOT_ITERS + 1
        R, Z, NEW = 0, 1, 2
        block = ctx.enter_context(nc.Block())

        def loop(engine, body):
            with engine.Fori(0, BLOCKS // 2 - 1) as r:
                body(r, True)
            body(BLOCKS // 2 - 1, False)

        def after(r, it, more):
            return (r, it + 1) if it + 1 < SLOT_ITERS else (r + 1, 0) if more else None

        @block.sync
        def _(sp):
            for dst, t in LOADS:
                sp.dma_start(dst[(slice(None),) * len(dst.shape)], d[f"slots_{t}"][
                    (slice(None),) * len(dst.shape)]).then_inc(weights_in, 16)

            def load(n, u):
                sp.dma_start(context[u][:, :, :], d["ctx"][:, chip.rows(n), :])\
                    .then_inc(context_in[u], 16)
            for u in TWO:
                load(u, u)
            with sp.Fori(0, BLOCKS // 2 - 1) as r:
                for u in TWO:
                    sp.wait_ge(unit_ready[u], r + 1)
                    load(2 * (r + 1) + u, u)

        @block.tensor
        def _(pe):
            def turn(r, u):
                pe.wait_ge(xn_ready[u], r + 1)
                for j in range(GROUP):
                    last = nc.tensor.transpose(bank[:, 4 * u + 1, seq(j)], xn[u][:, j, :],
                                               chip.ident[:, :])
                last.then_inc(turned[u], 1)

            def turn_context(r, u):
                pe.wait_ge(unit_ready[u], r + 1)
                for j in range(GROUP):
                    last = nc.tensor.transpose(bank[:, 4 * u + 2, j * KEYS:(j + 1) * KEYS],
                                               unit[u][:, j, :], chip.ident[0:KEYS, 0:KEYS])
                last.then_inc(unit_turned[u], 1)

            def keys(r, u):
                pe.wait_ge(unitT_ready[u], r + 1)
                nc.tensor.matmul(bank[:, 4 * u + 2, 0:KCOLS], w_k[:, :], unitT[u][:, :],
                                 start=True, stop=True).then_inc(k_made[u], 1)

            def values(r, u):
                pe.wait_ge(k_ready[u], r + 1)
                for j in range(GROUP):
                    last = nc.tensor.matmul(bank[0:KEYS, 4 * u + 2, seq(j)],
                                            unitT[u][:, j * KEYS:(j + 1) * KEYS], w_v[:, :],
                                            start=True, stop=True)
                last.then_inc(v_made[u], 1)

            def from_h(r, it, u):
                pe.wait_ge(squared[u], count(r, it))
                for j in range(GROUP):
                    last = nc.tensor.matmul(bank[:, 4 * u, j:j + 1], square[u][:, seq(j)],
                                            mean_col[:, :], start=True, stop=True)
                last.then_inc(squares_summed[u], 1)
                nc.tensor.matmul(bank[:, 4 * u + 1, :], w_q[:, :], h[u][:, :],
                                 start=True, stop=True).then_inc(q_made[u], 1)

            def hidden(r, it, u, first=False):
                if it == 0 and not first:
                    pe.wait_ge(ln.updated, 2 * r + u - 1)
                nc.tensor.matmul(bank[:, 4 * u + 3, :], w_hh[:, NEW, :], h[u][:, :],
                                 start=True, stop=True).then_inc(hidden_made[u], 1)

            def spread_rms(r, it, u):
                pe.wait_ge(rms_ready[u], count(r, it))
                for j in range(GROUP):
                    last = nc.tensor.matmul(bank[:, 4 * u, seq(j)],
                                            rms[u][:, j:j + 1].broadcast_to([128, 128]),
                                            chip.ident[:, :], start=True, stop=True)
                last.then_inc(rms_spread[u], 1)

            def scores(r, it, u):
                pe.wait_ge(q_ready[u], count(r, it))
                if it == 0:
                    pe.wait_ge(v_ready[u], r + 1)
                for j in range(GROUP):
                    last = nc.tensor.matmul(bank[0:KEYS, 4 * u + 2, seq(j)],
                                            kT[u][:, j * KEYS:(j + 1) * KEYS],
                                            qT[u][:, seq(j)], start=True, stop=True)
                last.then_inc(scores_ready[u], 1)

            def from_shares(r, it, u):
                pe.wait_ge(shares_ready[u], count(r, it))
                for j in range(GROUP):
                    at = DIM + 1 if j % 2 else 0
                    last = nc.tensor.matmul(bank[:, 4 * u + j // 2, at:at + DIM + 1],
                                            powers[u][:, seq(j)], v[u][:, j, :],
                                            start=True, stop=True)
                last.then_inc(updates_made[u], 1)
                nc.tensor.matmul(bank[:, 4 * u + 2, :], w_hh[:, R, :], h[u][:, :],
                                 start=True, stop=False)

            def turn_updates(r, it, u):
                pe.wait_ge(mixed_ready[u], count(r, it))
                for j in range(GROUP):
                    last = nc.tensor.transpose(bank[:, 4 * u + 1, seq(j)], mixed[u][:, j, :],
                                               chip.ident[:, :])
                last.then_inc(update_turned[u], 1)
                nc.tensor.matmul(bank[:, 4 * u, :], w_hh[:, Z, :], h[u][:, :],
                                 start=True, stop=False)

            def gates(r, it, u):
                pe.wait_ge(update_ready[u], count(r, it))
                nc.tensor.matmul(bank[:, 4 * u + 2, :], w_ih[:, R, :], update[u][:, :],
                                 start=False, stop=True).then_inc(r_made[u], 1)
                nc.tensor.matmul(bank[:, 4 * u + 1, :], w_ih[:, NEW, :], update[u][:, :],
                                 start=True, stop=True).then_inc(new_made[u], 1)
                nc.tensor.matmul(bank[:, 4 * u, :], w_ih[:, Z, :], update[u][:, :],
                                 start=False, stop=True).then_inc(z_made[u], 1)

            def turn_out(r, u):
                pe.wait_ge(h_ready[u], HS * (r + 1))
                for j in range(GROUP):
                    last = nc.tensor.transpose(bank[:, 4 * u + 3, seq(j)], h[u][:, seq(j)],
                                               chip.ident[:, :])
                last.then_inc(out_turned[u], 1)

            def start(u):
                turn(0, u)
                turn_context(0, u)
                keys(0, u)
                values(0, u)

            def body(r, more):
                for it in range(SLOT_ITERS):
                    then = after(r, it, more)
                    change = it == SLOT_ITERS - 1
                    from_h(r, it, 1)
                    hidden(r, it, 1)
                    spread_rms(r, it, 1)
                    if change:
                        turn_out(r, 0)
                        if more:
                            turn(r + 1, 0)
                            turn_context(r + 1, 0)
                    elif then:
                        from_h(*then, 0)
                    scores(r, it, 1)
                    if change and then:
                        keys(r + 1, 0)
                        from_h(*then, 0)
                        values(r + 1, 0)
                    if then:
                        spread_rms(*then, 0)
                        hidden(*then, 0)
                    from_shares(r, it, 1)
                    if then:
                        scores(*then, 0)
                    turn_updates(r, it, 1)
                    gates(r, it, 1)
                    if then:
                        from_shares(*then, 0)
                        turn_updates(*then, 0)
                        gates(*then, 0)
                turn_out(r, 1)
                if more:
                    turn(r + 1, 1)
                    turn_context(r + 1, 1)
                    keys(r + 1, 1)
                    values(r + 1, 1)

            pe.wait_ge(folded, 3)
            pe.wait_ge(consts, 3)
            start(0)
            from_h(0, 0, 0)
            hidden(0, 0, 0, True)
            start(1)
            spread_rms(0, 0, 0)
            scores(0, 0, 0)
            from_shares(0, 0, 0)
            turn_updates(0, 0, 0)
            gates(0, 0, 0)
            loop(pe, body)

        @block.scalar
        def _(act):
            def square_context(r, u):
                act.wait_ge(context_in[u], 16 * (r + 1))
                act.wait_ge(unit_turned[u], r)
                for j in range(GROUP):
                    last = nc.scalar.activation(unit[u][:, j, :], context[u][:, j, :],
                                                ACT.Square, scale=scale,
                                                accum_out=context_energy[u][:, j:j + 1])
                last.then_inc(context_squared[u], 1)

            def take_turned(r, u):
                act.wait_ge(turned[u], r + 1)
                nc.scalar.copy(h[u][:, :], bank[:, 4 * u + 1, :]).then_inc(h_ready[u], 1)

            def take_context(r, u):
                act.wait_ge(unit_turned[u], r + 1)
                nc.scalar.copy(unitT[u][:, :], bank[:, 4 * u + 2, 0:KCOLS])\
                    .then_inc(unitT_ready[u], 1)

            def take_keys(r, u):
                act.wait_ge(k_made[u], r + 1)
                nc.scalar.copy(kT[u][:, :], bank[:, 4 * u + 2, 0:KCOLS]).then_inc(k_ready[u], 1)

            def square_h(r, it, u):
                act.wait_ge(h_ready[u], HS * r + it + 1)
                nc.scalar.activation(square[u][:, :], h[u][:, :], ACT.Square)\
                    .then_inc(squared[u], 1)

            def take_rms(r, it, u):
                act.wait_ge(rms_spread[u], count(r, it))
                nc.scalar.copy(spread[u][:, :], bank[:, 4 * u, :]).then_inc(rms_taken[u], 1)

            def take_hidden(r, it, u):
                act.wait_ge(hidden_made[u], count(r, it))
                nc.scalar.activation(half_hidden[u][:, :], bank[:, 4 * u + 3, :], ACT.Identity,
                                     bias=half_b[:, NEW:NEW + 1],
                                     scale=0.5).then_inc(hidden_taken[u], 1)

            def exps(r, it, u):
                act.wait_ge(offset_ready[u], count(r, it))
                for j in range(GROUP):
                    last = nc.scalar.activation(
                        powers[u][:, seq(j)], bank[0:KEYS, 4 * u + 2, seq(j)], ACT.Exp,
                        bias=offset[u][:, j:j + 1], scale=scale, accum_out=total[u][:, j:j + 1])
                last.then_inc(powers_ready[u], 1)

            def take_updates(r, it, u):
                act.wait_ge(update_turned[u], count(r, it))
                nc.scalar.copy(update[u][:, :], bank[:, 4 * u + 1, :]).then_inc(update_ready[u], 1)

            def gate_tanhs(r, it, u):
                act.wait_ge(r_made[u], count(r, it))
                nc.scalar.activation(tanh_r[u][:, :], bank[:, 4 * u + 2, :], ACT.Tanh,
                                     bias=half_b[:, R:R + 1], scale=0.5).then_inc(r_ready[u], 1)
                act.wait_ge(z_made[u], count(r, it))
                nc.scalar.activation(tanh_z[u][:, :], bank[:, 4 * u, :], ACT.Tanh,
                                     bias=half_b[:, Z:Z + 1], scale=0.5).then_inc(z_ready[u], 1)

            def new_tanh(r, it, u):
                act.wait_ge(drive_ready[u], count(r, it))
                nc.scalar.activation(new[u][:, :], new[u][:, :], ACT.Tanh,
                                     bias=b_ih[:, NEW:NEW + 1]).then_inc(new_ready[u], 1)

            def body(r, more):
                for it in range(SLOT_ITERS):
                    then = after(r, it, more)
                    change = it == SLOT_ITERS - 1
                    gate_tanhs(r, it, 0)
                    new_tanh(r, it, 0)
                    take_rms(r, it, 1)
                    take_hidden(r, it, 1)
                    if change and then:
                        take_turned(r + 1, 0)
                        take_context(r + 1, 0)
                    if then:
                        square_h(*then, 0)
                    if change and then:
                        take_keys(r + 1, 0)
                    exps(r, it, 1)
                    if then:
                        take_rms(*then, 0)
                        take_hidden(*then, 0)
                    take_updates(r, it, 1)
                    if then:
                        exps(*then, 0)
                    gate_tanhs(r, it, 1)
                    new_tanh(r, it, 1)
                    if then:
                        take_updates(*then, 0)
                    if it == 0 and more:
                        square_context(r + 1, 0)
                        square_context(r + 1, 1)
                    if not change:
                        square_h(r, it + 1, 1)
                if more:
                    take_turned(r + 1, 1)
                    take_context(r + 1, 1)
                    square_h(r + 1, 0, 1)
                    take_keys(r + 1, 1)

            act.wait_ge(folded, 3)
            square_context(0, 0)
            square_context(0, 1)
            for u in TWO:
                take_turned(0, u)
                take_context(0, u)
                square_h(0, 0, u)
                take_keys(0, u)
            take_rms(0, 0, 0)
            take_hidden(0, 0, 0)
            exps(0, 0, 0)
            take_updates(0, 0, 0)
            loop(act, body)

        @block.vector
        def _(dve):
            OWN = 7
            done = [0]

            def step(r, instruction):
                instruction.then_inc(dve_step, 1)
                done[0] += 1
                dve.wait_ge(dve_step, 2 * SLOT_ITERS * OWN * r + done[0])

            def normalise(r, u):
                dve.wait_ge(turned[u], r)
                chip.normalise(2 * r + u, xn[u]).then_inc(xn_ready[u], 1)

            def scale_context(r, u):
                dve.wait_ge(context_rms_ready[u], r + 1)
                nc.vector.tensor_tensor(out=unit[u][:, :, :], in0=context[u][:, :, :],
                                        in1=bc(context_rms[u][:, :], 2, DIM),
                                        op=ALU.mult).then_inc(unit_ready[u], 1)

            def take_values(r, u):
                dve.wait_ge(v_made[u], r + 1)
                nc.vector.tensor_copy(v[u][:, :, 0:DIM],
                                      bank[0:KEYS, 4 * u + 2, :].rearrange(
                                          "p (b d) -> p b d", b=GROUP)).then_inc(v_ready[u], 1)

            def add_eps(r, it, u):
                dve.wait_ge(squares_summed[u], count(r, it))
                nc.vector.tensor_tensor(out=energy[u][:, :], in0=bank[:, 4 * u, 0:GROUP],
                                        in1=chip.rms_eps[:, :],
                                        op=ALU.add).then_inc(energy_ready[u], 1)

            def queries(r, it, u):
                dve.wait_ge(rms_taken[u], count(r, it))
                dve.wait_ge(q_made[u], count(r, it))
                nc.vector.tensor_tensor(out=qT[u][:, :], in0=bank[:, 4 * u + 1, :],
                                        in1=spread[u][:, :], op=ALU.mult).then_inc(q_ready[u], 1)

            def offsets(r, base, it, u):
                dve.wait_ge(scores_ready[u], count(r, it))
                step(base, nc.vector.tensor_reduce(
                    offset[u][:, :], bank[0:KEYS, 4 * u + 2, :].rearrange(
                        "p (b s) -> p b s", b=GROUP), AX.X, ALU.max))
                nc.vector.tensor_scalar(offset[u][:, :], offset[u][:, :], -scale, None,
                                        ALU.mult).then_inc(offset_ready[u], 1)

            def shares(r, base, it, u):
                dve.wait_ge(powers_ready[u], count(r, it))
                step(base, nc.vector.reciprocal(total[u][:, :], total[u][:, :]))
                by_seq = powers[u][:, :].rearrange("p (b s) -> p b s", b=GROUP)
                nc.vector.tensor_tensor(out=by_seq, in0=by_seq, in1=bc(total[u][:, :], 2, TOK),
                                        op=ALU.mult).then_inc(shares_ready[u], 1)

            def mix(r, base, it, u):
                dve.wait_ge(updates_made[u], count(r, it))
                raw = bank[:, 4 * u:4 * u + 2, 0:2 * (DIM + 1)].rearrange(
                    "p c (j d) -> p c j d", d=DIM + 1)
                by_bank = inverse[u][:, :].rearrange("p (c j) -> p c j", c=2)
                step(base, nc.vector.tensor_scalar(by_bank, raw[:, :, :, DIM], RMS_EPS, None,
                                                   ALU.add))
                step(base, nc.vector.reciprocal(inverse[u][:, :], inverse[u][:, :]))
                nc.vector.tensor_tensor(
                    out=mixed[u][:, :, :].rearrange("p (c j) d -> p c j d", c=2),
                    in0=raw[:, :, :, 0:DIM], in1=bc(by_bank, 3, DIM),
                    op=ALU.mult).then_inc(mixed_ready[u], 1)

            def drive(r, base, it, u):
                dve.wait_ge(r_ready[u], count(r, it))
                dve.wait_ge(hidden_taken[u], count(r, it))
                step(base, nc.vector.scalar_tensor_tensor(
                    out=new[u][:, :], in0=tanh_r[u][:, :], scalar=1.0,
                    in1=half_hidden[u][:, :], op0=ALU.add, op1=ALU.mult))
                dve.wait_ge(new_made[u], count(r, it))
                nc.vector.tensor_tensor(out=new[u][:, :], in0=new[u][:, :],
                                        in1=bank[:, 4 * u + 1, :],
                                        op=ALU.add).then_inc(drive_ready[u], 1)

            def next_h(r, base, it, u):
                dve.wait_ge(new_ready[u], count(r, it))
                step(base, nc.vector.tensor_tensor(out=h[u][:, :], in0=h[u][:, :],
                                                   in1=new[u][:, :], op=ALU.subtract))
                dve.wait_ge(z_ready[u], count(r, it))
                step(base, nc.vector.scalar_tensor_tensor(
                    out=h[u][:, :], in0=tanh_z[u][:, :], scalar=1.0, in1=h[u][:, :],
                    op0=ALU.add, op1=ALU.mult))
                nc.vector.scalar_tensor_tensor(
                    out=h[u][:, :], in0=h[u][:, :], scalar=0.5, in1=new[u][:, :],
                    op0=ALU.mult, op1=ALU.add).then_inc(h_ready[u], 1)

            def add(r, u):
                dve.wait_ge(out_turned[u], r + 1)
                chip.add_to_x(dve, 2 * r + u, bank[:, 4 * u + 3, :].rearrange(
                    "p (b d) -> p b d", b=GROUP), ln)

            FIRST = 4

            def body(r, more):
                done[0] = FIRST
                for it in range(SLOT_ITERS):
                    then = after(r, it, more)
                    change = it == SLOT_ITERS - 1
                    drive(r, r, it, 0)
                    add_eps(r, it, 1)
                    next_h(r, r, it, 0)
                    queries(r, it, 1)
                    if then and not change:
                        add_eps(*then, 0)
                    offsets(r, r, it, 1)
                    if then and change:
                        add_eps(*then, 0)
                        take_values(r + 1, 0)
                    if more and not change:
                        (normalise, scale_context)[it](r + 1, 1)
                    shares(r, r, it, 1)
                    if change:
                        add(r, 0)
                    if then:
                        queries(*then, 0)
                    mix(r, r, it, 1)
                    if more and not change:
                        (normalise, scale_context)[it](r + 1, 0)
                    if then:
                        offsets(then[0], r, then[1], 0)
                        shares(then[0], r, then[1], 0)
                    drive(r, r, it, 1)
                    if then:
                        mix(then[0], r, then[1], 0)
                    next_h(r, r, it, 1)
                add(r, 1)
                if more:
                    take_values(r + 1, 1)

            dve.wait_ge(weights_in, 16 * len(LOADS))
            nc.vector.tensor_scalar(w_q[:, :], w_q[:, :], slot_norm[:, 0:1], None, ALU.mult)
            nc.vector.tensor_scalar(w_k[:, :], w_k[:, :], input_norm[:, 0:1], None, ALU.mult)
            nc.vector.tensor_scalar(w_v[:, :], w_v[:, :], input_norm[:, 0:1], None, ALU.mult)\
                .then_inc(folded, 1)
            nc.vector.tensor_tensor(out=half_b[:, 0:2], in0=b_ih[:, 0:2], in1=b_hh[:, 0:2],
                                    op=ALU.add)
            nc.vector.tensor_scalar(half_b[:, 2:3], b_hh[:, 2:3], 0.5, None, ALU.mult)\
                .then_inc(folded, 1)
            dve.wait_ge(folded, 2)
            nc.vector.tensor_scalar(half_b[:, 0:2], half_b[:, 0:2], 0.5, None, ALU.mult)\
                .then_inc(folded, 1)
            for u in TWO:
                normalise(0, u)
                scale_context(0, u)
            take_values(0, 0)
            add_eps(0, 0, 0)
            take_values(0, 1)
            queries(0, 0, 0)
            offsets(0, 0, 0, 0)
            shares(0, 0, 0, 0)
            mix(0, 0, 0, 0)
            assert done[0] == FIRST
            loop(dve, body)

        @block.gpsimd
        def _(pool):
            chip.clear_last()
            def context_power(r, u):
                pool.wait_ge(context_squared[u], r + 1)
                nc.gpsimd.tensor_tensor(out=context_energy[u][:, :], in0=context_energy[u][:, :],
                                        in1=chip.rms_eps[0:KEYS, :],
                                        op=ALU.add).then_inc(context_shifted[u], 1)
                pool.wait_ge(context_shifted[u], r + 1)
                nc.gpsimd.tensor_tensor(out=context_rms[u][:, :], in0=context_energy[u][:, :],
                                        in1=chip.minus_half[0:KEYS, :],
                                        op=ALU.pow).then_inc(context_rms_ready[u], 1)

            def power(r, it, u):
                pool.wait_ge(energy_ready[u], count(r, it))
                nc.gpsimd.tensor_tensor(out=rms[u][:, :], in0=energy[u][:, :],
                                        in1=chip.minus_half[:, :],
                                        op=ALU.pow).then_inc(rms_ready[u], 1)

            def body(r, more):
                for it in range(SLOT_ITERS):
                    then = after(r, it, more)
                    power(r, it, 1)
                    if then:
                        power(*then, 0)
                    if it == SLOT_ITERS - 1:
                        chip.rstd_of(pool, 2 * r, ln)
                    if it == 0 and more:
                        context_power(r + 1, 0)
                        context_power(r + 1, 1)
                chip.rstd_of(pool, 2 * r + 1, ln)
            nc.gpsimd.memset(mean_col[:, :], 1.0 / DIM).then_inc(consts, 1)
            for u in TWO:
                nc.gpsimd.memset(v[u][:, :, DIM], 1.0).then_inc(consts, 1)
            context_power(0, 0)
            context_power(0, 1)
            power(0, 0, 0)
            loop(pool, body)


def context_attention(chip):
    nc, d, bank = chip.nc, chip.dram, chip.bank
    ctx, sb, sem = phase(chip, "x3")
    with ctx:
        scale = DIM ** -0.5
        ctxT = sb("ctxT", [128, 2, GROUP, KEYS])
        values = sb("values", [KEYS, 2, GROUP, DIM])
        mask = sb("mask", [128, 2, GROUP, KEYS])
        xn = sb("xn", [128, GROUP, DIM])
        xnT = sb("xnT", [128, 2, COLS])
        scaled = sb("scaled", [128, GROUP, KEYS])
        masks = sb("masks", [128, GROUP, KEYS], U32)
        largest = sb("largest", [128, GROUP])
        below = sb("below", [128, GROUP, KEYS])
        powers = sb("powers", [128, GROUP, KEYS])
        total = sb("total", [128, GROUP])
        share = sb("share", [128, GROUP, KEYS])
        number = sb("number", [128, GROUP, KEYS], U32)
        weight = sb("weight", [128, GROUP, KEYS])
        weightT = sb("weightT", [KEYS, COLS])
        loaded, xn_ready, turned, xnT_ready = (
            [sem("loaded0"), sem("loaded1")], sem("xn_ready"), sem("turned"), sem("xnT_ready"))
        scores_ready, step_done, below_ready, powers_ready = (
            sem("scores_ready"), sem("step_done"), sem("below_ready"), sem("powers_ready"))
        weight_turned, weightT_ready, summed, ln = (
            sem("weight_turned"), sem("weightT_ready"), sem("summed"), NormSignals(sem))
        TURN, SCORES, WEIGHTS, OUT = 0, 1, 3, 4
        STEPS = 11
        block = ctx.enter_context(nc.Block())

        @block.sync
        def _(sp):
            def load(n, u, r=None):
                rows = chip.rows(n)
                sp.dma_start(ctxT[:, u, :, :], d["ctxT"][:, rows, :]).then_inc(loaded[u], 16)
                sp.dma_start(values[:, u, :, :], d["ctx"][:, rows, :]).then_inc(loaded[u], 16)
                sp.dma_start(mask[:, u, :, :], d["x3_mask"][:, rows, :]).then_inc(loaded[u], 16)

            def body(n, u, more):
                if more:
                    sp.wait_ge(summed, n)
                    load(n + 1, 1 - u)
            load(0, 0)
            engine_loop_pairs(sp, body)

        def landed(engine, n, u):
            engine.wait_ge(loaded[u], 24 * (n - u) + 48)

        @block.tensor
        def _(pe):
            def turn(n):
                pe.wait_ge(xn_ready, n + 1)
                for j in range(GROUP):
                    last = nc.tensor.transpose(bank[:, TURN, j * TOK:(j + 1) * TOK], xn[:, j, :],
                                               chip.ident[:, :])
                last.then_inc(turned, 1)

            def scores(n, u):
                landed(pe, n, u)
                pe.wait_ge(xnT_ready, n + 1)
                for j in range(GROUP):
                    last = nc.tensor.matmul(bank[:, SCORES + u, j * KEYS:(j + 1) * KEYS],
                                            xnT[:, u, j * TOK:(j + 1) * TOK], ctxT[:, u, j, :],
                                            start=True, stop=True)
                last.then_inc(scores_ready, 1)

            def body(n, u, more):
                if more:
                    turn(n + 1)
                    scores(n + 1, 1 - u)
                pe.wait_ge(step_done, STEPS * (n + 1))
                for j in range(GROUP):
                    last = nc.tensor.transpose(bank[0:KEYS, WEIGHTS, j * TOK:(j + 1) * TOK],
                                               weight[:, j, :], chip.ident[:, :])
                last.then_inc(weight_turned, 1)
                pe.wait_ge(ln.updated, n)
                pe.wait_ge(weightT_ready, n + 1)
                for j in range(GROUP):
                    last = nc.tensor.matmul(bank[:, OUT, j * DIM:(j + 1) * DIM],
                                            weightT[:, j * TOK:(j + 1) * TOK], values[:, u, j, :],
                                            start=True, stop=True)
                last.then_inc(summed, 1)

            turn(0)
            scores(0, 0)
            engine_loop_pairs(pe, body)

        @block.scalar
        def _(act):
            def take_turned(n, u):
                act.wait_ge(turned, n + 1)
                nc.scalar.copy(xnT[:, u, :], bank[:, TURN, :]).then_inc(xnT_ready, 1)

            def body(n, u, more):
                if more:
                    take_turned(n + 1, 1 - u)
                act.wait_ge(below_ready, n + 1)
                nc.scalar.activation(powers[:, :, :].rearrange("p b k -> p (b k)"),
                                     below[:, :, :].rearrange("p b k -> p (b k)"), ACT.Exp)\
                    .then_inc(powers_ready, 1)
                act.wait_ge(weight_turned, n + 1)
                nc.scalar.copy(weightT[:, :], bank[0:KEYS, WEIGHTS, :]).then_inc(weightT_ready, 1)

            take_turned(0, 0)
            engine_loop_pairs(act, body)

        @block.vector
        def _(dve):
            def body(n, u, more):
                done = [0]

                def step(instruction):
                    instruction.then_inc(step_done, 1)
                    done[0] += 1
                    dve.wait_ge(step_done, STEPS * n + done[0])
                if more:
                    dve.wait_ge(turned, n + 1)
                    chip.normalise(n + 1, xn).then_inc(xn_ready, 1)
                landed(dve, n, u)
                dve.wait_ge(scores_ready, n + 1)
                step(nc.vector.tensor_scalar(
                    scaled[:, :, :], bank[:, SCORES + u, 0:KCOLS].rearrange(
                        "p (b k) -> p b k", b=GROUP), scale, None, ALU.mult))
                step(nc.vector.tensor_scalar(masks[:, :, :], mask[:, u, :, :], -1.0, None,
                                             ALU.is_lt))
                chip.settle()
                step(nc.vector.copy_predicated(scaled[:, :, :], masks[:, :, :], mask[:, u, :, :]))
                step(nc.vector.tensor_reduce(largest[:, :], scaled[:, :, :], AX.X, ALU.max))
                step(nc.vector.tensor_tensor(out=below[:, :, :], in0=scaled[:, :, :],
                                             in1=bc(largest[:, :], 2, KEYS), op=ALU.subtract))
                nc.vector.memset(weight[:, :, :], 0.0).then_inc(below_ready, 1)
                dve.wait_ge(powers_ready, n + 1)
                step(nc.vector.tensor_reduce(total[:, :], powers[:, :, :], AX.X, ALU.add))
                step(nc.vector.reciprocal(total[:, :], total[:, :]))
                step(nc.vector.tensor_tensor(out=share[:, :, :], in0=powers[:, :, :],
                                             in1=bc(total[:, :], 2, KEYS), op=ALU.mult))
                step(nc.vector.tensor_tensor(out=number[:, :, :], in0=share[:, :, :],
                                             in1=share[:, :, :], op=ALU.is_equal))
                dve.wait_ge(below_ready, n + 1)
                chip.settle()
                step(nc.vector.copy_predicated(weight[:, :, :], number[:, :, :], share[:, :, :]))
                step(nc.vector.memset(chip.carrier[:, :], 0.0))
                dve.wait_ge(summed, n + 1)
                chip.add_to_x(dve, n, bank[:, OUT, :].rearrange("p (b d) -> p b d", b=GROUP), ln)

            chip.normalise(0, xn).then_inc(xn_ready, 1)
            engine_loop_pairs(dve, body)

        @block.gpsimd
        def _(pool):
            chip.clear_last()
            def body(n, u, more):
                chip.rstd_of(pool, n, ln)
            engine_loop_pairs(pool, body)


def mix_ffn(chip):
    nc, d, bank = chip.nc, chip.dram, chip.bank
    ctx, sb, sem = phase(chip, "mix")
    with ctx:
        w_r, w_k, w_v = (sb(t, [128, DIM]) for t in ("w_r", "w_k", "w_v"))
        mu = sb("mu", [128, 2])
        one_less_mu = sb("one_less_mu", [128, 2])
        xn = sb("xn", [128, GROUP, DIM])
        padded = sb("padded", [128, 2, GROUP, TOK + 1])
        scaled = sb("scaled", [128, 2, GROUP, TOK])
        mixed = sb("mixed", [128, 2, GROUP, TOK])
        gate = sb("gate", [128, COLS])
        relu = sb("relu", [128, COLS])
        square = sb("square", [128, COLS])
        outT = sb("outT", [128, COLS])
        weights_in, xn_ready, turned, padded_ready = (
            sem("weights_in"), sem("xn_ready"), sem("turned"), sem("padded_ready"))
        mu_ready, cleared, scaled_ready, mixed_ready = (
            sem("mu_ready"), sem("cleared"), sem("scaled_ready"), sem("mixed_ready"))
        pre_ready, gate_ready, relu_ready, square_ready, value_ready, outT_ready, out_turned, updated = (
            sem("pre_ready"), sem("gate_ready"), sem("relu_ready"), sem("square_ready"),
            sem("value_ready"), sem("outT_ready"), sem("out_turned"), sem("updated"))
        stored = sem("stored")
        TURN, R, K, V, BACK = 0, 1, 2, 3, 4
        block = ctx.enter_context(nc.Block())

        @block.sync
        def _(sp):
            for dst, name in ((w_r, "mix_w_r"), (w_k, "mix_w_k"), (w_v, "mix_w_v"), (mu, "mix_mu")):
                sp.dma_start(dst[:, :], d[name][:, :]).then_inc(weights_in, 16)

            def body(n, u, more):
                sp.wait_ge(updated, n + 1)
                r = chip.rows(n)
                sp.dma_start(d["out"][r, :, :].rearrange("b t d -> t b d"), chip.x[:, r, :])\
                    .then_inc(stored, 16)
            engine_loop_pairs(sp, body)
            sp.wait_ge(stored, 16 * BLOCKS)

        @block.tensor
        def _(pe):
            def turn(n):
                pe.wait_ge(xn_ready, n + 1)
                for j in range(GROUP):
                    last = nc.tensor.transpose(bank[:, TURN, j * TOK:(j + 1) * TOK], xn[:, j, :],
                                               chip.ident[:, :])
                last.then_inc(turned, 1)

            def pre(n):
                for i, (w, at) in enumerate(((w_k, K), (w_r, R))):
                    if i:
                        pe.wait_ge(gate_ready, n)
                    pe.wait_ge(mixed_ready, 2 * n + i + 1)
                    nc.tensor.matmul(bank[:, at, :], w[:, :],
                                     mixed[:, i, :, :].rearrange("p b t -> p (b t)"),
                                     start=True, stop=True).then_inc(pre_ready, 1)

            def body(n, u, more):
                if more:
                    turn(n + 1)
                pe.wait_ge(square_ready, n + 1)
                nc.tensor.matmul(bank[:, V, :], w_v[:, :], square[:, :], start=True, stop=True)\
                    .then_inc(value_ready, 1)
                if more:
                    pre(n + 1)
                pe.wait_ge(outT_ready, n + 1)
                for j in range(GROUP):
                    last = nc.tensor.transpose(bank[:, BACK, j * TOK:(j + 1) * TOK],
                                               outT[:, j * TOK:(j + 1) * TOK], chip.ident[:, :])
                last.then_inc(out_turned, 1)

            pe.wait_ge(weights_in, 64)
            turn(0)
            pre(0)
            engine_loop_pairs(pe, body)

        @block.scalar
        def _(act):
            def take_turned(n, u):
                act.wait_ge(turned, n + 1)
                nc.scalar.copy(padded[:, u, :, 1:], bank[:, TURN, :].rearrange(
                    "p (b t) -> p b t", b=GROUP)).then_inc(padded_ready, 1)

            def body(n, u, more):
                if more:
                    take_turned(n + 1, 1 - u)
                act.wait_ge(pre_ready, 2 * n + 1)
                nc.scalar.activation(relu[:, :], bank[:, K, :], ACT.Relu).then_inc(relu_ready, 1)
                act.wait_ge(pre_ready, 2 * n + 2)
                act.wait_ge(outT_ready, n)
                nc.scalar.activation(gate[:, :], bank[:, R, :], ACT.Sigmoid).then_inc(gate_ready, 1)

            act.wait_ge(cleared, 1)
            take_turned(0, 0)
            engine_loop_pairs(act, body)

        @block.vector
        def _(dve):
            def mix(n, u):
                dve.wait_ge(padded_ready, n + 1)
                for i in range(2):
                    at = 1 - i
                    nc.vector.tensor_scalar(scaled[:, i, :, :], padded[:, u, :, 1:],
                                            mu[:, at:at + 1], None, ALU.mult)\
                        .then_inc(scaled_ready, 1)
                for i in range(2):
                    at = 1 - i
                    dve.wait_ge(scaled_ready, 2 * n + i + 1)
                    nc.vector.scalar_tensor_tensor(
                        out=mixed[:, i, :, :], in0=padded[:, u, :, 0:TOK],
                        scalar=one_less_mu[:, at:at + 1], in1=scaled[:, i, :, :],
                        op0=ALU.mult, op1=ALU.add).then_inc(mixed_ready, 1)

            def body(n, u, more):
                if more:
                    dve.wait_ge(pre_ready, 2 * n + 2)
                    mix(n + 1, 1 - u)
                dve.wait_ge(gate_ready, n + 1)
                dve.wait_ge(value_ready, n + 1)
                nc.vector.tensor_tensor(out=outT[:, :], in0=gate[:, :], in1=bank[:, V, :],
                                        op=ALU.mult).then_inc(outT_ready, 1)
                dve.wait_ge(out_turned, n + 1)
                r = chip.rows(n)
                nc.vector.tensor_tensor(out=chip.x[:, r, :], in1=chip.x[:, r, :],
                                        in0=bank[:, BACK, :].rearrange("p (b d) -> p b d", b=GROUP),
                                        op=ALU.add).then_inc(updated, 1)

            dve.wait_ge(weights_in, 64)
            nc.vector.tensor_scalar(one_less_mu[:, :], mu[:, :], -1.0, 1.0, ALU.mult, ALU.add)\
                .then_inc(mu_ready, 1)
            chip.normalise(0, xn).then_inc(xn_ready, 1)
            dve.wait_ge(mu_ready, 1)
            mix(0, 0)

            def whole(n, u, more):
                if more:
                    dve.wait_ge(turned, n + 1)
                    chip.normalise(n + 1, xn).then_inc(xn_ready, 1)
                body(n, u, more)
            engine_loop_pairs(dve, whole)

        @block.gpsimd
        def _(pool):
            chip.clear_last()
            nc.gpsimd.memset(padded[:, :, :, 0], 0.0).then_inc(cleared, 1)

            def body(n, u, more):
                pool.wait_ge(relu_ready, n + 1)
                nc.gpsimd.tensor_tensor(out=square[:, :], in0=relu[:, :], in1=relu[:, :],
                                        op=ALU.mult).then_inc(square_ready, 1)
            engine_loop_pairs(pool, body)


def store_stream(chip):
    nc, d = chip.nc, chip.dram
    ctx, sb, sem = phase(chip, "store")
    with ctx:
        stored = sem("stored")
        block = ctx.enter_context(nc.Block())

        @block.sync
        def _(sp):
            sp.dma_start(d["out"].rearrange("b t d -> t b d"), chip.x[:, :, :]).then_inc(stored, 16)
            sp.wait_ge(stored, 16)


PHASES = ["x0", "tree", "x1", "moe", "slots", "gated", "x3", "mix"]


def build(nc, dram):
    with ExitStack() as top:
        chip = Chip(nc, top, dram)
        load_stream(chip)
        fns = {"x0": lambda c: heads_attention(c, "x0", False),
               "x1": lambda c: heads_attention(c, "x1", True), "x3": context_attention, "slots": slot_attention,
               "tree": tree_ffn, "moe": moe_ffn, "gated": gated_ffn, "mix": mix_ffn}
        for p in PHASES:
            fns[p](chip)
        if PHASES[-1] != "mix":
            store_stream(chip)


def ancestor_matrix():
    a = np.zeros((128, NODES), np.float32)
    rights = np.zeros(NODES, np.float32)
    for node in range(1, NODES):
        m = node
        while m:
            up = (m - 1) // 2
            right = m == 2 * up + 2
            a[up, node] = 1.0 if right else -1.0
            rights[node] += right
            m = up
    return a, rights


def layouts(inputs):
    g = {k: np.ascontiguousarray(v) for k, v in inputs.items()}
    t = lambda name: np.ascontiguousarray(g[name].T)
    rows = lambda a: np.ascontiguousarray(np.broadcast_to(a, (128,) + a.shape))
    bf16 = mybir.dt.np(BF16)
    out = {"x": g["x"], "ident": np.eye(128, dtype=np.float32)}

    out["tree_w_in"] = t("L0_ffn_W_in")
    two = np.zeros((TREES, 256) + (DIM,), np.float32)
    two[:, :NODES] = g["L0_ffn_W_out"].T.reshape(TREES, NODES, DIM)
    out["tree_w_out"] = np.ascontiguousarray(two.reshape(TREES, 2, 128, DIM).transpose(2, 0, 1, 3))
    b = np.zeros((TREES, 256), np.float32)
    b[:, :NODES] = g["L0_ffn_b_in"].reshape(TREES, NODES)
    out["tree_b_in"] = np.ascontiguousarray(b.reshape(TREES, 2, 128).transpose(2, 0, 1))
    a, rights = ancestor_matrix()
    out["tree_ancestors"] = a.astype(bf16)
    r = np.zeros(256, np.float32)
    r[:NODES] = rights
    out["tree_target"] = np.ascontiguousarray(r.reshape(2, 128).T)

    for name, at, upper in (("x0", "L0_xattn", True), ("x1", "L1_xattn", False)):
        for p in "qkvo":
            w = f"{at}_W{p}" if upper else f"{at}_w{p}"
            out[f"{name}_w_{p}"] = t(w)
        out[f"{name}_b_q"], out[f"{name}_b_k"] = g[f"{at}_bq"][:, None], g[f"{at}_bk"][:, None]
        out[f"{name}_b_v"] = rows(g[f"{at}_bv"])[:KEYS]
        out[f"{name}_b_o"] = g[f"{at}_bo"][None, :]
    part = np.arange(128)[:, None]
    out["own_head"] = (part // HEAD_DIM == np.arange(HEADS)).astype(np.float32)
    out["ctxT"] = np.ascontiguousarray(g["ctx_1024"].transpose(2, 0, 1))
    out["ctx"] = np.ascontiguousarray(g["ctx_1024"].transpose(1, 0, 2))
    out["mask"] = np.ascontiguousarray(g["mask_Bx1xSxS2_ik1"][:, 0].transpose(1, 0, 2))
    out["x3_mask"] = np.ascontiguousarray(g["mask_BxSxS2_fk0"].transpose(1, 0, 2))

    out["moe_w_route"] = t("L1_ffn_Wg")
    out["moe_bias"] = rows(g["L1_ffn_bias_corr"])
    up = g["L1_ffn_W1"].reshape(MOE_CHUNKS, 128, DIM)
    up = np.concatenate([up, g["L1_ffn_Ws1"][None]])
    out["moe_w_up"] = np.ascontiguousarray(up.transpose(2, 0, 1))
    down = g["L1_ffn_W2"].transpose(0, 2, 1).reshape(MOE_CHUNKS, 128, DIM)
    down = np.concatenate([down, g["L1_ffn_Ws2"].T[None]])
    out["moe_w_down"] = np.ascontiguousarray(down.transpose(1, 0, 2))
    e = np.arange(EXPERTS)[:, None]
    owner = (np.arange(MOE_CHUNKS * 128) // EXP_HID)[None, :]
    out["moe_spread"] = np.tile(e == owner, (3, 1)).reshape(3 * EXPERTS, MOE_CHUNKS, 128).astype(bf16)
    for size, dt in ((EXP_GROUPS, np.float32), (GATED, bf16), (EXPERTS, bf16)):
        out[f"earlier{size}"] = rows(np.tril(np.ones((size, size), np.float32), -1).astype(dt))

    for p in "qkv":
        out[f"slots_w_{p}"] = t(f"L2_xattn_W{p}")
    for p in ("ih", "hh"):
        w = g[f"L2_xattn_gru_w{p}"].reshape(3, DIM, DIM)
        out[f"slots_w_{p}"] = np.ascontiguousarray(w.transpose(2, 0, 1))
        out[f"slots_b_{p}"] = np.ascontiguousarray(g[f"L2_xattn_gru_b{p}"].reshape(3, DIM).T)
    out["slots_slot_norm"] = g["L2_xattn_slot_norm_w"][:, None]
    out["slots_input_norm"] = g["L2_xattn_input_norm_w"][:, None]

    out["gated_w_gate"] = t("L2_ffn_gate_w")
    out["gated_b_gate"] = rows(g["L2_ffn_gate_b"])
    out["gated_w"] = np.ascontiguousarray(g["L2_ffn_expert_w"].transpose(1, 0, 2))
    out["gated_b"] = np.tile(g["L2_ffn_expert_b"], (3, 1))
    out["gated_spread"] = np.broadcast_to(np.tile(np.eye(GATED), (3, 1))[:, :, None],
                                          (3 * GATED, GATED, 128)).astype(bf16)

    out["mix_w_r"], out["mix_w_k"], out["mix_w_v"] = t("L3_ffn_W_r"), t("L3_ffn_W_k"), t("L3_ffn_W_v")
    out["mix_mu"] = np.stack([g["L3_ffn_mu_r"], g["L3_ffn_mu_k"]], axis=1)
    return out


def kernel(**inputs):
    import concourse.bacc as bacc
    from concourse.bass_utils import run_bass_kernel_spmd

    arrays = layouts(inputs)
    nc = bacc.Bacc("TRN2", target_bir_lowering=False, num_devices=1)
    dram = {k: nc.dram_tensor(f"in_{k}", v.shape, mybir.dt.from_np(v.dtype), kind="ExternalInput").ap()
            for k, v in arrays.items()}
    dram["out"] = nc.dram_tensor("out", (SEQS, TOK, DIM), F32, kind="ExternalOutput").ap()
    build(nc, dram)
    r = run_bass_kernel_spmd(nc, [{f"in_{k}": v for k, v in arrays.items()}], core_ids=[0])
    return r.results[0]["out"]
```

```python
from contextlib import ExitStack

import numpy as np

import concourse.bass as bass
from concourse import mybir

F32 = mybir.dt.float32
BF16 = mybir.dt.bfloat16
I32 = mybir.dt.int32
U32 = mybir.dt.uint32
ALU = mybir.AluOpType
ACT = mybir.ActivationFunctionType
AX = mybir.AxisListType

SEQS, TOK, DIM, KEYS = 32, 128, 128, 77
GROUP = 4
BLOCKS = SEQS // GROUP
COLS = GROUP * TOK
KCOLS = GROUP * KEYS
LN_EPS = 1e-5
PAIR = 2 * DIM

TREES, DEPTH = 8, 7
NODES = 2 ** (DEPTH + 1) - 1
INNER = 2 ** DEPTH - 1
CHUNK = (128, NODES - 128)

EXPERTS, EXP_HID, EXP_GROUPS, TOP_GROUPS, TOP_EXPERTS, ROUTE_SCALE = 16, 64, 4, 2, 4, 2.5
PER_GROUP = EXPERTS // EXP_GROUPS
MOE_CHUNKS = EXPERTS * EXP_HID // 128
GATED, TOP_GATED = 8, 2

HEADS = 16
HEAD_DIM = DIM // HEADS
QUAD = 4
SPAN = 96
CLIP = 100.0
SLOT_ITERS, RMS_EPS = 3, 1e-6


def engine_loop(engine, body):
    with engine.Fori(0, BLOCKS - 1) as n:
        body(n, True)
    body(BLOCKS - 1, False)


def bc(ap, at, size):
    a = ap.unsqueeze(at)
    shape = list(a.shape)
    shape[at] = size
    return a.broadcast_to(shape)


class Chip:

    def __init__(self, nc, top, dram):
        self.nc, self.dram = nc, dram
        sb = lambda name, shape, dt=F32: top.enter_context(nc.sbuf_tensor(name, shape, dt))
        self.x = sb("x_res", [128, SEQS, DIM])
        self.mean_var = sb("mean_var", [128, SEQS, 2])
        self.rstd = sb("rstd", [128, SEQS])
        self.stats = sb("stats", [128, GROUP, 6])
        self.block_stats = sb("block_stats", [128, GROUP, 2])
        self.shifted_var = sb("shifted_var", [128, GROUP])
        self.carrier = sb("carrier", [128, 1])
        self.consts_set = top.enter_context(nc.semaphore("consts_set"))
        self.bank = top.enter_context(nc.psum_tensor("bank", [128, 8, 512], F32))
        self.weights = {name: Weights(nc, top, dram, name, arrays)
                        for name, arrays in WEIGHTS.items()}
        self.semaphores, self.to_clear = [], []
        self.ident = sb("ident", [128, 128])
        self.ident16 = sb("ident16", [128, 128], BF16)
        self.ln_eps = sb("ln_eps", [128, GROUP])
        self.rms_eps = sb("rms_eps", [128, GROUP])
        self.minus_half = sb("minus_half", [128, GROUP])
        self.act_carrier = sb("act_carrier", [128, 1])
        self.heads = HeadsBuffers(nc, top)

    def load_table(self, function):
        self.nc.scalar.activation(self.act_carrier[:, :], self.ln_eps[:, 0:1], function)

    def clear_last(self):
        for old in self.to_clear:
            self.nc.gpsimd.sem_clear(old)

    def rows(self, n):
        return bass.ds(n * GROUP, GROUP)

    def normalise(self, n, xn):
        for j in range(GROUP):
            b = n * GROUP + j
            last = self.nc.vector.tensor_scalar(
                xn[:, j, :], self.x[:, bass.ds(b, 1), :].rearrange("p a d -> p (a d)"),
                self.mean_var[:, bass.ds(b, 1), 0], self.rstd[:, bass.ds(b, 1)],
                ALU.subtract, ALU.mult)
        return last

    def add_to_x(self, dve, n, added, ln):
        nc, r = self.nc, self.rows(n)
        nc.vector.tensor_tensor(out=self.x[:, r, :], in0=added, in1=self.x[:, r, :],
                                op=ALU.add).then_inc(ln.updated, 1)
        dve.wait_ge(ln.updated, n + 1)
        self.settle()
        self.statistics(dve, n, lambda j: self.x[:, bass.ds(n * GROUP + j, 1), :]
                        .rearrange("p a d -> p (a d)"), ln)

    def settle(self):
        self.nc.vector.memset(self.carrier[:, :], 0.0)

    def statistics(self, dve, n, seq, ln):
        nc = self.nc
        for j in range(GROUP):
            last = nc.vector.bn_stats(self.stats[:, j, :], seq(j))
        last.then_inc(ln.stats_ready, 1)
        dve.wait_ge(ln.shifted, n)
        dve.wait_ge(ln.stats_ready, n + 1)
        self.settle()
        for j in range(GROUP):
            last = nc.vector.bn_aggr(self.block_stats[:, j, :], self.stats[:, j, :])
        last.then_inc(ln.merged, 1)
        dve.wait_ge(ln.merged, n + 1)
        nc.vector.tensor_scalar(self.mean_var[:, self.rows(n), :], self.block_stats[:, :, :],
                                1.0, None, ALU.mult).then_inc(ln.var_ready, 1)

    def rstd_of(self, pool, n, ln):
        nc = self.nc
        pool.wait_ge(ln.rstd_ready, n)
        pool.wait_ge(ln.var_ready, n + 1)
        nc.gpsimd.tensor_tensor(out=self.shifted_var[:, :], in0=self.block_stats[:, :, 1],
                                in1=self.ln_eps[:, :], op=ALU.add).then_inc(ln.shifted, 1)
        pool.wait_ge(ln.shifted, n + 1)
        nc.gpsimd.tensor_tensor(out=self.rstd[:, self.rows(n)], in0=self.shifted_var[:, :],
                                in1=self.minus_half[:, :], op=ALU.pow).then_inc(ln.rstd_ready, 1)


class Weights:

    def __init__(self, nc, top, dram, name, arrays):
        self.loads = []
        for key, array in arrays.items():
            src = dram[array]
            tile = top.enter_context(nc.sbuf_tensor(f"{name}_{key}", list(src.shape), src.dtype))
            self.loads.append((tile, src))
        self.keys = list(arrays)
        self.loaded = top.enter_context(nc.semaphore(f"{name}_weights_in"))
        self.all = 16 * len(arrays)

    def load(self, sp):
        for tile, src in self.loads:
            whole = (slice(None),) * len(src.shape)
            sp.dma_start(tile[whole], src[whole]).then_inc(self.loaded, 16)

    def tiles(self, *keys):
        return [self.loads[self.keys.index(k)][0] for k in keys]


def heads_weights(name):
    own = {k: f"{name}_{k}" for k in ("w_q", "w_k", "w_v", "w_o", "b_q", "b_k", "b_v", "b_o")}
    return own | {"own_head": "own_head"}


WEIGHTS = {
    "x0": heads_weights("x0"),
    "tree": {k: f"tree_{k}" for k in ("w_in", "b_in", "ancestors", "target", "w_out")},
    "x1": heads_weights("x1"),
    "moe": {"w_route": "moe_w_route", "bias": "moe_bias", "w_up": "moe_w_up",
            "w_down": "moe_w_down", "spread": "moe_spread", "earlier_group": "earlier4",
            "earlier_expert": "earlier16"},
    "slots": {k: f"slots_{k}" for k in ("w_q", "w_k", "w_v", "w_ih", "w_hh", "b_ih", "b_hh",
                                        "slot_norm", "input_norm")},
    "gated": {"w_gate": "gated_w_gate", "b_gate": "gated_b_gate", "w_expert": "gated_w",
              "b_expert": "gated_b", "spread": "gated_spread", "earlier": "earlier8"},
    "mix": {k: f"mix_{k}" for k in ("w_r", "w_k", "w_v", "mu")},
}


class HeadsBuffers:

    CHUNKS = QUAD * SPAN // 128
    WIDTH = QUAD * (HEAD_DIM + 1)
    PIECES = [(0, 0, 0, 96), (0, 1, 96, 128), (1, 1, 0, 64), (1, 2, 64, 128),
              (2, 2, 0, 32), (2, 3, 32, 64), (2, 3, 64, 128)]

    def __init__(self, nc, top):
        sb = lambda name, shape, dt=F32: top.enter_context(nc.sbuf_tensor(name, shape, dt))
        self.ones = sb("head_ones", [1, TOK])
        self.ctxT = sb("head_ctxT", [128, GROUP, 2, SPAN])
        self.mask = sb("head_mask", [128, GROUP, KEYS], I32)
        self.v = sb("head_v", [128, 2, GROUP, HEADS // QUAD, self.CHUNKS, self.WIDTH])
        self.powers = sb("head_powers", [128, 2, HEADS // 2, SPAN])
        self.filled = top.enter_context(nc.semaphore("heads_filled"))
        self.first_in = {name: top.enter_context(nc.semaphore(f"{name}_first_in"))
                         for name in ("x0", "x1")}

    def fill(self, nc, pool):
        zeros = [self.ctxT[:, :, :, KEYS:SPAN], self.powers[:, :, :, KEYS:SPAN]]
        zeros += [self.v[:, u, :, :, :, :].rearrange("p b g c w -> p (b g c w)") for u in range(2)]
        columns = [self.v[lo:hi, u, :, :, c, h * (HEAD_DIM + 1) + HEAD_DIM]
                   for c, h, lo, hi in self.PIECES for u in range(2)]
        fills = [(part, 0.0) for part in zeros] + [(part, 1.0) for part in columns]
        for i, (part, value) in enumerate(fills + [(self.ones[:, :], 1.0)]):
            if i:
                pool.wait_ge(self.filled, i)
            nc.gpsimd.memset(part, value).then_inc(self.filled, 1)

    def load(self, sp, dram, rows, masked, ctx_in, mask_in):
        for copy in range(2):
            sp.dma_start(self.ctxT[:, :, copy, 0:KEYS], dram["ctxT"][:, rows, :])\
                .then_inc(ctx_in, 16)
        if masked:
            sp.dma_start(self.mask[:, :, :], dram["mask"][:, rows, :]).then_inc(mask_in, 16)

    def load_first(self, sp, dram, name):
        masked, arrived = name == "x1", self.first_in[name]
        self.load(sp, dram, slice(0, GROUP), masked, arrived, arrived)


class NormSignals:

    def __init__(self, sem):
        self.updated = sem("updated")
        self.stats_ready = sem("stats_ready")
        self.merged = sem("merged")
        self.var_ready = sem("var_ready")
        self.shifted = sem("shifted")
        self.rstd_ready = sem("rstd_ready")


def phase(chip, name):
    ctx, nc = ExitStack(), chip.nc
    chip.to_clear, own = chip.semaphores, []
    chip.semaphores = own

    def sb(t, shape, dt=F32):
        return ctx.enter_context(nc.sbuf_tensor(f"{name}_{t}", shape, dt))

    def sem(t):
        own.append(ctx.enter_context(nc.semaphore(f"{name}_{t}")))
        return own[-1]
    return ctx, sb, sem


def load_stream(chip):
    nc, d = chip.nc, chip.dram
    ctx, sb, sem = phase(chip, "load")
    with ctx:
        halves = sb("halves", [128, SEQS, 6])
        shifted = sb("shifted", [128, SEQS])
        x_in = [sem(f"x_in{i}") for i in range(BLOCKS)]
        const_in = sem("const_in")
        measured, merged, var_shifted = sem("measured"), sem("merged"), sem("var_shifted")
        block = ctx.enter_context(nc.Block())

        @block.sync
        def _(sp):
            for n in range(BLOCKS):
                r = slice(n * GROUP, (n + 1) * GROUP)
                sp.dma_start(chip.x[:, r, :], d["x"][r, :, :].rearrange("b t d -> t b d"))\
                    .then_inc(x_in[n], 16)
            sp.dma_start(chip.ident[:, :], d["ident"][:, :]).then_inc(const_in, 16)
            chip.heads.load_first(sp, d, "x0")
            chip.weights["x0"].load(sp)

        @block.scalar
        def _(act):
            act.wait_ge(chip.consts_set, 3)
            chip.load_table(ACT.Exp)

        @block.vector
        def _(dve):
            for n in range(BLOCKS + 1):
                if n < BLOCKS:
                    dve.wait_ge(x_in[n], 16)
                    for b in range(n * GROUP, (n + 1) * GROUP):
                        last = nc.vector.bn_stats(halves[:, b, :], chip.x[:, b, :])
                    last.then_inc(measured, 1)
                if n:
                    dve.wait_ge(measured, n)
                    if n > 1:
                        dve.wait_ge(merged, n - 1)
                    chip.settle()
                    for b in range((n - 1) * GROUP, n * GROUP):
                        last = nc.vector.bn_aggr(chip.mean_var[:, b, :], halves[:, b, :])
                    last.then_inc(merged, 1)
            dve.wait_ge(const_in, 16)
            nc.vector.tensor_copy(chip.ident16[:, :], chip.ident[:, :])

        @block.gpsimd
        def _(pool):
            chip.clear_last()
            nc.gpsimd.memset(chip.ln_eps[:, :], LN_EPS).then_inc(chip.consts_set, 1)
            nc.gpsimd.memset(chip.rms_eps[:, :], RMS_EPS).then_inc(chip.consts_set, 1)
            nc.gpsimd.memset(chip.minus_half[:, :], -0.5).then_inc(chip.consts_set, 1)
            chip.heads.fill(nc, pool)
            pool.wait_ge(chip.consts_set, 3)
            by_block = lambda a: a.rearrange("p (n b) -> p n b", b=GROUP)
            parts = ((0, BLOCKS // 2), (BLOCKS // 2, BLOCKS - 2), (BLOCKS - 2, BLOCKS))
            for i, (first, end) in enumerate(parts):
                s = slice(first * GROUP, end * GROUP)
                pool.wait_ge(merged, end)
                nc.gpsimd.tensor_tensor(out=by_block(shifted[:, s]),
                                        in0=by_block(chip.mean_var[:, s, 1]),
                                        in1=bc(chip.ln_eps[:, :], 1, end - first),
                                        op=ALU.add).then_inc(var_shifted, 1)
                pool.wait_ge(var_shifted, i + 1)
                nc.gpsimd.tensor_tensor(out=by_block(chip.rstd[:, s]), in0=by_block(shifted[:, s]),
                                        in1=bc(chip.minus_half[:, :], 1, end - first),
                                        op=ALU.pow)


def tree_ffn(chip):
    nc, d, bank = chip.nc, chip.dram, chip.bank
    ctx, sb, sem = phase(chip, "tree")
    with ctx:
        w = chip.weights["tree"]
        w_in, b_in, w_out, ancestors, target = w.tiles("w_in", "b_in", "w_out", "ancestors",
                                                       "target")
        xn = sb("xn", [128, GROUP, DIM])
        xnT = sb("xnT", [128, COLS])
        decide = sb("decide", [128, 2, COLS], BF16)
        act_of = sb("act_of", [128, 4, COLS])
        masked = sb("masked", [128, 4, COLS])
        outT = sb("outT", [128, COLS])
        xn_ready, turned, xnT_ready = (
            sem("xn_ready"), sem("turned"), sem("xnT_ready"))
        logits_ready, decided, act_ready, counted, masked_ready, product_done = (
            sem("logits_ready"), sem("decided"), sem("act_ready"), sem("counted"),
            sem("masked_ready"), sem("product_done"))
        outT_ready, out_turned, ln = sem("outT_ready"), sem("out_turned"), NormSignals(sem)
        TURN, OUT, IN, COUNT = 0, 1, 2, 6
        PER = 2 * TREES
        block = ctx.enter_context(nc.Block())

        @block.sync
        def _(sp):
            chip.heads.load_first(sp, d, "x1")

        @block.tensor
        def _(pe):
            def turn(n):
                pe.wait_ge(xn_ready, n + 1)
                for j in range(GROUP):
                    last = nc.tensor.transpose(bank[:, TURN, j * TOK:(j + 1) * TOK], xn[:, j, :],
                                               chip.ident[:, :])
                last.then_inc(turned, 1)

            def logits(n, k):
                t, c = divmod(k, 2)
                m = CHUNK[c]
                if k >= 4:
                    pe.wait_ge(act_ready, PER * n + k - 3)
                nc.tensor.matmul(bank[0:m, IN + k % 4, :],
                                 w_in[:, t * NODES + 128 * c:t * NODES + 128 * c + m], xnT[:, :],
                                 start=True, stop=True).then_inc(logits_ready, 1)

            def count(n, t):
                pe.wait_ge(decided, TREES * n + t + 1)
                for c in range(2):
                    if t:
                        pe.wait_ge(masked_ready, PER * n + 2 * t + c - 1)
                    nc.tensor.matmul(bank[0:CHUNK[c], COUNT + c, :],
                                     ancestors[0:INNER, 128 * c:128 * c + CHUNK[c]],
                                     decide[0:INNER, t % 2, :],
                                     start=True, stop=True).then_inc(counted, 1)

            def product(n, t):
                for c in range(2):
                    k = 2 * t + c
                    pe.wait_ge(masked_ready, PER * n + k + 1)
                    nc.tensor.matmul(bank[:, OUT, :], w_out[0:CHUNK[c], t, c, :],
                                     masked[0:CHUNK[c], k % 4, :],
                                     start=(k == 0), stop=(k == PER - 1)).then_inc(product_done, 1)

            def first_logits(n):
                pe.wait_ge(xnT_ready, n + 1)
                logits(n, 0)
                logits(n, 1)

            def body(n, more):
                for t in range(TREES):
                    if t < TREES - 1:
                        logits(n, 2 * t + 2)
                        logits(n, 2 * t + 3)
                    elif more:
                        turn(n + 1)
                    count(n, t)
                    if t:
                        product(n, t - 1)
                product(n, TREES - 1)
                if more:
                    first_logits(n + 1)
                pe.wait_ge(outT_ready, n + 1)
                for j in range(GROUP):
                    last = nc.tensor.transpose(bank[:, TURN, j * TOK:(j + 1) * TOK],
                                               outT[:, j * TOK:(j + 1) * TOK], chip.ident[:, :])
                last.then_inc(out_turned, 1)

            pe.wait_ge(w.loaded, w.all)
            turn(0)
            first_logits(0)
            engine_loop(pe, body)

        @block.scalar
        def _(act):
            def silu(n, k):
                t, c = divmod(k, 2)
                m = CHUNK[c]
                if c == 0:
                    act.wait_ge(decided, TREES * n + t + 1)
                else:
                    act.wait_ge(logits_ready, PER * n + k + 1)
                if k >= 4:
                    act.wait_ge(masked_ready, PER * n + k - 3)
                nc.scalar.activation(act_of[0:m, k % 4, :], bank[0:m, IN + k % 4, :], ACT.Silu,
                                     bias=b_in[0:m, t, c:c + 1]).then_inc(act_ready, 1)

            def take_turned(n):
                act.wait_ge(turned, n + 1)
                nc.scalar.copy(xnT[:, :], bank[:, TURN, :]).then_inc(xnT_ready, 1)

            def body(n, more):
                for k in range(2, PER):
                    silu(n, k)
                if more:
                    take_turned(n + 1)
                act.wait_ge(product_done, PER * (n + 1))
                nc.scalar.copy(outT[:, :], bank[:, OUT, :]).then_inc(outT_ready, 1)
                if more:
                    silu(n + 1, 0)
                    silu(n + 1, 1)

            chip.load_table(ACT.Silu)
            act.wait_ge(w.loaded, w.all)
            take_turned(0)
            silu(0, 0)
            silu(0, 1)
            engine_loop(act, body)

        @block.vector
        def _(dve):
            def decisions(n, t):
                dve.wait_ge(logits_ready, PER * n + 2 * t + 1)
                if t >= 2:
                    dve.wait_ge(counted, PER * n + 2 * t - 2)
                nc.vector.tensor_scalar(decide[:, t % 2, :], bank[:, IN + (2 * t) % 4, :],
                                        b_in[:, t, 0:1], 0.0, ALU.add, ALU.is_gt)\
                    .then_inc(decided, 1)

            def mask(n, k):
                t, c = divmod(k, 2)
                m = CHUNK[c]
                dve.wait_ge(counted, PER * n + k + 1)
                dve.wait_ge(act_ready, PER * n + k + 1)
                if k >= 4:
                    dve.wait_ge(product_done, PER * n + k - 3)
                nc.vector.scalar_tensor_tensor(
                    out=masked[0:m, k % 4, :], in0=bank[0:m, COUNT + c, :],
                    scalar=target[0:m, c:c + 1], in1=act_of[0:m, k % 4, :],
                    op0=ALU.is_equal, op1=ALU.mult).then_inc(masked_ready, 1)

            def body(n, more):
                for t in range(TREES):
                    if t < TREES - 1:
                        decisions(n, t + 1)
                    mask(n, 2 * t)
                    mask(n, 2 * t + 1)
                    if t == TREES // 2 and more:
                        chip.normalise(n + 1, xn).then_inc(xn_ready, 1)
                if more:
                    decisions(n + 1, 0)
                dve.wait_ge(out_turned, n + 1)
                chip.add_to_x(dve, n, bank[:, TURN, :].rearrange("p (b d) -> p b d", b=GROUP),
                              ln)

            dve.wait_ge(w.loaded, w.all)
            chip.normalise(0, xn).then_inc(xn_ready, 1)
            decisions(0, 0)
            engine_loop(dve, body)

        @block.gpsimd
        def _(pool):
            chip.clear_last()

            def body(n, more):
                chip.rstd_of(pool, n, ln)
            engine_loop(pool, body)


def engine_loop_pairs(engine, body):
    with engine.Fori(0, BLOCKS // 2 - 1) as r:
        body(2 * r, 0, True)
        body(2 * r + 1, 1, True)
    body(BLOCKS - 2, 0, True)
    body(BLOCKS - 1, 1, False)


def engine_loop_ahead(engine, body):
    with engine.Fori(0, BLOCKS // 2 - 1) as r:
        body(2 * r, 0, True, True)
        body(2 * r + 1, 1, True, True)
    body(BLOCKS - 2, 0, True, False)
    body(BLOCKS - 1, 1, False, False)


def compare(nc, size, sc, step, larger, equal_or_larger):
    other, own = bc(sc, 2, size), bc(sc, 3, size)
    step(nc.vector.tensor_tensor(out=larger, in0=other, in1=own, op=ALU.is_gt))
    step(nc.vector.tensor_tensor(out=equal_or_larger, in0=other, in1=own, op=ALU.is_ge))


def join_ties(nc, step, larger, equal_or_larger, earlier):
    step(nc.vector.tensor_tensor(out=equal_or_larger, in0=equal_or_larger, in1=bc(earlier, 1, GROUP),
                                 op=ALU.mult))
    step(nc.vector.tensor_tensor(out=larger, in0=larger, in1=equal_or_larger, op=ALU.max))


def count_wins(nc, step, larger, rank):
    step(nc.vector.tensor_reduce(rank, larger, AX.X, ALU.add))


def moe_ffn(chip):
    nc, d, bank = chip.nc, chip.dram, chip.bank
    ctx, sb, sem = phase(chip, "moe")
    with ctx:
        E, G, C = EXPERTS, EXP_GROUPS, MOE_CHUNKS + 1
        w = chip.weights["moe"]
        w_route, bias, w_up, w_down, spread, earlier_group, earlier_expert = w.tiles(
            "w_route", "bias", "w_up", "w_down", "spread", "earlier_group", "earlier_expert")
        xn = sb("xn", [128, GROUP, DIM])
        xnT = sb("xnT", [128, 2, COLS])
        score = sb("score", [128, 2, GROUP, E])
        choice = sb("choice", [128, GROUP, E])
        pair_sum = sb("pair_sum", [128, GROUP * G, 6])
        group_score = sb("group_score", [128, GROUP, G])
        group_larger = sb("group_larger", [128, GROUP, G, G])
        group_equal = sb("group_equal", [128, GROUP, G, G])
        group_rank = sb("group_rank", [128, GROUP, G])
        allowed = sb("allowed", [128, GROUP, E])
        larger = sb("larger", [128, GROUP, E, E], BF16)
        equal = sb("equal", [128, GROUP, E, E], BF16)
        rank = sb("rank", [128, GROUP, E])
        chosen = sb("chosen", [128, GROUP, E])
        total = sb("total", [128, GROUP])
        weight = sb("weight", [128, GROUP, E])
        rest = sb("rest", [128, GROUP, E])
        parts = sb("parts", [128, GROUP, 128], BF16)
        partsT = sb("partsT", [3 * E, 2, COLS], BF16)
        relu = sb("relu", [128, 2, COLS])
        square = sb("square", [128, 3, COLS])
        hidden = sb("hidden", [128, 4, COLS])
        outT = sb("outT", [128, COLS])
        xn_ready, turned, xnT_ready = (
            sem("xn_ready"), sem("turned"), sem("xnT_ready"))
        routed, scores_ready, step_done, parts_turned, partsT_ready = (
            sem("routed"), sem("scores_ready"), sem("step_done"), sem("parts_turned"),
            sem("partsT_ready"))
        up_ready, relu_ready, square_ready, spread_ready, hidden_ready, product_done = (
            sem("up_ready"), sem("relu_ready"), sem("square_ready"), sem("spread_ready"),
            sem("hidden_ready"), sem("product_done"))
        cleared = sem("cleared")
        outT_ready, out_turned, ln = sem("outT_ready"), sem("out_turned"), NormSignals(sem)
        TURN, OUT, UP, SPREAD, PARTS, LEAD = 0, 1, 2, 4, 7, 3
        STEPS, BY_GROUPS = 26, 11
        partsT_bank = bank[:, PARTS, :].bitcast(BF16)
        block = ctx.enter_context(nc.Block())

        @block.tensor
        def _(pe):
            def turn(n):
                pe.wait_ge(xn_ready, n + 1)
                for j in range(GROUP):
                    last = nc.tensor.transpose(bank[:, TURN, j * TOK:(j + 1) * TOK], xn[:, j, :],
                                               chip.ident[:, :])
                last.then_inc(turned, 1)

            def route(n, u):
                pe.wait_ge(xnT_ready, n + 1)
                for j in range(GROUP):
                    last = nc.tensor.matmul(bank[:, TURN, j * E:(j + 1) * E],
                                            xnT[:, u, j * TOK:(j + 1) * TOK], w_route[:, :],
                                            start=True, stop=True)
                last.then_inc(routed, 1)

            def turn_parts(n):
                pe.wait_ge(step_done, STEPS * (n + 1))
                for j in range(GROUP):
                    last = nc.tensor.transpose(partsT_bank[:, j * TOK:(j + 1) * TOK], parts[:, j, :],
                                               chip.ident16[:, :])
                last.then_inc(parts_turned, 1)

            def up(n, u, k, first=False):
                if not first:
                    pe.wait_ge(relu_ready, C * n + k - 1)
                nc.tensor.matmul(bank[:, UP + (k + u) % 2, :], w_up[:, k, :], xnT[:, u, :],
                                 start=True, stop=True).then_inc(up_ready, 1)

            def spread_weights(n, u, k):
                if k >= MOE_CHUNKS:
                    return
                if k >= 3:
                    pe.wait_ge(hidden_ready, MOE_CHUNKS * n + k - 2)
                if k == 0:
                    pe.wait_ge(partsT_ready, n + 1)
                nc.tensor.matmul(bank[:, SPREAD + k % 3, :], spread[:, k, :], partsT[:, u, :],
                                 start=True, stop=True).then_inc(spread_ready, 1)

            def product(n, k):
                if k < MOE_CHUNKS:
                    pe.wait_ge(hidden_ready, MOE_CHUNKS * n + k + 1)
                    units, slot = hidden, k % 4
                else:
                    pe.wait_ge(square_ready, C * n + k + 1)
                    units, slot = square, k % 3
                nc.tensor.matmul(bank[:, OUT, :], w_down[:, k, :], units[:, slot, :],
                                 start=(k == 0), stop=(k == C - 1)).then_inc(product_done, 1)

            def body(n, u, more, more2):
                for k in range(C):
                    if k + LEAD < C:
                        up(n, u, k + LEAD)
                        spread_weights(n, u, k + LEAD)
                    elif more:
                        if more2 and k == C - 3:
                            turn(n + 2)
                        elif more2 and k == C - 2:
                            route(n + 2, u)
                        elif k == C - 1:
                            turn_parts(n + 1)
                        up(n + 1, 1 - u, k + LEAD - C)
                    product(n, k)
                if more:
                    for k in range(LEAD):
                        spread_weights(n + 1, 1 - u, k)
                pe.wait_ge(outT_ready, n + 1)
                for j in range(GROUP):
                    last = nc.tensor.transpose(bank[:, TURN, j * TOK:(j + 1) * TOK],
                                               outT[:, j * TOK:(j + 1) * TOK], chip.ident[:, :])
                last.then_inc(out_turned, 1)

            pe.wait_ge(w.loaded, w.all)
            turn(0)
            route(0, 0)
            up(0, 0, 0, True)
            up(0, 0, 1, True)
            pe.wait_ge(scores_ready, 1)
            turn(1)
            route(1, 1)
            up(0, 0, 2)
            turn_parts(0)
            for k in range(LEAD):
                spread_weights(0, 0, k)
            engine_loop_ahead(pe, body)

        @block.scalar
        def _(act):
            def take_turned(n, u):
                act.wait_ge(turned, n + 1)
                nc.scalar.copy(xnT[:, u, :], bank[:, TURN, :]).then_inc(xnT_ready, 1)

            def scores(n, u):
                act.wait_ge(routed, n + 1)
                nc.scalar.activation(score[:, u, :, :].rearrange("p b e -> p (b e)"),
                                     bank[:, TURN, 0:GROUP * E], ACT.Sigmoid)\
                    .then_inc(scores_ready, 1)

            def take_parts(n, u):
                act.wait_ge(parts_turned, n + 1)
                nc.scalar.copy(partsT[:, u, :], partsT_bank[0:3 * E, 0:COLS])\
                    .then_inc(partsT_ready, 1)

            def rectify(n, u, k, first=False):
                act.wait_ge(up_ready, C * n + k + 1)
                if not first or k:
                    act.wait_ge(square_ready, C * n + k)
                nc.scalar.activation(relu[:, k % 2, :], bank[:, UP + (k + u) % 2, :], ACT.Relu)\
                    .then_inc(relu_ready, 1)
                act.wait_ge(relu_ready, C * n + k + 1)
                if k == 2 and not first:
                    act.wait_ge(product_done, C * n)
                elif not first:
                    act.wait_ge(hidden_ready, MOE_CHUNKS * n + (k - 2 if k > 2 else k - 1))
                nc.scalar.activation(square[:, k % 3, :], relu[:, k % 2, :], ACT.Square)\
                    .then_inc(square_ready, 1)

            def body(n, u, more, more2):
                for k in range(LEAD, C):
                    rectify(n, u, k)
                if more2:
                    take_turned(n + 2, u)
                if more:
                    rectify(n + 1, 1 - u, 0)
                if more2:
                    scores(n + 2, u)
                if more:
                    rectify(n + 1, 1 - u, 1)
                    take_parts(n + 1, 1 - u)
                act.wait_ge(product_done, C * (n + 1))
                nc.scalar.copy(outT[:, :], bank[:, OUT, :]).then_inc(outT_ready, 1)
                if more:
                    rectify(n + 1, 1 - u, 2)

            chip.load_table(ACT.Sigmoid)
            take_turned(0, 0)
            scores(0, 0)
            rectify(0, 0, 0, True)
            rectify(0, 0, 1, True)
            take_turned(1, 1)
            scores(1, 1)
            take_parts(0, 0)
            rectify(0, 0, 2, True)
            engine_loop_ahead(act, body)

        @block.vector
        def _(dve):
            def routing(n, u, done_before=0):
                done = [done_before]

                def step(instruction):
                    instruction.then_inc(step_done, 1)
                    done[0] += 1
                    dve.wait_ge(step_done, STEPS * n + done[0])
                quads = lambda t: t[:, :, :].rearrange("p b (g e) -> p (b g) e", e=PER_GROUP)
                flat = lambda t: t[:, :, :].rearrange("p b g -> p (b g)")

                def group_sums():
                    dve.wait_ge(scores_ready, n + 1)
                    step(nc.vector.tensor_tensor(out=choice[:, :, :], in0=score[:, u, :, :],
                                                 in1=bc(bias[:, :], 1, GROUP), op=ALU.add))
                    c, at = quads(choice), 0
                    for apart in range(1, PER_GROUP):
                        size = PER_GROUP - apart
                        add = nc.vector.tensor_tensor(out=pair_sum[:, :, at:at + size],
                                                      in0=c[:, :, 0:size], in1=c[:, :, apart:],
                                                      op=ALU.add)
                        at += size
                        step(add)
                    step(nc.vector.tensor_reduce(flat(group_score), pair_sum[:, :, :], AX.X, ALU.max))

                def group_ranks():
                    compare(nc, G, group_score[:, :, :], step, group_larger[:, :, :, :],
                            group_equal[:, :, :, :])
                    join_ties(nc, step, group_larger[:, :, :, :], group_equal[:, :, :, :],
                              earlier_group[:, :, :])
                    count_wins(nc, step, group_larger[:, :, :, :], group_rank[:, :, :])

                def allow():
                    step(nc.vector.scalar_tensor_tensor(
                        out=quads(allowed), in0=bc(flat(group_rank), 2, PER_GROUP),
                        scalar=float(TOP_GROUPS), in1=quads(choice), op0=ALU.is_lt, op1=ALU.mult))

                def compare_experts():
                    compare(nc, E, allowed[:, :, :], step, larger[:, :, :, :],
                            equal[:, :, :, :])

                def join_expert_ties():
                    join_ties(nc, step, larger[:, :, :, :], equal[:, :, :, :],
                              earlier_expert[:, :, :])

                def count_expert_wins():
                    count_wins(nc, step, larger[:, :, :, :], rank[:, :, :])

                def weigh():
                    step(nc.vector.scalar_tensor_tensor(
                        out=chosen[:, :, :], in0=rank[:, :, :], scalar=float(TOP_EXPERTS),
                        in1=score[:, u, :, :], op0=ALU.is_lt, op1=ALU.mult))
                    step(nc.vector.tensor_reduce(total[:, :], chosen[:, :, :], AX.X, ALU.add))
                    step(nc.vector.tensor_scalar(total[:, :], total[:, :], 1e-20, None, ALU.add))
                    step(nc.vector.reciprocal(total[:, :], total[:, :]))
                    step(nc.vector.scalar_tensor_tensor(
                        out=weight[:, :, :], in0=chosen[:, :, :], scalar=ROUTE_SCALE,
                        in1=bc(total[:, :], 2, E), op0=ALU.mult, op1=ALU.mult))

                def split():
                    bf16_parts(nc, step, weight[:, :, :], rest[:, :, :],
                               [parts[:, :, i * E:(i + 1) * E] for i in range(3)])
                return (group_sums, group_ranks, allow, compare_experts, join_expert_ties,
                        count_expert_wins, weigh, split)

            def by_groups(n, u):
                group_sums, group_ranks, allow, *_ = routing(n, u)
                group_sums()
                group_ranks()
                allow()

            def weigh_hidden(n, k, first=False):
                dve.wait_ge(square_ready, C * n + k + 1)
                dve.wait_ge(spread_ready, MOE_CHUNKS * n + k + 1)
                if not first and k != 3:
                    dve.wait_ge(product_done, C * n + (k - 3 if k > 3 else k - 4))
                nc.vector.tensor_tensor(out=hidden[:, k % 4, :], in0=square[:, k % 3, :],
                                        in1=bank[:, SPREAD + k % 3, :], op=ALU.mult)\
                    .then_inc(hidden_ready, 1)

            def body(n, u, more, more2):
                if more:
                    *_, compare_experts, join_expert_ties, count_expert_wins, weigh, split = (
                        routing(n + 1, 1 - u, BY_GROUPS))
                weigh_hidden(n, 3)
                if more2:
                    dve.wait_ge(turned, n + 2)
                    chip.normalise(n + 2, xn).then_inc(xn_ready, 1)
                weigh_hidden(n, 4)
                if more:
                    compare_experts()
                weigh_hidden(n, 5)
                if more:
                    join_expert_ties()
                weigh_hidden(n, 6)
                if more:
                    count_expert_wins()
                    weigh()
                weigh_hidden(n, 7)
                if more:
                    split()
                if more2:
                    by_groups(n + 2, u)
                if more:
                    for k in range(LEAD):
                        weigh_hidden(n + 1, k)
                dve.wait_ge(out_turned, n + 1)
                chip.add_to_x(dve, n, bank[:, TURN, :].rearrange("p (b d) -> p b d", b=GROUP), ln)

            dve.wait_ge(w.loaded, w.all)
            nc.vector.memset(parts[:, :, :], 0.0).then_inc(cleared, 1)
            dve.wait_ge(cleared, 1)
            chip.normalise(0, xn).then_inc(xn_ready, 1)
            dve.wait_ge(turned, 1)
            chip.normalise(1, xn).then_inc(xn_ready, 1)
            for piece in routing(0, 0):
                piece()
            by_groups(1, 1)
            for k in range(LEAD):
                weigh_hidden(0, k, True)
            engine_loop_ahead(dve, body)

        @block.gpsimd
        def _(pool):
            chip.clear_last()

            def body(n, u, more, more2):
                chip.rstd_of(pool, n, ln)
            engine_loop_ahead(pool, body)


def bf16_parts(nc, step, value, rest, parts):
    step(nc.vector.tensor_copy(parts[0], value))
    step(nc.vector.tensor_tensor(out=rest, in0=value, in1=parts[0], op=ALU.subtract))
    step(nc.vector.tensor_copy(parts[1], rest))
    step(nc.vector.tensor_tensor(out=rest, in0=rest, in1=parts[1], op=ALU.subtract))
    step(nc.vector.tensor_copy(parts[2], rest))


def gated_ffn(chip):
    nc, d, bank = chip.nc, chip.dram, chip.bank
    ctx, sb, sem = phase(chip, "gated")
    with ctx:
        E, BUFFERS = GATED, 4
        w = chip.weights["gated"]
        w_gate, b_gate, w_expert, b_expert, spread, earlier = w.tiles(
            "w_gate", "b_gate", "w_expert", "b_expert", "spread", "earlier")
        xn = sb("xn", [128, GROUP, DIM])
        xnT = sb("xnT", [128, 2, COLS])
        logit = sb("logit", [128, GROUP, E])
        larger = sb("larger", [128, GROUP, E, E], BF16)
        equal = sb("equal", [128, GROUP, E, E], BF16)
        rank = sb("rank", [128, GROUP, E])
        best = sb("best", [128, GROUP])
        shifted = sb("shifted", [128, GROUP, E])
        power = sb("power", [128, GROUP, E])
        kept = sb("kept", [128, GROUP, E])
        total = sb("total", [128, GROUP])
        gate = sb("gate", [128, GROUP, E])
        rest = sb("rest", [128, GROUP, E])
        parts = sb("parts", [128, GROUP, 3, E], BF16)
        partsT = sb("partsT", [3 * E, 2, COLS], BF16)
        partsT32 = sb("partsT32", [3 * E, 2, COLS])
        gated = sb("gated", [128, BUFFERS, COLS])
        outT = sb("outT", [128, COLS])
        xn_ready, turned, xnT_ready = (
            sem("xn_ready"), sem("turned"), sem("xnT_ready"))
        routed, shift_ready, power_ready, step_done, parts_turned, partsT_ready = (
            sem("routed"), sem("shift_ready"), sem("power_ready"), sem("step_done"),
            sem("parts_turned"), sem("partsT_ready"))
        partsT32_ready = sem("partsT32_ready")
        spread_ready, gated_ready, product_done = (
            sem("spread_ready"), sem("gated_ready"), sem("product_done"))
        outT_ready, out_turned, ln = sem("outT_ready"), sem("out_turned"), NormSignals(sem)
        TURN, ROUTE, OUT, SPREAD, PARTS = 0, 1, 2, 3, 7
        SPREADS = 4
        partsT_bank = bank[:, PARTS, :].bitcast(BF16)
        STEPS = 17
        block = ctx.enter_context(nc.Block())

        @block.tensor
        def _(pe):
            def turn(n):
                pe.wait_ge(xn_ready, n + 1)
                for j in range(GROUP):
                    last = nc.tensor.transpose(bank[:, TURN, j * TOK:(j + 1) * TOK], xn[:, j, :],
                                               chip.ident[:, :])
                last.then_inc(turned, 1)

            def route(n, u):
                pe.wait_ge(xnT_ready, n + 1)
                for j in range(GROUP):
                    last = nc.tensor.matmul(bank[:, ROUTE, j * E:(j + 1) * E],
                                            xnT[:, u, j * TOK:(j + 1) * TOK], w_gate[:, :],
                                            start=True, stop=True)
                last.then_inc(routed, 1)

            def turn_parts(n):
                pe.wait_ge(step_done, STEPS * (n + 1))
                for j in range(GROUP):
                    last = nc.tensor.transpose(partsT_bank[0:3 * E, j * TOK:(j + 1) * TOK],
                                               parts[:, j, :, :].rearrange("p a e -> p (a e)"),
                                               chip.ident16[:, :])
                last.then_inc(parts_turned, 1)

            def spread_gate(n, u, k, first=False):
                if k == 0:
                    pe.wait_ge(partsT_ready, n + 1)
                if not first:
                    pe.wait_ge(gated_ready, E * n + k - SPREADS + 1)
                nc.tensor.matmul(bank[:, SPREAD + k % SPREADS, :], spread[:, k, :], partsT[:, u, :],
                                 start=True, stop=True).then_inc(spread_ready, 1)

            def product(n, k):
                pe.wait_ge(gated_ready, E * n + k + 1)
                nc.tensor.matmul(bank[:, OUT, :], w_expert[:, k, :], gated[:, k % BUFFERS, :],
                                 start=False, stop=(k == E - 1)).then_inc(product_done, 1)

            def body(n, u, more, more2):
                pe.wait_ge(partsT32_ready, n + 1)
                nc.tensor.matmul(bank[:, OUT, :], b_expert[:, :], partsT32[:, u, :],
                                 start=True, stop=False)
                for k in range(E):
                    if k == 1 and more:
                        pe.wait_ge(ln.updated, n)
                        route(n + 1, 1 - u)
                    if k + 3 < E:
                        spread_gate(n, u, k + 3, k == 0)
                    if k == E - 1 and more:
                        turn_parts(n + 1)
                    product(n, k)
                if more:
                    for k in range(3):
                        spread_gate(n + 1, 1 - u, k)
                if more2:
                    turn(n + 2)
                pe.wait_ge(outT_ready, n + 1)
                for j in range(GROUP):
                    last = nc.tensor.transpose(bank[:, ROUTE, j * TOK:(j + 1) * TOK],
                                               outT[:, j * TOK:(j + 1) * TOK], chip.ident[:, :])
                last.then_inc(out_turned, 1)

            pe.wait_ge(w.loaded, w.all)
            turn(0)
            route(0, 0)
            turn(1)
            turn_parts(0)
            for k in range(3):
                spread_gate(0, 0, k, True)
            engine_loop_ahead(pe, body)

        @block.scalar
        def _(act):
            def take_turned(n, u, first=False):
                act.wait_ge(turned, n + 1)
                if not first:
                    act.wait_ge(gated_ready, E * (n - 1))
                nc.scalar.copy(xnT[:, u, :], bank[:, TURN, :]).then_inc(xnT_ready, 1)

            def exps(n):
                act.wait_ge(shift_ready, n + 1)
                nc.scalar.activation(power[:, :, :].rearrange("p b e -> p (b e)"),
                                     shifted[:, :, :].rearrange("p b e -> p (b e)"), ACT.Exp)\
                    .then_inc(power_ready, 1)

            def take_parts(n, u):
                act.wait_ge(parts_turned, n + 1)
                nc.scalar.copy(partsT[:, u, :], partsT_bank[0:3 * E, 0:COLS])\
                    .then_inc(partsT_ready, 1)

            def widen_parts(n, u):
                act.wait_ge(partsT_ready, n + 1)
                nc.scalar.copy(partsT32[:, u, :], partsT[:, u, :]).then_inc(partsT32_ready, 1)

            def body(n, u, more, more2):
                if more:
                    exps(n + 1)
                    take_parts(n + 1, 1 - u)
                act.wait_ge(product_done, E * (n + 1))
                nc.scalar.copy(outT[:, :], bank[:, OUT, :]).then_inc(outT_ready, 1)
                if more:
                    widen_parts(n + 1, 1 - u)
                if more2:
                    take_turned(n + 2, u)

            take_turned(0, 0, True)
            exps(0)
            take_turned(1, 1, True)
            take_parts(0, 0)
            widen_parts(0, 0)
            engine_loop_ahead(act, body)

        @block.vector
        def _(dve):
            def gates(n):
                done = [0]

                def step(instruction):
                    instruction.then_inc(step_done, 1)
                    done[0] += 1
                    dve.wait_ge(step_done, STEPS * n + done[0])

                def logits():
                    dve.wait_ge(routed, n + 1)
                    step(nc.vector.tensor_tensor(
                        out=logit[:, :, :],
                        in0=bank[:, ROUTE, 0:GROUP * E].rearrange("p (b e) -> p b e", e=E),
                        in1=bc(b_gate[:, :], 1, GROUP), op=ALU.add))
                    step(nc.vector.tensor_reduce(best[:, :], logit[:, :, :], AX.X, ALU.max))
                    step(nc.vector.tensor_tensor(out=shifted[:, :, :], in0=logit[:, :, :],
                                                 in1=bc(best[:, :], 2, E), op=ALU.subtract))
                    nc.vector.memset(chip.carrier[:, :], 0.0).then_inc(shift_ready, 1)

                def ranks():
                    compare(nc, E, logit[:, :, :], step, larger[:, :, :, :], equal[:, :, :, :])
                    join_ties(nc, step, larger[:, :, :, :], equal[:, :, :, :], earlier[:, :, :])
                    count_wins(nc, step, larger[:, :, :, :], rank[:, :, :])

                def mix():
                    dve.wait_ge(power_ready, n + 1)
                    step(nc.vector.scalar_tensor_tensor(
                        out=kept[:, :, :], in0=rank[:, :, :], scalar=float(TOP_GATED),
                        in1=power[:, :, :], op0=ALU.is_lt, op1=ALU.mult))
                    step(nc.vector.tensor_reduce(total[:, :], kept[:, :, :], AX.X, ALU.add))
                    step(nc.vector.reciprocal(total[:, :], total[:, :]))
                    step(nc.vector.tensor_tensor(out=gate[:, :, :], in0=kept[:, :, :],
                                                 in1=bc(total[:, :], 2, E), op=ALU.mult))

                def split():
                    bf16_parts(nc, step, gate[:, :, :], rest[:, :, :],
                               [parts[:, :, i, :] for i in range(3)])
                return [logits, ranks, mix, split]

            def times_gate(n, u, k, first=False):
                dve.wait_ge(spread_ready, E * n + k + 1)
                if not first:
                    dve.wait_ge(product_done, E * n + k - BUFFERS + 1)
                nc.vector.tensor_tensor(out=gated[:, k % BUFFERS, :], in0=xnT[:, u, :],
                                        in1=bank[:, SPREAD + k % SPREADS, :], op=ALU.mult)\
                    .then_inc(gated_ready, 1)

            def body(n, u, more, more2):
                if more:
                    logits, ranks, mix, split = gates(n + 1)
                times_gate(n, u, 3, True)
                if more:
                    logits()
                times_gate(n, u, 4)
                if more:
                    ranks()
                times_gate(n, u, 5)
                if more:
                    mix()
                times_gate(n, u, 6)
                if more:
                    split()
                times_gate(n, u, 7)
                if more2:
                    dve.wait_ge(turned, n + 2)
                    chip.normalise(n + 2, xn).then_inc(xn_ready, 1)
                if more:
                    for k in range(3):
                        times_gate(n + 1, 1 - u, k)
                dve.wait_ge(out_turned, n + 1)
                chip.add_to_x(dve, n, bank[:, ROUTE, :].rearrange("p (b d) -> p b d", b=GROUP), ln)

            dve.wait_ge(w.loaded, w.all)
            chip.normalise(0, xn).then_inc(xn_ready, 1)
            for piece in gates(0):
                piece()
            dve.wait_ge(turned, 1)
            chip.normalise(1, xn).then_inc(xn_ready, 1)
            for k in range(3):
                times_gate(0, 0, k, True)
            engine_loop_ahead(dve, body)

        @block.gpsimd
        def _(pool):
            chip.clear_last()

            def body(n, more):
                chip.rstd_of(pool, n, ln)
            engine_loop(pool, body)


def heads_attention(chip, name, clipped):
    nc, d, bank = chip.nc, chip.dram, chip.bank
    ctx, sb, sem = phase(chip, name)
    with ctx:
        QUARTERS = HEADS // QUAD
        shared = chip.heads
        CHUNKS, WIDTH, PIECES = shared.CHUNKS, shared.WIDTH, shared.PIECES
        ones, ctxT, mask, v, powers = (shared.ones, shared.ctxT, shared.mask, shared.v,
                                       shared.powers)
        first_in = shared.first_in[name]
        HALF = HEADS // 2
        UNITS = 2 * GROUP
        scale = HEAD_DIM ** -0.5
        w = chip.weights[name]
        w_q, w_k, w_v, w_o, b_q, b_k, b_v, b_o, own_head = w.tiles(
            "w_q", "w_k", "w_v", "w_o", "b_q", "b_k", "b_v", "b_o", "own_head")
        xn = sb("xn", [128, GROUP, DIM])
        xnT = sb("xnT", [128, COLS])
        qT = sb("qT", [128, COLS])
        kT = sb("kT", [128, GROUP, KEYS])
        own_kT = sb("own_kT", [128, 2, HEADS, KEYS])
        largest = sb("largest", [128, 2, HALF])
        below = sb("below", [128, 2, HALF, KEYS])
        powersT = sb("powersT", [128, QUARTERS, CHUNKS * TOK])
        raw = sb("raw", [128, 2, HEADS, HEAD_DIM + 1])
        inverse = sb("inverse", [128, 2, HEADS])
        heads_out = sb("heads_out", [128, GROUP, DIM])
        heads_outT = sb("heads_outT", [128, COLS])
        if clipped:
            limit = sb("limit", [128, GROUP, KEYS])
            forbidden, limit_ready = sem("forbidden"), sem("limit_ready")
        mask_in = sem("mask_in")
        ctx_in, xn_ready, turned, xnT_ready = (
            sem("ctx_in"), sem("xn_ready"), sem("turned"), sem("xnT_ready"))
        own_ready, sums_taken = sem("own_ready"), sem("sums_taken")
        q_made, k_made, v_made, q_ready, k_ready, v_ready = (
            sem("q_made"), sem("k_made"), sem("v_made"), sem("q_ready"), sem("k_ready"),
            sem("v_ready"))
        scores_ready, scores_taken, largest_ready, below_ready, powers_ready = (
            sem("scores_ready"), sem("scores_taken"), sem("largest_ready"), sem("below_ready"),
            sem("powers_ready"))
        powers_turned, powersT_ready, heads_summed, inverse_ready, heads_out_ready = (
            sem("powers_turned"), sem("powersT_ready"), sem("heads_summed"), sem("inverse_ready"),
            sem("heads_out_ready"))
        heads_turned, heads_outT_ready, projected, ln = (
            sem("heads_turned"), sem("heads_outT_ready"), sem("projected"), NormSignals(sem))
        SCORES, TURNED, SUMS, MISC = 0, 4, 6, 7
        sums = bank[:, SUMS, 0:HEADS * (HEAD_DIM + 1)].rearrange("p (h c) -> p h c", h=HEADS)
        block = ctx.enter_context(nc.Block())

        @block.sync
        def _(sp):
            def load(n):
                sp.wait_ge(v_made, CHUNKS * n)
                if clipped:
                    sp.wait_ge(forbidden, n)
                shared.load(sp, d, chip.rows(n), clipped, ctx_in, mask_in)

            load(1)
            if name == "x0":
                for later, weights in chip.weights.items():
                    if later != "x0":
                        weights.load(sp)
            with sp.Fori(2, BLOCKS) as n:
                load(n)

        @block.tensor
        def _(pe):
            def turn(n):
                pe.wait_ge(xn_ready, n + 1)
                for j in range(GROUP):
                    last = nc.tensor.transpose(bank[:, MISC, j * TOK:(j + 1) * TOK], xn[:, j, :],
                                               chip.ident[:, :])
                last.then_inc(turned, 1)

            def project_q(n, half):
                if half == 0:
                    pe.wait_ge(xnT_ready, n + 1)
                else:
                    pe.wait_ge(q_ready, 2 * n + 1)
                cols = slice(half * COLS // 2, (half + 1) * COLS // 2)
                nc.tensor.matmul(bank[:, MISC, cols], w_q[:, :], xnT[:, cols],
                                 start=True, stop=True).then_inc(q_made, 1)

            def project_k(n, first=False):
                if not first:
                    pe.wait_ge(ctx_in, 32 * n)
                nc.tensor.matmul(bank[:, MISC, 0:KCOLS], w_k[:, :],
                                 ctxT[:, :, 0, 0:KEYS], start=True, stop=True).then_inc(k_made, 1)

            def project_v(n, c):
                first_key = 128 * c % SPAN
                for j in range(GROUP):
                    keys = ctxT[:, j, :, :].rearrange("p a k -> p (a k)")
                    last = nc.tensor.matmul(bank[:, MISC, j * DIM:(j + 1) * DIM],
                                            keys[:, first_key:first_key + 128], w_v[:, :],
                                            start=True, stop=True)
                last.then_inc(v_made, 1)

            def scores(n, i, first=False):
                j, half = divmod(i, 2)
                x = UNITS * n + i
                if i % 4 == 0:
                    pe.wait_ge(q_ready, 2 * n + i // 4 + 1)
                if half == 0:
                    pe.wait_ge(own_ready, GROUP * n + j + 1)
                if not first:
                    pe.wait_ge(scores_taken, x - 1)
                for g in range(2):
                    h = HALF * half + QUAD * g
                    last = nc.tensor.matmul(bank[:, SCORES + 2 * half + g, 0:QUAD * KEYS],
                                            qT[:, j * TOK:(j + 1) * TOK],
                                            own_kT[:, j % 2, h:h + QUAD, :]
                                            .rearrange("p h k -> p (h k)"),
                                            start=True, stop=True)
                last.then_inc(scores_ready, 1)

            def turn_powers(n, i, g, first=False):
                x = UNITS * n + i
                if g == 0:
                    pe.wait_ge(powers_ready, x + 1)
                if not first:
                    pe.wait_ge(powersT_ready, 2 * x + g - 1)
                padded = powers[:, i % 2, :, :].rearrange("p h k -> p (h k)")
                for c in range(CHUNKS):
                    at = 128 * (CHUNKS * g + c)
                    last = nc.tensor.transpose(bank[:, TURNED + g, c * TOK:(c + 1) * TOK],
                                               padded[:, at:at + 128], chip.ident[:, :])
                last.then_inc(powers_turned, 1)

            def sum_values(n, u, i, g):
                j, half = divmod(i, 2)
                if half == 0 and g == 0:
                    pe.wait_ge(sums_taken, GROUP * n + j)
                    if j == 0:
                        pe.wait_ge(v_ready, CHUNKS * (n + 1))
                        pe.wait_ge(heads_outT_ready, n)
                pe.wait_ge(powersT_ready, 2 * (UNITS * n + i) + g + 1)
                part = 2 * half + g
                for c in range(CHUNKS):
                    last = nc.tensor.matmul(bank[:, SUMS, WIDTH * part:WIDTH * (part + 1)],
                                            powersT[:, part, c * TOK:(c + 1) * TOK],
                                            v[:, u, j, part, c, :],
                                            start=(c == 0), stop=(c == CHUNKS - 1))
                last.then_inc(heads_summed, 1)

            def project_out(n, more):
                pe.wait_ge(heads_out_ready, GROUP * (n + 1))
                pe.wait_ge(sums_taken, GROUP * (n + 1))
                for j in range(GROUP):
                    last = nc.tensor.transpose(bank[:, SUMS, j * TOK:(j + 1) * TOK],
                                               heads_out[:, j, :], chip.ident[:, :])
                last.then_inc(heads_turned, 1)
                pe.wait_ge(v_ready, CHUNKS * (n + 2 if more else n + 1))
                pe.wait_ge(heads_outT_ready, n + 1)
                for j in range(GROUP):
                    nc.tensor.matmul(bank[:, MISC, j * DIM:(j + 1) * DIM],
                                     heads_outT[:, j * TOK:(j + 1) * TOK], w_o[:, :],
                                     start=True, stop=False)
                    last = nc.tensor.matmul(bank[:, MISC, j * DIM:(j + 1) * DIM], ones[:, :],
                                            b_o[:, :], start=False, stop=True)
                last.then_inc(projected, 1)

            def body(n, u, more):
                for i in range(UNITS):
                    if i:
                        turn_powers(n, i, 0)
                    if i < UNITS - 2:
                        scores(n, i + 2)
                    elif more:
                        scores(n + 1, i + 2 - UNITS)
                    if i:
                        turn_powers(n, i, 1)
                    sum_values(n, u, i, 0)
                    if more:
                        if i == 2:
                            pe.wait_ge(ln.updated, n)
                            project_k(n + 1)
                        elif i == 3:
                            pe.wait_ge(k_ready, n + 2)
                            turn(n + 1)
                        elif i == 4:
                            project_q(n + 1, 0)
                        elif i == 5:
                            pe.wait_ge(q_ready, 2 * n + 3)
                            project_v(n + 1, 0)
                        elif i == 6:
                            pe.wait_ge(v_ready, CHUNKS * (n + 1) + 1)
                            project_q(n + 1, 1)
                        elif i == 7:
                            pe.wait_ge(q_ready, 2 * n + 4)
                            project_v(n + 1, 1)
                    sum_values(n, u, i, 1)
                if more:
                    turn_powers(n + 1, 0, 0)
                    turn_powers(n + 1, 0, 1)
                    pe.wait_ge(v_ready, CHUNKS * (n + 1) + 2)
                    project_v(n + 1, 2)
                project_out(n, more)

            pe.wait_ge(w.loaded, w.all)
            pe.wait_ge(first_in, 48 if clipped else 32)
            project_k(0, True)
            pe.wait_ge(k_ready, 1)
            turn(0)
            project_q(0, 0)
            project_q(0, 1)
            scores(0, 0, True)
            pe.wait_ge(q_ready, 2)
            project_v(0, 0)
            scores(0, 1, True)
            pe.wait_ge(v_ready, 1)
            project_v(0, 1)
            pe.wait_ge(v_ready, 2)
            project_v(0, 2)
            turn_powers(0, 0, 0, True)
            turn_powers(0, 0, 1, True)
            engine_loop_pairs(pe, body)

        @block.scalar
        def _(act):
            def take_turned(n):
                act.wait_ge(turned, n + 1)
                nc.scalar.copy(xnT[:, :], bank[:, MISC, :]).then_inc(xnT_ready, 1)

            def take_q(n, half):
                act.wait_ge(q_made, 2 * n + half + 1)
                act.wait_ge(scores_ready, UNITS * n - 4 + 4 * half)
                cols = slice(half * COLS // 2, (half + 1) * COLS // 2)
                nc.scalar.activation(qT[:, cols], bank[:, MISC, cols], ACT.Identity,
                                     bias=b_q[:, 0:1]).then_inc(q_ready, 1)

            def exps(n, i, first=False):
                x = UNITS * n + i
                act.wait_ge(below_ready, x + 1)
                if not first:
                    act.wait_ge(powers_turned, 2 * (x - 1))
                nc.scalar.activation(powers[:, i % 2, :, 0:KEYS], below[:, i % 2, :, :],
                                     ACT.Exp, scale=scale).then_inc(powers_ready, 1)

            def take_powers(n, i, g, first=False):
                q = 2 * (UNITS * n + i) + g
                act.wait_ge(powers_turned, q + 1)
                if not first:
                    act.wait_ge(heads_summed, q - QUARTERS + 1)
                nc.scalar.copy(powersT[:, 2 * (i % 2) + g, :], bank[:, TURNED + g, 0:CHUNKS * TOK])\
                    .then_inc(powersT_ready, 1)

            def take_sums(n, j):
                m = GROUP * n + j
                act.wait_ge(heads_summed, QUARTERS * (m + 1))
                if j >= 2:
                    act.wait_ge(heads_out_ready, m - 1)
                elif j == 0:
                    act.wait_ge(heads_out_ready, GROUP * n)
                nc.scalar.copy(raw[:, j % 2, :, :], sums).then_inc(sums_taken, 1)

            def body(n, more):
                for i in range(UNITS):
                    if i:
                        take_powers(n, i, 0, i < 2)
                        take_powers(n, i, 1, i < 2)
                    if i < UNITS - 1:
                        exps(n, i + 1)
                    elif more:
                        exps(n + 1, 0)
                    if i % 2:
                        take_sums(n, i // 2)
                    if more:
                        if i == 3:
                            take_turned(n + 1)
                        elif i == 4:
                            take_q(n + 1, 0)
                        elif i == 6:
                            take_q(n + 1, 1)
                if more:
                    take_powers(n + 1, 0, 0)
                    take_powers(n + 1, 0, 1)
                act.wait_ge(heads_turned, n + 1)
                nc.scalar.copy(heads_outT[:, :], bank[:, SUMS, :]).then_inc(heads_outT_ready, 1)

            chip.load_table(ACT.Exp)
            act.wait_ge(w.loaded, w.all)
            take_turned(0)
            for half in range(2):
                act.wait_ge(q_made, half + 1)
                cols = slice(half * COLS // 2, (half + 1) * COLS // 2)
                nc.scalar.activation(qT[:, cols], bank[:, MISC, cols], ACT.Identity,
                                     bias=b_q[:, 0:1]).then_inc(q_ready, 1)
            exps(0, 0, True)
            take_powers(0, 0, 0, True)
            take_powers(0, 0, 1, True)
            engine_loop(act, body)

        @block.vector
        def _(dve):
            def take_k(n):
                dve.wait_ge(k_made, n + 1)
                dve.wait_ge(own_ready, GROUP * n)
                nc.vector.tensor_scalar(
                    kT[:, :, :], bank[:, MISC, 0:KCOLS].rearrange("p (b k) -> p b k", b=GROUP),
                    b_k[:, 0:1], None, ALU.add).then_inc(k_ready, 1)

            def take_v(n, u, c):
                dve.wait_ge(v_made, CHUNKS * n + c + 1)
                for chunk, h, lo, hi in PIECES:
                    if chunk == c:
                        at = h * (HEAD_DIM + 1)
                        rows = slice(lo, hi)
                        last = nc.vector.tensor_tensor(
                            out=v[rows, u, :, :, c, at:at + HEAD_DIM],
                            in0=bank[rows, MISC, :].rearrange(
                                "p (b g h d) -> p b g h d", b=GROUP, g=QUARTERS, h=QUAD)[:, :, :, h],
                            in1=bc(b_v[rows, :].rearrange(
                                "p (g h d) -> p g h d", g=QUARTERS, h=QUAD)[:, :, h], 1, GROUP),
                            op=ALU.add)
                last.then_inc(v_ready, 1)

            def limits(n, first=False):
                if first:
                    dve.wait_ge(first_in, 48)
                else:
                    dve.wait_ge(mask_in, 16 * n)
                nc.vector.tensor_scalar(limit[:, :, :], mask[:, :, :], 0.0, -1e30, ALU.is_equal,
                                        ALU.mult).then_inc(forbidden, 1)
                dve.wait_ge(forbidden, n + 1)
                nc.vector.tensor_scalar(limit[:, :, :], limit[:, :, :], CLIP / scale, None,
                                        ALU.add).then_inc(limit_ready, 1)
                dve.wait_ge(limit_ready, n + 1)

            def softmax(n, i, first=False):
                j, half = divmod(i, 2)
                x = UNITS * n + i
                scores = bank[:, SCORES + 2 * half:SCORES + 2 * half + 2, 0:QUAD * KEYS].rearrange(
                    "p g (h k) -> p g h k", k=KEYS)
                result = below[:, half, :, :].rearrange("p (g h) k -> p g h k", g=2)
                dve.wait_ge(scores_ready, x + 1)
                if clipped:
                    if not first:
                        dve.wait_ge(powers_ready, x - 1)
                    for g in range(2):
                        last = nc.vector.scalar_tensor_tensor(
                            out=result[:, g], in0=scores[:, g], scalar=-CLIP / scale,
                            in1=bc(limit[:, j, :], 1, QUAD), op0=ALU.max, op1=ALU.min)
                    last.then_inc(scores_taken, 1)
                    dve.wait_ge(scores_taken, x + 1)
                    scores = result
                nc.vector.tensor_reduce(largest[:, half, :].rearrange("p (g h) -> p g h", g=2),
                                        scores, AX.X, ALU.max).then_inc(largest_ready, 1)
                if not clipped and not first:
                    dve.wait_ge(powers_ready, x - 1)
                dve.wait_ge(largest_ready, x + 1)
                nc.vector.tensor_tensor(
                    out=result, in0=scores,
                    in1=bc(largest[:, half, :].rearrange("p (g h) -> p g h", g=2), 3, KEYS),
                    op=ALU.subtract).then_inc(below_ready, 1)
                if not clipped:
                    nc.vector.memset(chip.carrier[:, :], 0.0).then_inc(scores_taken, 1)

            def divide(n, j):
                m = GROUP * n + j
                dve.wait_ge(sums_taken, m + 1)
                nc.vector.reciprocal(inverse[:, j % 2, :], raw[:, j % 2, :, HEAD_DIM])\
                    .then_inc(inverse_ready, 1)
                dve.wait_ge(inverse_ready, m + 1)
                nc.vector.tensor_tensor(
                    out=heads_out[:, j, :].rearrange("p (h c) -> p h c", h=HEADS),
                    in0=raw[:, j % 2, :, 0:HEAD_DIM], in1=bc(inverse[:, j % 2, :], 2, HEAD_DIM),
                    op=ALU.mult).then_inc(heads_out_ready, 1)

            def body(n, u, more):
                for i in range(1, UNITS):
                    if i < UNITS - 2:
                        softmax(n, i + 2)
                    elif more:
                        if clipped and i == UNITS - 2:
                            limits(n + 1)
                        softmax(n + 1, i + 2 - UNITS)
                    if i == 2 and more:
                        chip.normalise(n + 1, xn).then_inc(xn_ready, 1)
                        take_k(n + 1)
                    if i % 2:
                        divide(n, i // 2)
                    if i == 5 and more:
                        take_v(n + 1, 1 - u, 0)
                    if i == 7 and more:
                        take_v(n + 1, 1 - u, 1)
                if more:
                    take_v(n + 1, 1 - u, 2)
                    softmax(n + 1, 2)
                dve.wait_ge(projected, n + 1)
                chip.add_to_x(dve, n, bank[:, MISC, :].rearrange("p (b d) -> p b d", b=GROUP), ln)

            dve.wait_ge(w.loaded, w.all)
            chip.normalise(0, xn).then_inc(xn_ready, 1)
            take_k(0)
            if clipped:
                limits(0, True)
            softmax(0, 0, True)
            take_v(0, 0, 0)
            softmax(0, 1, True)
            take_v(0, 0, 1)
            take_v(0, 0, 2)
            softmax(0, 2)
            engine_loop_pairs(dve, body)

        @block.gpsimd
        def _(pool):
            chip.clear_last()

            def own(n, j):
                if j == 0:
                    pool.wait_ge(k_ready, n + 1)
                nc.gpsimd.tensor_tensor(out=own_kT[:, j % 2, :, :], in0=bc(kT[:, j, :], 1, HEADS),
                                        in1=bc(own_head[:, :], 2, KEYS),
                                        op=ALU.mult).then_inc(own_ready, 1)

            def body(n, more):
                pool.wait_ge(scores_ready, UNITS * n + 4)
                own(n, 3)
                if more:
                    for j in range(3):
                        pool.wait_ge(scores_ready, UNITS * n + 2 * (j + 3))
                        own(n + 1, j)
                chip.rstd_of(pool, n, ln)
            pool.wait_ge(w.loaded, w.all)
            own(0, 0)
            own(0, 1)
            pool.wait_ge(scores_ready, 2)
            own(0, 2)
            engine_loop(pool, body)


def slot_attention(chip):
    nc, d, bank = chip.nc, chip.dram, chip.bank
    ctx, sb, sem = phase(chip, "slots")
    with ctx:
        scale = DIM ** -0.5
        TWO = (0, 1)
        w = chip.weights["slots"]
        w_q, w_k, w_v, w_ih, w_hh, b_ih, b_hh, slot_norm, input_norm = w.tiles(
            "w_q", "w_k", "w_v", "w_ih", "w_hh", "b_ih", "b_hh", "slot_norm", "input_norm")
        half_b = sb("half_b", [128, 3])
        mean_col = sb("mean_col", [128, 1])
        each = lambda t, shape: [sb(f"{t}{u}", shape) for u in TWO]
        context = each("context", [KEYS, GROUP, DIM])
        square = each("square", [128, COLS])
        energy = each("energy", [128, GROUP])
        rms = each("rms", [128, GROUP])
        context_energy = each("context_energy", [KEYS, GROUP])
        context_rms = each("context_rms", [KEYS, GROUP])
        inverse = each("inverse", [128, GROUP])
        unit = each("unit", [KEYS, GROUP, DIM])
        unitT = each("unitT", [128, KCOLS])
        kT = each("kT", [128, KCOLS])
        v = each("v", [KEYS, GROUP, DIM + 1])
        xn = each("xn", [128, GROUP, DIM])
        h = each("h", [128, COLS])
        spread = each("spread", [128, COLS])
        qT = each("qT", [128, COLS])
        offset = each("offset", [KEYS, GROUP])
        powers = each("powers", [KEYS, COLS])
        total = each("total", [KEYS, GROUP])
        mixed = each("mixed", [128, GROUP, DIM])
        update = each("update", [128, COLS])
        half_hidden = each("half_hidden", [128, COLS])
        tanh_r, tanh_z = each("tanh_r", [128, COLS]), each("tanh_z", [128, COLS])
        new = each("new", [128, COLS])
        consts, folded = sem("consts"), sem("folded")
        context_in = [sem("context_in0"), sem("context_in1")]
        pair = lambda t: [sem(f"{t}{u}") for u in TWO]
        context_squared, context_shifted, context_rms_ready, unit_ready, unit_turned = (
            pair("context_squared"), pair("context_shifted"), pair("context_rms_ready"),
            pair("unit_ready"), pair("unit_turned"))
        unitT_ready, k_made, v_made, k_ready, v_ready = (
            pair("unitT_ready"), pair("k_made"), pair("v_made"), pair("k_ready"), pair("v_ready"))
        xn_ready, turned, out_turned = pair("xn_ready"), pair("turned"), pair("out_turned")
        h_ready, squared, squares_summed, energy_ready, rms_ready = (
            pair("h_ready"), pair("squared"), pair("squares_summed"), pair("energy_ready"),
            pair("rms_ready"))
        rms_spread, q_made, hidden_made, rms_taken, hidden_taken, q_ready = (
            pair("rms_spread"), pair("q_made"), pair("hidden_made"), pair("rms_taken"),
            pair("hidden_taken"), pair("q_ready"))
        scores_ready, offset_ready, powers_ready, shares_ready = (
            pair("scores_ready"), pair("offset_ready"), pair("powers_ready"),
            pair("shares_ready"))
        updates_made, mixed_ready, update_turned = (
            pair("updates_made"), pair("mixed_ready"), pair("update_turned"))
        update_ready, r_made, new_made, z_made, r_ready, z_ready, drive_ready, new_ready = (
            pair("update_ready"), pair("r_made"), pair("new_made"), pair("z_made"),
            pair("r_ready"), pair("z_ready"), pair("drive_ready"), pair("new_ready"))
        dve_step, ln = sem("dve_step"), NormSignals(sem)
        seq = lambda j: slice(j * TOK, (j + 1) * TOK)
        count = lambda r, it: SLOT_ITERS * r + it + 1
        HS = SLOT_ITERS + 1
        R, Z, NEW = 0, 1, 2
        block = ctx.enter_context(nc.Block())

        def loop(engine, body):
            with engine.Fori(0, BLOCKS // 2 - 1) as r:
                body(r, True)
            body(BLOCKS // 2 - 1, False)

        def after(r, it, more):
            return (r, it + 1) if it + 1 < SLOT_ITERS else (r + 1, 0) if more else None

        @block.sync
        def _(sp):
            def load(n, u):
                sp.dma_start(context[u][:, :, :], d["ctx"][:, chip.rows(n), :])\
                    .then_inc(context_in[u], 16)
            for u in TWO:
                load(u, u)
            with sp.Fori(0, BLOCKS // 2 - 1) as r:
                for u in TWO:
                    sp.wait_ge(unit_ready[u], r + 1)
                    load(2 * (r + 1) + u, u)

        @block.tensor
        def _(pe):
            def turn(r, u):
                pe.wait_ge(xn_ready[u], r + 1)
                for j in range(GROUP):
                    last = nc.tensor.transpose(bank[:, 4 * u + 1, seq(j)], xn[u][:, j, :],
                                               chip.ident[:, :])
                last.then_inc(turned[u], 1)

            def turn_context(r, u):
                pe.wait_ge(unit_ready[u], r + 1)
                for j in range(GROUP):
                    last = nc.tensor.transpose(bank[:, 4 * u + 2, j * KEYS:(j + 1) * KEYS],
                                               unit[u][:, j, :], chip.ident[0:KEYS, 0:KEYS])
                last.then_inc(unit_turned[u], 1)

            def keys(r, u):
                pe.wait_ge(unitT_ready[u], r + 1)
                nc.tensor.matmul(bank[:, 4 * u + 2, 0:KCOLS], w_k[:, :], unitT[u][:, :],
                                 start=True, stop=True).then_inc(k_made[u], 1)

            def values(r, u):
                pe.wait_ge(k_ready[u], r + 1)
                for j in range(GROUP):
                    last = nc.tensor.matmul(bank[0:KEYS, 4 * u + 2, seq(j)],
                                            unitT[u][:, j * KEYS:(j + 1) * KEYS], w_v[:, :],
                                            start=True, stop=True)
                last.then_inc(v_made[u], 1)

            def from_h(r, it, u):
                pe.wait_ge(squared[u], count(r, it))
                for j in range(GROUP):
                    last = nc.tensor.matmul(bank[:, 4 * u, j:j + 1], square[u][:, seq(j)],
                                            mean_col[:, :], start=True, stop=True)
                last.then_inc(squares_summed[u], 1)
                nc.tensor.matmul(bank[:, 4 * u + 1, :], w_q[:, :], h[u][:, :],
                                 start=True, stop=True).then_inc(q_made[u], 1)

            def hidden(r, it, u, first=False):
                if it == 0 and not first:
                    pe.wait_ge(ln.updated, 2 * r + u - 1)
                nc.tensor.matmul(bank[:, 4 * u + 3, :], w_hh[:, NEW, :], h[u][:, :],
                                 start=True, stop=True).then_inc(hidden_made[u], 1)

            def spread_rms(r, it, u):
                pe.wait_ge(rms_ready[u], count(r, it))
                for j in range(GROUP):
                    last = nc.tensor.matmul(bank[:, 4 * u, seq(j)],
                                            rms[u][:, j:j + 1].broadcast_to([128, 128]),
                                            chip.ident[:, :], start=True, stop=True)
                last.then_inc(rms_spread[u], 1)

            def scores(r, it, u):
                pe.wait_ge(q_ready[u], count(r, it))
                if it == 0:
                    pe.wait_ge(v_ready[u], r + 1)
                for j in range(GROUP):
                    last = nc.tensor.matmul(bank[0:KEYS, 4 * u + 2, seq(j)],
                                            kT[u][:, j * KEYS:(j + 1) * KEYS],
                                            qT[u][:, seq(j)], start=True, stop=True)
                last.then_inc(scores_ready[u], 1)

            def from_shares(r, it, u):
                pe.wait_ge(shares_ready[u], count(r, it))
                for j in range(GROUP):
                    at = DIM + 1 if j % 2 else 0
                    last = nc.tensor.matmul(bank[:, 4 * u + j // 2, at:at + DIM + 1],
                                            powers[u][:, seq(j)], v[u][:, j, :],
                                            start=True, stop=True)
                last.then_inc(updates_made[u], 1)
                nc.tensor.matmul(bank[:, 4 * u + 2, :], w_hh[:, R, :], h[u][:, :],
                                 start=True, stop=False)

            def turn_updates(r, it, u):
                pe.wait_ge(mixed_ready[u], count(r, it))
                for j in range(GROUP):
                    last = nc.tensor.transpose(bank[:, 4 * u + 1, seq(j)], mixed[u][:, j, :],
                                               chip.ident[:, :])
                last.then_inc(update_turned[u], 1)
                nc.tensor.matmul(bank[:, 4 * u, :], w_hh[:, Z, :], h[u][:, :],
                                 start=True, stop=False)

            def gates(r, it, u):
                pe.wait_ge(update_ready[u], count(r, it))
                nc.tensor.matmul(bank[:, 4 * u + 2, :], w_ih[:, R, :], update[u][:, :],
                                 start=False, stop=True).then_inc(r_made[u], 1)
                nc.tensor.matmul(bank[:, 4 * u + 1, :], w_ih[:, NEW, :], update[u][:, :],
                                 start=True, stop=True).then_inc(new_made[u], 1)
                nc.tensor.matmul(bank[:, 4 * u, :], w_ih[:, Z, :], update[u][:, :],
                                 start=False, stop=True).then_inc(z_made[u], 1)

            def turn_out(r, u):
                pe.wait_ge(h_ready[u], HS * (r + 1))
                for j in range(GROUP):
                    last = nc.tensor.transpose(bank[:, 4 * u + 3, seq(j)], h[u][:, seq(j)],
                                               chip.ident[:, :])
                last.then_inc(out_turned[u], 1)

            def start(u):
                turn(0, u)
                turn_context(0, u)
                keys(0, u)
                values(0, u)

            def body(r, more):
                for it in range(SLOT_ITERS):
                    then = after(r, it, more)
                    change = it == SLOT_ITERS - 1
                    from_h(r, it, 1)
                    hidden(r, it, 1)
                    spread_rms(r, it, 1)
                    if change:
                        turn_out(r, 0)
                        if more:
                            turn(r + 1, 0)
                            turn_context(r + 1, 0)
                    elif then:
                        from_h(*then, 0)
                    scores(r, it, 1)
                    if change and then:
                        keys(r + 1, 0)
                        from_h(*then, 0)
                        values(r + 1, 0)
                    if then:
                        spread_rms(*then, 0)
                        hidden(*then, 0)
                    from_shares(r, it, 1)
                    if then:
                        scores(*then, 0)
                    turn_updates(r, it, 1)
                    gates(r, it, 1)
                    if then:
                        from_shares(*then, 0)
                        turn_updates(*then, 0)
                        gates(*then, 0)
                turn_out(r, 1)
                if more:
                    turn(r + 1, 1)
                    turn_context(r + 1, 1)
                    keys(r + 1, 1)
                    values(r + 1, 1)

            pe.wait_ge(folded, 3)
            pe.wait_ge(consts, 3)
            start(0)
            from_h(0, 0, 0)
            hidden(0, 0, 0, True)
            start(1)
            spread_rms(0, 0, 0)
            scores(0, 0, 0)
            from_shares(0, 0, 0)
            turn_updates(0, 0, 0)
            gates(0, 0, 0)
            loop(pe, body)

        @block.scalar
        def _(act):
            def square_context(r, u):
                act.wait_ge(context_in[u], 16 * (r + 1))
                act.wait_ge(unit_turned[u], r)
                for j in range(GROUP):
                    last = nc.scalar.activation(unit[u][:, j, :], context[u][:, j, :],
                                                ACT.Square, scale=scale,
                                                accum_out=context_energy[u][:, j:j + 1])
                last.then_inc(context_squared[u], 1)

            def take_turned(r, u):
                act.wait_ge(turned[u], r + 1)
                nc.scalar.copy(h[u][:, :], bank[:, 4 * u + 1, :]).then_inc(h_ready[u], 1)

            def take_context(r, u):
                act.wait_ge(unit_turned[u], r + 1)
                nc.scalar.copy(unitT[u][:, :], bank[:, 4 * u + 2, 0:KCOLS])\
                    .then_inc(unitT_ready[u], 1)

            def take_keys(r, u):
                act.wait_ge(k_made[u], r + 1)
                nc.scalar.copy(kT[u][:, :], bank[:, 4 * u + 2, 0:KCOLS]).then_inc(k_ready[u], 1)

            def square_h(r, it, u):
                act.wait_ge(h_ready[u], HS * r + it + 1)
                nc.scalar.activation(square[u][:, :], h[u][:, :], ACT.Square)\
                    .then_inc(squared[u], 1)

            def take_rms(r, it, u):
                act.wait_ge(rms_spread[u], count(r, it))
                nc.scalar.activation(spread[u][:, :], bank[:, 4 * u, :], ACT.Identity,
                                     scale=-scale).then_inc(rms_taken[u], 1)

            def take_hidden(r, it, u):
                act.wait_ge(hidden_made[u], count(r, it))
                nc.scalar.activation(half_hidden[u][:, :], bank[:, 4 * u + 3, :], ACT.Identity,
                                     bias=half_b[:, NEW:NEW + 1],
                                     scale=0.5).then_inc(hidden_taken[u], 1)

            def exps(r, it, u):
                act.wait_ge(offset_ready[u], count(r, it))
                for j in range(GROUP):
                    last = nc.scalar.activation(
                        powers[u][:, seq(j)], bank[0:KEYS, 4 * u + 2, seq(j)], ACT.Exp,
                        bias=offset[u][:, j:j + 1], scale=-1.0, accum_out=total[u][:, j:j + 1])
                last.then_inc(powers_ready[u], 1)

            def take_updates(r, it, u):
                act.wait_ge(update_turned[u], count(r, it))
                nc.scalar.copy(update[u][:, :], bank[:, 4 * u + 1, :]).then_inc(update_ready[u], 1)

            def gate_tanhs(r, it, u):
                act.wait_ge(r_made[u], count(r, it))
                nc.scalar.activation(tanh_r[u][:, :], bank[:, 4 * u + 2, :], ACT.Tanh,
                                     bias=half_b[:, R:R + 1], scale=0.5).then_inc(r_ready[u], 1)
                act.wait_ge(z_made[u], count(r, it))
                nc.scalar.activation(tanh_z[u][:, :], bank[:, 4 * u, :], ACT.Tanh,
                                     bias=half_b[:, Z:Z + 1], scale=0.5).then_inc(z_ready[u], 1)

            def new_tanh(r, it, u):
                act.wait_ge(drive_ready[u], count(r, it))
                nc.scalar.activation(new[u][:, :], new[u][:, :], ACT.Tanh,
                                     bias=b_ih[:, NEW:NEW + 1]).then_inc(new_ready[u], 1)

            def body(r, more):
                for it in range(SLOT_ITERS):
                    then = after(r, it, more)
                    change = it == SLOT_ITERS - 1
                    if it:
                        gate_tanhs(r, it, 0)
                        new_tanh(r, it, 0)
                    else:
                        square_h(*then, 0)
                    take_rms(r, it, 1)
                    take_hidden(r, it, 1)
                    if change and then:
                        take_turned(r + 1, 0)
                        take_context(r + 1, 0)
                    if then and it:
                        square_h(*then, 0)
                    if change and then:
                        take_keys(r + 1, 0)
                    exps(r, it, 1)
                    if then:
                        take_rms(*then, 0)
                        take_hidden(*then, 0)
                    take_updates(r, it, 1)
                    if then:
                        exps(*then, 0)
                    gate_tanhs(r, it, 1)
                    new_tanh(r, it, 1)
                    if then:
                        take_updates(*then, 0)
                    if it == 0 and more:
                        square_context(r + 1, 0)
                        square_context(r + 1, 1)
                    if not change:
                        square_h(r, it + 1, 1)
                if more:
                    gate_tanhs(r + 1, 0, 0)
                    take_turned(r + 1, 1)
                    take_context(r + 1, 1)
                    new_tanh(r + 1, 0, 0)
                    square_h(r + 1, 0, 1)
                    take_keys(r + 1, 1)

            chip.load_table(ACT.Exp)
            act.wait_ge(folded, 3)
            square_context(0, 0)
            square_context(0, 1)
            for u in TWO:
                take_turned(0, u)
                take_context(0, u)
                square_h(0, 0, u)
                take_keys(0, u)
            take_rms(0, 0, 0)
            take_hidden(0, 0, 0)
            exps(0, 0, 0)
            take_updates(0, 0, 0)
            gate_tanhs(0, 0, 0)
            new_tanh(0, 0, 0)
            loop(act, body)

        @block.vector
        def _(dve):
            OWN = 6
            done = [0]

            def step(r, instruction):
                instruction.then_inc(dve_step, 1)
                done[0] += 1
                dve.wait_ge(dve_step, 2 * SLOT_ITERS * OWN * r + done[0])

            def normalise(r, u):
                dve.wait_ge(turned[u], r)
                chip.normalise(2 * r + u, xn[u]).then_inc(xn_ready[u], 1)

            def scale_context(r, u):
                dve.wait_ge(context_rms_ready[u], r + 1)
                nc.vector.tensor_tensor(out=unit[u][:, :, :], in0=context[u][:, :, :],
                                        in1=bc(context_rms[u][:, :], 2, DIM),
                                        op=ALU.mult).then_inc(unit_ready[u], 1)

            def take_values(r, u):
                dve.wait_ge(v_made[u], r + 1)
                nc.vector.tensor_copy(v[u][:, :, 0:DIM],
                                      bank[0:KEYS, 4 * u + 2, :].rearrange(
                                          "p (b d) -> p b d", b=GROUP)).then_inc(v_ready[u], 1)

            def add_eps(r, it, u):
                dve.wait_ge(squares_summed[u], count(r, it))
                nc.vector.tensor_tensor(out=energy[u][:, :], in0=bank[:, 4 * u, 0:GROUP],
                                        in1=chip.rms_eps[:, :],
                                        op=ALU.add).then_inc(energy_ready[u], 1)

            def queries(r, it, u):
                dve.wait_ge(rms_taken[u], count(r, it))
                dve.wait_ge(q_made[u], count(r, it))
                nc.vector.tensor_tensor(out=qT[u][:, :], in0=bank[:, 4 * u + 1, :],
                                        in1=spread[u][:, :], op=ALU.mult).then_inc(q_ready[u], 1)

            def offsets(r, it, u):
                dve.wait_ge(scores_ready[u], count(r, it))
                nc.vector.tensor_reduce(
                    offset[u][:, :], bank[0:KEYS, 4 * u + 2, :].rearrange(
                        "p (b s) -> p b s", b=GROUP), AX.X, ALU.min).then_inc(offset_ready[u], 1)

            def shares(r, base, it, u):
                dve.wait_ge(powers_ready[u], count(r, it))
                step(base, nc.vector.reciprocal(total[u][:, :], total[u][:, :]))
                by_seq = powers[u][:, :].rearrange("p (b s) -> p b s", b=GROUP)
                nc.vector.tensor_tensor(out=by_seq, in0=by_seq, in1=bc(total[u][:, :], 2, TOK),
                                        op=ALU.mult).then_inc(shares_ready[u], 1)

            def mix(r, base, it, u):
                dve.wait_ge(updates_made[u], count(r, it))
                raw = bank[:, 4 * u:4 * u + 2, 0:2 * (DIM + 1)].rearrange(
                    "p c (j d) -> p c j d", d=DIM + 1)
                by_bank = inverse[u][:, :].rearrange("p (c j) -> p c j", c=2)
                step(base, nc.vector.tensor_scalar(by_bank, raw[:, :, :, DIM], RMS_EPS, None,
                                                   ALU.add))
                step(base, nc.vector.reciprocal(inverse[u][:, :], inverse[u][:, :]))
                nc.vector.tensor_tensor(
                    out=mixed[u][:, :, :].rearrange("p (c j) d -> p c j d", c=2),
                    in0=raw[:, :, :, 0:DIM], in1=bc(by_bank, 3, DIM),
                    op=ALU.mult).then_inc(mixed_ready[u], 1)

            def drive(r, base, it, u):
                dve.wait_ge(r_ready[u], count(r, it))
                dve.wait_ge(hidden_taken[u], count(r, it))
                step(base, nc.vector.scalar_tensor_tensor(
                    out=new[u][:, :], in0=tanh_r[u][:, :], scalar=1.0,
                    in1=half_hidden[u][:, :], op0=ALU.add, op1=ALU.mult))
                dve.wait_ge(new_made[u], count(r, it))
                nc.vector.tensor_tensor(out=new[u][:, :], in0=new[u][:, :],
                                        in1=bank[:, 4 * u + 1, :],
                                        op=ALU.add).then_inc(drive_ready[u], 1)

            def next_h(r, base, it, u):
                dve.wait_ge(z_ready[u], count(r, it))
                nc.vector.tensor_scalar(half_hidden[u][:, :], tanh_z[u][:, :], -0.5, 0.5,
                                        ALU.mult, ALU.add)
                step(base, nc.vector.scalar_tensor_tensor(
                    out=h[u][:, :], in0=tanh_z[u][:, :], scalar=1.0, in1=h[u][:, :],
                    op0=ALU.add, op1=ALU.mult))
                dve.wait_ge(new_ready[u], count(r, it))
                step(base, nc.vector.tensor_tensor(out=new[u][:, :], in0=new[u][:, :],
                                                   in1=half_hidden[u][:, :], op=ALU.mult))
                nc.vector.scalar_tensor_tensor(
                    out=h[u][:, :], in0=h[u][:, :], scalar=0.5, in1=new[u][:, :],
                    op0=ALU.mult, op1=ALU.add).then_inc(h_ready[u], 1)

            def add(r, u):
                dve.wait_ge(out_turned[u], r + 1)
                chip.add_to_x(dve, 2 * r + u, bank[:, 4 * u + 3, :].rearrange(
                    "p (b d) -> p b d", b=GROUP), ln)

            FIRST = 6

            def body(r, more):
                done[0] = FIRST
                for it in range(SLOT_ITERS):
                    then = after(r, it, more)
                    change = it == SLOT_ITERS - 1
                    if it:
                        drive(r, r, it, 0)
                        add_eps(r, it, 1)
                        next_h(r, r, it, 0)
                    else:
                        add_eps(*then, 0)
                    queries(r, it, 1)
                    if then and it == 1:
                        add_eps(*then, 0)
                    offsets(r, it, 1)
                    if then and change:
                        add_eps(*then, 0)
                        take_values(r + 1, 0)
                    if more and not change:
                        (normalise, scale_context)[it](r + 1, 1)
                    shares(r, r, it, 1)
                    if change:
                        add(r, 0)
                    if then:
                        queries(*then, 0)
                    mix(r, r, it, 1)
                    if more and not change:
                        (normalise, scale_context)[it](r + 1, 0)
                    if then:
                        offsets(*then, 0)
                        shares(then[0], r, then[1], 0)
                    drive(r, r, it, 1)
                    if then:
                        mix(then[0], r, then[1], 0)
                    next_h(r, r, it, 1)
                if more:
                    drive(r + 1, r, 0, 0)
                    next_h(r + 1, r, 0, 0)
                    add_eps(r + 1, 0, 1)
                add(r, 1)
                if more:
                    take_values(r + 1, 1)

            dve.wait_ge(w.loaded, w.all)
            nc.vector.tensor_scalar(w_q[:, :], w_q[:, :], slot_norm[:, 0:1], None, ALU.mult)
            nc.vector.tensor_scalar(w_k[:, :], w_k[:, :], input_norm[:, 0:1], None, ALU.mult)
            nc.vector.tensor_scalar(w_v[:, :], w_v[:, :], input_norm[:, 0:1], None, ALU.mult)\
                .then_inc(folded, 1)
            nc.vector.tensor_tensor(out=half_b[:, 0:2], in0=b_ih[:, 0:2], in1=b_hh[:, 0:2],
                                    op=ALU.add)
            nc.vector.tensor_scalar(half_b[:, 2:3], b_hh[:, 2:3], 0.5, None, ALU.mult)\
                .then_inc(folded, 1)
            dve.wait_ge(folded, 2)
            nc.vector.tensor_scalar(half_b[:, 0:2], half_b[:, 0:2], 0.5, None, ALU.mult)\
                .then_inc(folded, 1)
            for u in TWO:
                normalise(0, u)
                scale_context(0, u)
            take_values(0, 0)
            add_eps(0, 0, 0)
            take_values(0, 1)
            queries(0, 0, 0)
            offsets(0, 0, 0)
            shares(0, 0, 0, 0)
            mix(0, 0, 0, 0)
            drive(0, 0, 0, 0)
            next_h(0, 0, 0, 0)
            add_eps(0, 0, 1)
            assert done[0] == FIRST
            loop(dve, body)

        @block.gpsimd
        def _(pool):
            chip.clear_last()

            def context_power(r, u):
                pool.wait_ge(context_squared[u], r + 1)
                nc.gpsimd.tensor_tensor(out=context_energy[u][:, :], in0=context_energy[u][:, :],
                                        in1=chip.rms_eps[0:KEYS, :],
                                        op=ALU.add).then_inc(context_shifted[u], 1)
                pool.wait_ge(context_shifted[u], r + 1)
                nc.gpsimd.tensor_tensor(out=context_rms[u][:, :], in0=context_energy[u][:, :],
                                        in1=chip.minus_half[0:KEYS, :],
                                        op=ALU.pow).then_inc(context_rms_ready[u], 1)

            def power(r, it, u):
                pool.wait_ge(energy_ready[u], count(r, it))
                nc.gpsimd.tensor_tensor(out=rms[u][:, :], in0=energy[u][:, :],
                                        in1=chip.minus_half[:, :],
                                        op=ALU.pow).then_inc(rms_ready[u], 1)

            def body(r, more):
                for it in range(SLOT_ITERS):
                    then = after(r, it, more)
                    if it:
                        power(r, it, 1)
                    if it and then:
                        power(*then, 0)
                    if it == SLOT_ITERS - 1:
                        chip.rstd_of(pool, 2 * r, ln)
                    if it == 0 and more:
                        context_power(r + 1, 0)
                        context_power(r + 1, 1)
                if more:
                    power(r + 1, 0, 1)
                    power(r + 1, 1, 0)
                chip.rstd_of(pool, 2 * r + 1, ln)
            nc.gpsimd.memset(mean_col[:, :], 1.0 / DIM).then_inc(consts, 1)
            for u in TWO:
                nc.gpsimd.memset(v[u][:, :, DIM], 1.0).then_inc(consts, 1)
            context_power(0, 0)
            context_power(0, 1)
            power(0, 0, 0)
            power(0, 0, 1)
            power(0, 1, 0)
            loop(pool, body)


def context_attention(chip):
    nc, d, bank = chip.nc, chip.dram, chip.bank
    ctx, sb, sem = phase(chip, "x3")
    with ctx:
        scale = DIM ** -0.5
        ctxT = sb("ctxT", [128, 2, GROUP, KEYS])
        values = sb("values", [KEYS, 2, GROUP, DIM])
        mask = sb("mask", [128, 2, GROUP, KEYS])
        xn = sb("xn", [128, GROUP, DIM])
        xnT = sb("xnT", [128, 2, COLS])
        scaled = sb("scaled", [128, GROUP, KEYS])
        masks = sb("masks", [128, GROUP, KEYS], U32)
        largest = sb("largest", [128, GROUP])
        below = sb("below", [128, GROUP, KEYS])
        powers = sb("powers", [128, GROUP, KEYS])
        total = sb("total", [128, GROUP])
        share = sb("share", [128, GROUP, KEYS])
        number = sb("number", [128, GROUP, KEYS], U32)
        weight = sb("weight", [128, GROUP, KEYS])
        weightT = sb("weightT", [KEYS, COLS])
        loaded, xn_ready, turned, xnT_ready = (
            [sem("loaded0"), sem("loaded1")], sem("xn_ready"), sem("turned"), sem("xnT_ready"))
        zeros_ready = sem("zeros_ready")
        scores_ready, step_done, below_ready, powers_ready = (
            sem("scores_ready"), sem("step_done"), sem("below_ready"), sem("powers_ready"))
        weight_turned, weightT_ready, summed, ln = (
            sem("weight_turned"), sem("weightT_ready"), sem("summed"), NormSignals(sem))
        TURN, SCORES, WEIGHTS, OUT = 0, 1, 3, 4
        STEPS, LOGIT_STEPS = 9, 4
        block = ctx.enter_context(nc.Block())

        @block.sync
        def _(sp):
            def load(n, u, r=None):
                rows = chip.rows(n)
                sp.dma_start(ctxT[:, u, :, :], d["ctxT"][:, rows, :]).then_inc(loaded[u], 16)
                sp.dma_start(values[:, u, :, :], d["ctx"][:, rows, :]).then_inc(loaded[u], 16)
                sp.dma_start(mask[:, u, :, :], d["x3_mask"][:, rows, :]).then_inc(loaded[u], 16)

            def body(n, u, more):
                if more:
                    sp.wait_ge(summed, n)
                    load(n + 1, 1 - u)
            load(0, 0)
            engine_loop_pairs(sp, body)

        def landed(engine, n, u):
            engine.wait_ge(loaded[u], 24 * (n - u) + 48)

        @block.tensor
        def _(pe):
            def turn(n):
                pe.wait_ge(xn_ready, n + 1)
                for j in range(GROUP):
                    last = nc.tensor.transpose(bank[:, TURN, j * TOK:(j + 1) * TOK], xn[:, j, :],
                                               chip.ident[:, :])
                last.then_inc(turned, 1)

            def scores(n, u):
                landed(pe, n, u)
                pe.wait_ge(xnT_ready, n + 1)
                for j in range(GROUP):
                    last = nc.tensor.matmul(bank[:, SCORES + u, j * KEYS:(j + 1) * KEYS],
                                            xnT[:, u, j * TOK:(j + 1) * TOK], ctxT[:, u, j, :],
                                            start=True, stop=True)
                last.then_inc(scores_ready, 1)

            def body(n, u, more, more2):
                if more:
                    scores(n + 1, 1 - u)
                pe.wait_ge(step_done, STEPS * (n + 1))
                for j in range(GROUP):
                    last = nc.tensor.transpose(bank[0:KEYS, WEIGHTS, j * TOK:(j + 1) * TOK],
                                               weight[:, j, :], chip.ident[:, :])
                last.then_inc(weight_turned, 1)
                pe.wait_ge(ln.updated, n)
                pe.wait_ge(weightT_ready, n + 1)
                for j in range(GROUP):
                    last = nc.tensor.matmul(bank[:, OUT, j * DIM:(j + 1) * DIM],
                                            weightT[:, j * TOK:(j + 1) * TOK], values[:, u, j, :],
                                            start=True, stop=True)
                last.then_inc(summed, 1)
                if more2:
                    turn(n + 2)

            turn(0)
            scores(0, 0)
            turn(1)
            engine_loop_ahead(pe, body)

        @block.scalar
        def _(act):
            def take_turned(n, u):
                act.wait_ge(turned, n + 1)
                nc.scalar.copy(xnT[:, u, :], bank[:, TURN, :]).then_inc(xnT_ready, 1)

            def exps(n):
                act.wait_ge(below_ready, n + 1)
                nc.scalar.activation(powers[:, :, :].rearrange("p b k -> p (b k)"),
                                     below[:, :, :].rearrange("p b k -> p (b k)"), ACT.Exp)\
                    .then_inc(powers_ready, 1)

            def body(n, u, more, more2):
                act.wait_ge(weight_turned, n + 1)
                nc.scalar.copy(weightT[:, :], bank[0:KEYS, WEIGHTS, :]).then_inc(weightT_ready, 1)
                if more:
                    exps(n + 1)
                if more2:
                    take_turned(n + 2, u)

            take_turned(0, 0)
            take_turned(1, 1)
            exps(0)
            engine_loop_ahead(act, body)

        @block.vector
        def _(dve):
            done = [0]

            def step(n, instruction):
                instruction.then_inc(step_done, 1)
                done[0] += 1
                dve.wait_ge(step_done, STEPS * n + done[0])

            def logits(n, u):
                done[0] = 0
                landed(dve, n, u)
                dve.wait_ge(scores_ready, n + 1)
                step(n, nc.vector.tensor_scalar(
                    scaled[:, :, :], bank[:, SCORES + u, 0:KCOLS].rearrange(
                        "p (b k) -> p b k", b=GROUP), scale, None, ALU.mult))
                step(n, nc.vector.tensor_scalar(masks[:, :, :], mask[:, u, :, :], -1.0, None,
                                                ALU.is_lt))
                chip.settle()
                step(n, nc.vector.copy_predicated(scaled[:, :, :], masks[:, :, :],
                                                  mask[:, u, :, :]))
                step(n, nc.vector.tensor_reduce(largest[:, :], scaled[:, :, :], AX.X, ALU.max))
                nc.vector.tensor_tensor(out=below[:, :, :], in0=scaled[:, :, :],
                                        in1=bc(largest[:, :], 2, KEYS),
                                        op=ALU.subtract).then_inc(below_ready, 1)

            def weights(n):
                done[0] = LOGIT_STEPS
                dve.wait_ge(weight_turned, n)
                nc.vector.memset(weight[:, :, :], 0.0).then_inc(zeros_ready, 1)
                dve.wait_ge(powers_ready, n + 1)
                step(n, nc.vector.tensor_reduce(total[:, :], powers[:, :, :], AX.X, ALU.add))
                step(n, nc.vector.reciprocal(total[:, :], total[:, :]))
                step(n, nc.vector.tensor_tensor(out=share[:, :, :], in0=powers[:, :, :],
                                                in1=bc(total[:, :], 2, KEYS), op=ALU.mult))
                step(n, nc.vector.tensor_tensor(out=number[:, :, :], in0=share[:, :, :],
                                                in1=share[:, :, :], op=ALU.is_equal))
                dve.wait_ge(zeros_ready, n + 1)
                chip.settle()
                step(n, nc.vector.copy_predicated(weight[:, :, :], number[:, :, :],
                                                  share[:, :, :]))

            def body(n, u, more, more2):
                weights(n)
                if more:
                    logits(n + 1, 1 - u)
                dve.wait_ge(summed, n + 1)
                chip.add_to_x(dve, n, bank[:, OUT, :].rearrange("p (b d) -> p b d", b=GROUP), ln)
                if more2:
                    dve.wait_ge(turned, n + 2)
                    chip.normalise(n + 2, xn).then_inc(xn_ready, 1)

            chip.normalise(0, xn).then_inc(xn_ready, 1)
            dve.wait_ge(turned, 1)
            chip.normalise(1, xn).then_inc(xn_ready, 1)
            logits(0, 0)
            engine_loop_ahead(dve, body)

        @block.gpsimd
        def _(pool):
            chip.clear_last()

            def body(n, u, more):
                chip.rstd_of(pool, n, ln)
            engine_loop_pairs(pool, body)


def mix_ffn(chip):
    nc, d, bank = chip.nc, chip.dram, chip.bank
    ctx, sb, sem = phase(chip, "mix")
    with ctx:
        w = chip.weights["mix"]
        w_r, w_k, w_v, mu = w.tiles("w_r", "w_k", "w_v", "mu")
        one_less_mu = sb("one_less_mu", [128, 2])
        xn = sb("xn", [128, GROUP, DIM])
        padded = sb("padded", [128, 2, GROUP, TOK + 1])
        scaled = sb("scaled", [128, 2, GROUP, TOK])
        mixed = sb("mixed", [128, 2, GROUP, TOK])
        gate = sb("gate", [128, COLS])
        relu = sb("relu", [128, COLS])
        square = sb("square", [128, COLS])
        outT = sb("outT", [128, COLS])
        xn_ready, turned, padded_ready = (
            sem("xn_ready"), sem("turned"), sem("padded_ready"))
        mu_ready, cleared, scaled_ready, mixed_ready = (
            sem("mu_ready"), sem("cleared"), sem("scaled_ready"), sem("mixed_ready"))
        pre_ready, gate_ready, relu_ready, square_ready = (
            sem("pre_ready"), sem("gate_ready"), sem("relu_ready"), sem("square_ready"))
        value_ready, outT_ready, out_turned, updated = (
            sem("value_ready"), sem("outT_ready"), sem("out_turned"), sem("updated"))
        stored = sem("stored")
        TURN, R, K, V, BACK = 0, 1, 2, 3, 4
        block = ctx.enter_context(nc.Block())

        @block.sync
        def _(sp):
            def body(n, u, more):
                sp.wait_ge(updated, n + 1)
                r = chip.rows(n)
                sp.dma_start(d["out"][r, :, :].rearrange("b t d -> t b d"), chip.x[:, r, :])\
                    .then_inc(stored, 16)
            engine_loop_pairs(sp, body)
            sp.wait_ge(stored, 16 * BLOCKS)

        @block.tensor
        def _(pe):
            def turn(n):
                pe.wait_ge(xn_ready, n + 1)
                for j in range(GROUP):
                    last = nc.tensor.transpose(bank[:, TURN, j * TOK:(j + 1) * TOK], xn[:, j, :],
                                               chip.ident[:, :])
                last.then_inc(turned, 1)

            def pre(n):
                for i, (w, at) in enumerate(((w_k, K), (w_r, R))):
                    if i:
                        pe.wait_ge(gate_ready, n)
                    pe.wait_ge(mixed_ready, 2 * n + i + 1)
                    nc.tensor.matmul(bank[:, at, :], w[:, :],
                                     mixed[:, i, :, :].rearrange("p b t -> p (b t)"),
                                     start=True, stop=True).then_inc(pre_ready, 1)

            def body(n, u, more, more2):
                pe.wait_ge(square_ready, n + 1)
                nc.tensor.matmul(bank[:, V, :], w_v[:, :], square[:, :], start=True, stop=True)\
                    .then_inc(value_ready, 1)
                if more:
                    pre(n + 1)
                if more2:
                    turn(n + 2)
                pe.wait_ge(outT_ready, n + 1)
                for j in range(GROUP):
                    last = nc.tensor.transpose(bank[:, BACK, j * TOK:(j + 1) * TOK],
                                               outT[:, j * TOK:(j + 1) * TOK], chip.ident[:, :])
                last.then_inc(out_turned, 1)

            pe.wait_ge(w.loaded, w.all)
            turn(0)
            turn(1)
            pre(0)
            engine_loop_ahead(pe, body)

        @block.scalar
        def _(act):
            def take_turned(n, u):
                act.wait_ge(turned, n + 1)
                nc.scalar.copy(padded[:, u, :, 1:], bank[:, TURN, :].rearrange(
                    "p (b t) -> p b t", b=GROUP)).then_inc(padded_ready, 1)

            def body(n, u, more, more2):
                act.wait_ge(pre_ready, 2 * n + 1)
                nc.scalar.activation(relu[:, :], bank[:, K, :], ACT.Relu).then_inc(relu_ready, 1)
                act.wait_ge(relu_ready, n + 1)
                act.wait_ge(value_ready, n)
                nc.scalar.activation(square[:, :], relu[:, :], ACT.Square)\
                    .then_inc(square_ready, 1)
                act.wait_ge(pre_ready, 2 * n + 2)
                act.wait_ge(outT_ready, n)
                nc.scalar.activation(gate[:, :], bank[:, R, :], ACT.Tanh,
                                     scale=0.5).then_inc(gate_ready, 1)
                if more2:
                    take_turned(n + 2, u)

            act.wait_ge(cleared, 1)
            take_turned(0, 0)
            take_turned(1, 1)
            engine_loop_ahead(act, body)

        @block.vector
        def _(dve):
            def mix(n, u):
                dve.wait_ge(padded_ready, n + 1)
                for i in range(2):
                    at = 1 - i
                    nc.vector.tensor_scalar(scaled[:, i, :, :], padded[:, u, :, 1:],
                                            mu[:, at:at + 1], None, ALU.mult)\
                        .then_inc(scaled_ready, 1)
                for i in range(2):
                    at = 1 - i
                    dve.wait_ge(scaled_ready, 2 * n + i + 1)
                    nc.vector.scalar_tensor_tensor(
                        out=mixed[:, i, :, :], in0=padded[:, u, :, 0:TOK],
                        scalar=one_less_mu[:, at:at + 1], in1=scaled[:, i, :, :],
                        op0=ALU.mult, op1=ALU.add).then_inc(mixed_ready, 1)

            def body(n, u, more, more2):
                if more:
                    dve.wait_ge(pre_ready, 2 * n + 2)
                    mix(n + 1, 1 - u)
                if more2:
                    dve.wait_ge(turned, n + 2)
                    chip.normalise(n + 2, xn).then_inc(xn_ready, 1)
                dve.wait_ge(gate_ready, n + 1)
                dve.wait_ge(value_ready, n + 1)
                nc.vector.scalar_tensor_tensor(
                    out=outT[:, :], in0=gate[:, :], scalar=1.0, in1=bank[:, V, :],
                    op0=ALU.add, op1=ALU.mult).then_inc(outT_ready, 1)
                dve.wait_ge(out_turned, n + 1)
                r = chip.rows(n)
                nc.vector.scalar_tensor_tensor(
                    out=chip.x[:, r, :], in0=bank[:, BACK, :].rearrange(
                        "p (b d) -> p b d", b=GROUP), scalar=0.5, in1=chip.x[:, r, :],
                    op0=ALU.mult, op1=ALU.add).then_inc(updated, 1)

            dve.wait_ge(w.loaded, w.all)
            nc.vector.tensor_scalar(one_less_mu[:, :], mu[:, :], -1.0, 1.0, ALU.mult, ALU.add)\
                .then_inc(mu_ready, 1)
            chip.normalise(0, xn).then_inc(xn_ready, 1)
            dve.wait_ge(mu_ready, 1)
            mix(0, 0)
            dve.wait_ge(turned, 1)
            chip.normalise(1, xn).then_inc(xn_ready, 1)
            engine_loop_ahead(dve, body)

        @block.gpsimd
        def _(pool):
            chip.clear_last()
            nc.gpsimd.memset(padded[:, :, :, 0], 0.0).then_inc(cleared, 1)


PHASES = ["x0", "tree", "x1", "moe", "slots", "gated", "x3", "mix"]


def build(nc, dram):
    with ExitStack() as top:
        chip = Chip(nc, top, dram)
        load_stream(chip)
        fns = {"x0": lambda c: heads_attention(c, "x0", False),
               "x1": lambda c: heads_attention(c, "x1", True), "x3": context_attention,
               "slots": slot_attention,
               "tree": tree_ffn, "moe": moe_ffn, "gated": gated_ffn, "mix": mix_ffn}
        for p in PHASES:
            fns[p](chip)


def ancestor_matrix():
    a = np.zeros((128, NODES), np.float32)
    rights = np.zeros(NODES, np.float32)
    for node in range(1, NODES):
        m = node
        while m:
            up = (m - 1) // 2
            right = m == 2 * up + 2
            a[up, node] = 1.0 if right else -1.0
            rights[node] += right
            m = up
    return a, rights


def layouts(inputs):
    g = {k: np.ascontiguousarray(v) for k, v in inputs.items()}
    t = lambda name: np.ascontiguousarray(g[name].T)
    rows = lambda a: np.ascontiguousarray(np.broadcast_to(a, (128,) + a.shape))
    bf16 = mybir.dt.np(BF16)
    out = {"x": g["x"], "ident": np.eye(128, dtype=np.float32)}

    out["tree_w_in"] = t("L0_ffn_W_in")
    two = np.zeros((TREES, 256) + (DIM,), np.float32)
    two[:, :NODES] = g["L0_ffn_W_out"].T.reshape(TREES, NODES, DIM)
    out["tree_w_out"] = np.ascontiguousarray(two.reshape(TREES, 2, 128, DIM).transpose(2, 0, 1, 3))
    b = np.zeros((TREES, 256), np.float32)
    b[:, :NODES] = g["L0_ffn_b_in"].reshape(TREES, NODES)
    out["tree_b_in"] = np.ascontiguousarray(b.reshape(TREES, 2, 128).transpose(2, 0, 1))
    a, rights = ancestor_matrix()
    out["tree_ancestors"] = a.astype(bf16)
    r = np.zeros(256, np.float32)
    r[:NODES] = rights
    out["tree_target"] = np.ascontiguousarray(r.reshape(2, 128).T)

    for name, at, upper in (("x0", "L0_xattn", True), ("x1", "L1_xattn", False)):
        for p in "qkvo":
            w = f"{at}_W{p}" if upper else f"{at}_w{p}"
            out[f"{name}_w_{p}"] = t(w)
        out[f"{name}_b_q"], out[f"{name}_b_k"] = g[f"{at}_bq"][:, None], g[f"{at}_bk"][:, None]
        out[f"{name}_b_v"] = rows(g[f"{at}_bv"])
        out[f"{name}_b_o"] = g[f"{at}_bo"][None, :]
    part = np.arange(128)[:, None]
    out["own_head"] = (part // HEAD_DIM == np.arange(HEADS)).astype(np.float32)
    out["ctxT"] = np.ascontiguousarray(g["ctx_1024"].transpose(2, 0, 1))
    out["ctx"] = np.ascontiguousarray(g["ctx_1024"].transpose(1, 0, 2))
    out["mask"] = np.ascontiguousarray(g["mask_Bx1xSxS2_ik1"][:, 0].transpose(1, 0, 2))
    out["x3_mask"] = np.ascontiguousarray(g["mask_BxSxS2_fk0"].transpose(1, 0, 2))

    out["moe_w_route"] = t("L1_ffn_Wg")
    out["moe_bias"] = rows(g["L1_ffn_bias_corr"])
    up = g["L1_ffn_W1"].reshape(MOE_CHUNKS, 128, DIM)
    up = np.concatenate([up, g["L1_ffn_Ws1"][None]])
    out["moe_w_up"] = np.ascontiguousarray(up.transpose(2, 0, 1))
    down = g["L1_ffn_W2"].transpose(0, 2, 1).reshape(MOE_CHUNKS, 128, DIM)
    down = np.concatenate([down, g["L1_ffn_Ws2"].T[None]])
    out["moe_w_down"] = np.ascontiguousarray(down.transpose(1, 0, 2))
    e = np.arange(EXPERTS)[:, None]
    owner = (np.arange(MOE_CHUNKS * 128) // EXP_HID)[None, :]
    out["moe_spread"] = np.tile(e == owner, (3, 1)).reshape(3 * EXPERTS, MOE_CHUNKS, 128).astype(bf16)
    for size, dt in ((EXP_GROUPS, np.float32), (GATED, bf16), (EXPERTS, bf16)):
        out[f"earlier{size}"] = rows(np.tril(np.ones((size, size), np.float32), -1).astype(dt))

    for p in "qkv":
        out[f"slots_w_{p}"] = t(f"L2_xattn_W{p}")
    for p in ("ih", "hh"):
        w = g[f"L2_xattn_gru_w{p}"].reshape(3, DIM, DIM)
        out[f"slots_w_{p}"] = np.ascontiguousarray(w.transpose(2, 0, 1))
        out[f"slots_b_{p}"] = np.ascontiguousarray(g[f"L2_xattn_gru_b{p}"].reshape(3, DIM).T)
    out["slots_slot_norm"] = g["L2_xattn_slot_norm_w"][:, None]
    out["slots_input_norm"] = g["L2_xattn_input_norm_w"][:, None]

    out["gated_w_gate"] = t("L2_ffn_gate_w")
    out["gated_b_gate"] = rows(g["L2_ffn_gate_b"])
    out["gated_w"] = np.ascontiguousarray(g["L2_ffn_expert_w"].transpose(1, 0, 2))
    out["gated_b"] = np.tile(g["L2_ffn_expert_b"], (3, 1))
    out["gated_spread"] = np.broadcast_to(np.tile(np.eye(GATED), (3, 1))[:, :, None],
                                          (3 * GATED, GATED, 128)).astype(bf16)

    out["mix_w_r"], out["mix_w_k"], out["mix_w_v"] = t("L3_ffn_W_r"), t("L3_ffn_W_k"), t("L3_ffn_W_v")
    out["mix_mu"] = np.stack([g["L3_ffn_mu_r"], g["L3_ffn_mu_k"]], axis=1)
    return out


def kernel(**inputs):
    import concourse.bacc as bacc
    from concourse.bass_utils import run_bass_kernel_spmd

    arrays = layouts(inputs)
    nc = bacc.Bacc("TRN2", target_bir_lowering=False, num_devices=1)
    dram = {k: nc.dram_tensor(f"in_{k}", v.shape, mybir.dt.from_np(v.dtype), kind="ExternalInput").ap()
            for k, v in arrays.items()}
    dram["out"] = nc.dram_tensor("out", (SEQS, TOK, DIM), F32, kind="ExternalOutput").ap()
    build(nc, dram)
    r = run_bass_kernel_spmd(nc, [{f"in_{k}": v for k, v in arrays.items()}], core_ids=[0])
    return r.results[0]["out"]
```
